# Optimizing a Trainium2 kernel written in Bass

```python
import numpy as np
import jax
import jax.numpy as jnp

def _softmax(x, axis=-1):
    return jax.nn.softmax(x, axis=axis)

def _gelu(x):
    return jax.nn.gelu(x, approximate=True)

def _silu(x):
    return jax.nn.silu(x)

def _sigmoid(x):
    return jax.nn.sigmoid(x)

def _layernorm(x, axis=-1, eps=1e-05):
    m = jnp.mean(x, axis=axis, keepdims=True)
    v = jnp.var(x, axis=axis, keepdims=True)
    return (x - m) / jnp.sqrt(v + eps)

def _scatter_add(tgt, idx, src, axis=0):
    return tgt.at[idx].add(src)

def _segment_sum(src, seg, n):
    return jax.ops.segment_sum(src, seg, n)
kernel_name = 'mk_xattn_ffn_d4_seqx_r4_4cb540'

def setup_inputs(seed: int=0):
    np.random.seed(seed)
    _w = jnp.asarray

    def _rec_inputs():
        import jax
        import jax.numpy as jnp
        _rk = jax.random.key(seed)
        x = 7.22e-05 + 1 * jax.random.normal(jax.random.fold_in(_rk, 1), (4, 512, 256), jnp.float32)
        _lenS = 512 - jax.random.randint(jax.random.fold_in(_rk, 7), (4,), 0, max(1, 512 // 4) + 1, jnp.int32)
        _lenS2 = 512 - jax.random.randint(jax.random.fold_in(_rk, 8), (4,), 0, max(1, 512 // 4) + 1, jnp.int32)
        _ctx_1024P = jax.random.normal(jax.random.fold_in(_rk, 11), (4, 16, 256), jnp.float32)
        _ctx_1024c = jax.random.dirichlet(jax.random.fold_in(_rk, 511), 0.3 * jnp.ones((16,), jnp.float32), (4, 512))
        _ctx_1024t = jnp.einsum('bsk,bkd->bsd', _ctx_1024c, _ctx_1024P)
        _ctx_1024t = _ctx_1024t * jax.lax.rsqrt(jnp.mean(jnp.square(_ctx_1024t)) + 1e-12) * 0.953939
        ctx_1024 = 4.13588e-05 + 0.999923 * (_ctx_1024t + 0.3 * jax.random.normal(jax.random.fold_in(_rk, 611), (4, 512, 256), jnp.float32))
        _validS = jnp.arange(512)[None, :] < _lenS[:, None]
        _validS2 = jnp.arange(512)[None, :] < _lenS2[:, None]
        _causal = jnp.tril(jnp.ones((512, 512), dtype=bool))
        mask_Bx1xSxS2_ik1 = jnp.where(jnp.broadcast_to(_validS2[:, None, None, :], (4, 1, 512, 512)), 1, 0).astype(jnp.int32)
        return (x, ctx_1024, mask_Bx1xSxS2_ik1)
    x, ctx_1024, mask_Bx1xSxS2_ik1 = _rec_inputs()

    def _L0_xattn_setup():
        import jax, jax.numpy as jnp
        import numpy as np
        BETA = 256
        NUM_HEADS = 16
        NORM = (BETA // NUM_HEADS) ** (-0.5)
        key = jax.random.key(seed)
        ks = jax.random.split(key, 6)
        B, N = (4, 512)
        D_in_q = D_in_k = D_in_v = 256
        D_out_k = D_out_v = 256
        q = jax.random.normal(ks[0], (B, N, D_in_q), dtype=jnp.float32)
        k = jax.random.normal(ks[1], (B, N, D_in_k), dtype=jnp.float32)
        v = jax.random.normal(ks[2], (B, N, D_in_v), dtype=jnp.float32)
        Wq = jax.random.normal(ks[3], (D_out_k, D_in_q), dtype=jnp.float32) * D_in_q ** (-0.5)
        Wk = jax.random.normal(ks[4], (D_out_k, D_in_k), dtype=jnp.float32) * D_in_k ** (-0.5)
        Wv = jax.random.normal(ks[5], (D_out_v, D_in_v), dtype=jnp.float32) * D_in_v ** (-0.5)
        return {'q': q, 'k': k, 'v': v, 'Wq': Wq, 'Wk': Wk, 'Wv': Wv}
    _L0_xattn_all = _L0_xattn_setup()
    _L0_xattn_in = {k: v for k, v in _L0_xattn_all.items() if k in ('Wq', 'Wk', 'Wv')}
    del _L0_xattn_all

    def _L0_ffn_setup():
        import jax, jax.numpy as jnp
        import numpy as np
        DIM = 256
        DEPTH = 2
        HEADS = 8
        DIM_HEAD = 64
        WINDOW = 128
        INNER = HEADS * DIM_HEAD
        HID = int(DIM * 4 * 2 / 3)
        B, N = (2, 2048)
        QK_SCALE = 8.0

        def shift_token(t):
            t1, t2 = jnp.split(t, 2, axis=-1)
            t2 = jnp.pad(t2, ((0, 0), (1, 0), (0, 0)))[:, :-1]
            return jnp.concatenate([t1, t2], axis=-1)

        def l2norm(t):
            return t / jnp.clip(jnp.linalg.norm(t, axis=-1, keepdims=True), 1e-12)

        def rotate_half(x):
            x1, x2 = jnp.split(x, 2, axis=-1)
            return jnp.concatenate([-x2, x1], axis=-1)

        def rotary_xpos(q, k):
            n = q.shape[-2]
            half_idx = jnp.arange(0, DIM_HEAD, 2, dtype=jnp.float32)
            inv_freq = 1.0 / 10000.0 ** (half_idx / DIM_HEAD)
            t = jnp.arange(n, dtype=jnp.float32)
            freqs = t[:, None] * inv_freq[None, :]
            freqs = jnp.concatenate([freqs, freqs], axis=-1)
            base = (half_idx + 0.4 * DIM_HEAD) / (1.4 * DIM_HEAD)
            power = (t - n // 2) / float(WINDOW // 2)
            scale = base[None, :] ** power[:, None]
            scale = jnp.concatenate([scale, scale], axis=-1)
            cos, sin = (jnp.cos(freqs), jnp.sin(freqs))
            q = q * cos * scale + rotate_half(q) * sin * scale
            k = k * cos / scale + rotate_half(k) * sin / scale
            return (q, k)

        def local_attention(q, k, v):
            b, h, n, d = q.shape
            w = n // WINDOW
            bq = q.reshape(b, h, w, WINDOW, d) * QK_SCALE
            bk = k.reshape(b, h, w, WINDOW, d)
            bv = v.reshape(b, h, w, WINDOW, d)

            def look_around(t):
                p = jnp.pad(t, ((0, 0), (0, 0), (1, 0), (0, 0), (0, 0)))
                return jnp.concatenate([p[:, :, :w], p[:, :, 1:]], axis=3)
            bk, bv = (look_around(bk), look_around(bv))
            bt = jnp.arange(n).reshape(w, WINDOW)
            btp = jnp.pad(bt, ((1, 0), (0, 0)), constant_values=-1)
            btk = jnp.concatenate([btp[:w], btp[1:]], axis=1)
            sim = jnp.einsum('bhwid,bhwjd->bhwij', bq, bk)
            i = bt[:, :, None]
            j = btk[:, None, :]
            mask = (i < j) | (i > j + WINDOW) | (j == -1)
            sim = jnp.where(mask, -jnp.finfo(sim.dtype).max, sim)
            attn = jax.nn.softmax(sim, axis=-1)
            out = jnp.einsum('bhwij,bhwjd->bhwid', attn, bv)
            return out.reshape(b, h, n, d)

        def _layer(x, wqkv, qs, ksc, wo, lg, lb, w1, b1, w2, b2):
            b, n, _ = x.shape
            h = shift_token(x)
            qkv = h @ wqkv
            q, k, v = jnp.split(qkv, 3, axis=-1)
            to_heads = lambda t: t.reshape(b, n, HEADS, DIM_HEAD).transpose(0, 2, 1, 3)
            q, k, v = (to_heads(q), to_heads(k), to_heads(v))
            q = l2norm(q) * qs
            k = l2norm(k) * ksc
            q, k = rotary_xpos(q, k)
            o = local_attention(q, k, v)
            o = o.transpose(0, 2, 1, 3).reshape(b, n, INNER)
            x = x + o @ wo
            h = shift_token(x)
            mu = h.mean(-1, keepdims=True)
            var = h.var(-1, keepdims=True)
            h = (h - mu) / jnp.sqrt(var + 1e-05) * lg + lb
            h = h @ w1 + b1
            a, g = jnp.split(h, 2, axis=-1)
            h = a * jax.nn.gelu(g, approximate=False)
            x = x + h @ w2 + b2
            return x
        key = jax.random.key(seed)
        ks = jax.random.split(key, 6)
        return {'x': jax.random.normal(ks[0], (B, N, DIM), jnp.float32), 'wqkv': jax.random.normal(ks[1], (DEPTH, DIM, 3 * INNER), jnp.float32) * 0.02, 'q_scale': jnp.ones((DEPTH, DIM_HEAD), jnp.float32), 'k_scale': jnp.ones((DEPTH, DIM_HEAD), jnp.float32), 'wo': jax.random.normal(ks[2], (DEPTH, INNER, DIM), jnp.float32) * 0.02, 'ln_g': jnp.ones((DEPTH, DIM), jnp.float32), 'ln_b': jnp.zeros((DEPTH, DIM), jnp.float32), 'w1': jax.random.normal(ks[3], (DEPTH, DIM, 2 * HID), jnp.float32) * 0.02, 'b1': jnp.zeros((DEPTH, 2 * HID), jnp.float32), 'w2': jax.random.normal(ks[4], (DEPTH, HID, DIM), jnp.float32) * 0.02, 'b2': jnp.zeros((DEPTH, DIM), jnp.float32)}
    _L0_ffn_all = _L0_ffn_setup()
    _L0_ffn_in = {k: v for k, v in _L0_ffn_all.items() if k in ('wqkv', 'q_scale', 'k_scale', 'wo', 'ln_g', 'ln_b', 'w1', 'b1', 'w2', 'b2')}
    del _L0_ffn_all

    def _L1_xattn_setup():
        import jax, jax.numpy as jnp
        import numpy as np
        HIDDEN = 256
        HEADS = 16
        HEAD_DIM = HIDDEN // HEADS
        SCALE = HEAD_DIM ** (-0.5)
        NEG_INF = -1000000000.0

        def _split_heads(x):
            B, S, _ = x.shape
            return x.reshape(B, S, HEADS, HEAD_DIM).transpose(0, 2, 1, 3)
        key = jax.random.key(seed)
        ks = jax.random.split(key, 12)
        B, Sq, Sk = (2, 512, 512)
        inp = {'query': jax.random.normal(ks[0], (B, Sq, HIDDEN), jnp.float32), 'key': jax.random.normal(ks[1], (B, Sk, HIDDEN), jnp.float32), 'value': jax.random.normal(ks[2], (B, Sk, HIDDEN), jnp.float32), 'mask': jax.random.randint(ks[3], (B, 1, Sq, Sk), 0, 2, jnp.int32), 'Wq': jax.random.normal(ks[4], (HIDDEN, HIDDEN), jnp.float32) * 0.02, 'bq': jax.random.normal(ks[5], (HIDDEN,), jnp.float32) * 0.02, 'Wk': jax.random.normal(ks[6], (HIDDEN, HIDDEN), jnp.float32) * 0.02, 'bk': jax.random.normal(ks[7], (HIDDEN,), jnp.float32) * 0.02, 'Wv': jax.random.normal(ks[8], (HIDDEN, HIDDEN), jnp.float32) * 0.02, 'bv': jax.random.normal(ks[9], (HIDDEN,), jnp.float32) * 0.02, 'Wo': jax.random.normal(ks[10], (HIDDEN, HIDDEN), jnp.float32) * 0.02}
        return inp
    _L1_xattn_all = _L1_xattn_setup()
    _L1_xattn_in = {k: v for k, v in _L1_xattn_all.items() if k in ('Wq', 'bq', 'Wk', 'bk', 'Wv', 'bv', 'Wo')}
    del _L1_xattn_all

    def _L1_ffn_setup():
        import jax, jax.numpy as jnp
        import numpy as np
        B, S, D, F, E, NS, K = (2, 256, 256, 1024, 8, 8, 2)
        FS = F // NS
        key = jax.random.key(seed)
        ks = jax.random.split(key, 8)
        scale = 0.02
        return {'hidden_states': jax.random.normal(ks[0], (B, S, D), jnp.float32), 'gate_W': jax.random.normal(ks[1], (E, D), jnp.float32) * scale, 'w1_e': jax.random.normal(ks[2], (E, D, F), jnp.float32) * scale, 'w3_e': jax.random.normal(ks[3], (E, D, F), jnp.float32) * scale, 'w2_e': jax.random.normal(ks[4], (E, F, D), jnp.float32) * scale, 'w1_s': jax.random.normal(ks[5], (NS, D, FS), jnp.float32) * scale, 'w3_s': jax.random.normal(ks[6], (NS, D, FS), jnp.float32) * scale, 'w2_s': jax.random.normal(ks[7], (NS, FS, D), jnp.float32) * scale}
    _L1_ffn_all = _L1_ffn_setup()
    _L1_ffn_in = {k: v for k, v in _L1_ffn_all.items() if k in ('gate_W', 'w1_e', 'w3_e', 'w2_e', 'w1_s', 'w3_s', 'w2_s')}
    del _L1_ffn_all

    def _L2_xattn_setup():
        import jax, jax.numpy as jnp
        import numpy as np
        DIM = 256
        NUM_HEADS = 8
        HEAD_DIM = 64
        INNER = NUM_HEADS * HEAD_DIM
        key = jax.random.key(seed)
        ks = jax.random.split(key, 7)
        B, N, M = (8, 128, 1024)
        x = jax.random.normal(ks[0], (B, N, DIM), dtype=jnp.float32)
        context = jax.random.normal(ks[1], (B, M, DIM), dtype=jnp.float32)
        s_in = 1.0 / np.sqrt(DIM)
        s_inner = 1.0 / np.sqrt(INNER)
        Wq = jax.random.normal(ks[2], (DIM, INNER), dtype=jnp.float32) * s_in
        Wk = jax.random.normal(ks[3], (DIM, INNER), dtype=jnp.float32) * s_in
        Wv = jax.random.normal(ks[4], (DIM, INNER), dtype=jnp.float32) * s_in
        Wo = jax.random.normal(ks[5], (INNER, DIM), dtype=jnp.float32) * s_inner
        bo = jax.random.normal(ks[6], (DIM,), dtype=jnp.float32) * 0.01
        return {'x': x, 'context': context, 'Wq': Wq, 'Wk': Wk, 'Wv': Wv, 'Wo': Wo, 'bo': bo}
    _L2_xattn_all = _L2_xattn_setup()
    _L2_xattn_in = {k: v for k, v in _L2_xattn_all.items() if k in ('Wq', 'Wk', 'Wv', 'Wo', 'bo')}
    del _L2_xattn_all

    def _L2_ffn_setup():
        import jax, jax.numpy as jnp
        import numpy as np
        D, H, E, K, S = (256, 512, 8, 2, 1)
        B, L = (4, 512)
        key = jax.random.key(seed)
        ks = jax.random.split(key, 9)
        std = 0.02
        return {'x': jax.random.normal(ks[0], (B, L, D), dtype=jnp.float32), 'router_w': jax.random.normal(ks[1], (E, D), dtype=jnp.float32) * std, 'experts_bias': jnp.zeros((E,), dtype=jnp.float32), 'w1': jax.random.normal(ks[2], (E, D, H), dtype=jnp.float32) * std, 'w3': jax.random.normal(ks[3], (E, D, H), dtype=jnp.float32) * std, 'w2': jax.random.normal(ks[4], (E, H, D), dtype=jnp.float32) * std, 'sw1': jax.random.normal(ks[5], (S, D, H), dtype=jnp.float32) * std, 'sw3': jax.random.normal(ks[6], (S, D, H), dtype=jnp.float32) * std, 'sw2': jax.random.normal(ks[7], (S, H, D), dtype=jnp.float32) * std}
    _L2_ffn_all = _L2_ffn_setup()
    _L2_ffn_in = {k: v for k, v in _L2_ffn_all.items() if k in ('router_w', 'experts_bias', 'w1', 'w3', 'w2', 'sw1', 'sw3', 'sw2')}
    del _L2_ffn_all

    def _L3_xattn_setup():
        import jax, jax.numpy as jnp
        import numpy as np
        B, S, D_IN, D_MODEL = (4, 512, 256, 256)
        key = jax.random.key(seed)
        ks = jax.random.split(key, 9)
        return {'q': jax.random.normal(ks[0], (B, S, D_IN), jnp.float32), 'k': jax.random.normal(ks[1], (B, S, D_IN), jnp.float32), 'v': jax.random.normal(ks[2], (B, S, D_IN), jnp.float32), 'Wq': jax.random.normal(ks[3], (D_IN, D_MODEL), jnp.float32) * 0.02, 'bq': jax.random.normal(ks[4], (D_MODEL,), jnp.float32) * 0.02, 'Wk': jax.random.normal(ks[5], (D_IN, D_MODEL), jnp.float32) * 0.02, 'bk': jax.random.normal(ks[6], (D_MODEL,), jnp.float32) * 0.02, 'Wv': jax.random.normal(ks[7], (D_IN, D_MODEL), jnp.float32) * 0.02, 'bv': jax.random.normal(ks[8], (D_MODEL,), jnp.float32) * 0.02}
    _L3_xattn_all = _L3_xattn_setup()
    _L3_xattn_in = {k: v for k, v in _L3_xattn_all.items() if k in ('Wq', 'bq', 'Wk', 'bk', 'Wv', 'bv')}
    del _L3_xattn_all

    def _L3_ffn_setup():
        import math
        import jax, jax.numpy as jnp
        import numpy as np
        B, T, H = (4, 512, 256)
        E, K, F = (8, 2, 512)
        CAP_FACTOR = 1.25

        def _moe_forward(x, Wg, W_in, W_out):
            b, t, h = x.shape
            xf = x.reshape(-1, h)
            S = xf.shape[0]
            C = int(math.ceil(K * S / E * CAP_FACTOR))
            logits = xf @ Wg
            probs = jax.nn.softmax(logits, axis=-1)
            top_vals, top_idx = jax.lax.top_k(probs, K)
            flat_idx = top_idx.T.reshape(-1)
            onehot = jax.nn.one_hot(flat_idx, E, dtype=jnp.int32)
            cum = jnp.cumsum(onehot, axis=0) - 1
            loc = jnp.take_along_axis(cum, flat_idx[:, None], axis=1)[:, 0]
            loc = loc.reshape(K, S).T
            keep = loc < C
            gates = top_vals * keep.astype(top_vals.dtype)
            denom = jnp.maximum(gates.sum(-1, keepdims=True), 1e-09)
            gates = gates / denom
            loc_c = jnp.where(keep, loc, C)
            e_flat = top_idx.reshape(-1)
            l_flat = loc_c.reshape(-1)
            xk = jnp.broadcast_to(xf[:, None, :], (S, K, h)).reshape(-1, h)
            xk = jnp.where(keep.reshape(-1, 1), xk, 0.0)
            buf = jnp.zeros((E, C + 1, h), x.dtype).at[e_flat, l_flat].set(xk)
            inp = buf[:, :C]
            hid = jnp.einsum('ech,ehf->ecf', inp, W_in)
            a, g = jnp.split(hid, 2, axis=-1)
            hid = jax.nn.gelu(a, approximate=False) * g
            out_e = jnp.einsum('ecf,efh->ech', hid, W_out)
            out_pad = jnp.concatenate([out_e, jnp.zeros((E, 1, h), out_e.dtype)], axis=1)
            gathered = out_pad[e_flat, l_flat].reshape(S, K, h)
            y = (gathered * gates[..., None]).sum(axis=1)
            return y.reshape(b, t, h)
        key = jax.random.key(seed)
        k1, k2, k3, k4 = jax.random.split(key, 4)
        x = jax.random.normal(k1, (B, T, H), dtype=jnp.float32)
        Wg = jax.random.normal(k2, (H, E), dtype=jnp.float32) * 0.02
        W_in = jax.random.normal(k3, (E, H, 2 * F), dtype=jnp.float32) * (1.0 / math.sqrt(H))
        W_out = jax.random.normal(k4, (E, F, H), dtype=jnp.float32) * (1.0 / math.sqrt(F))
        return {'x': x, 'Wg': Wg, 'W_in': W_in, 'W_out': W_out}
    _L3_ffn_all = _L3_ffn_setup()
    _L3_ffn_in = {k: v for k, v in _L3_ffn_all.items() if k in ('Wg', 'W_in', 'W_out')}
    del _L3_ffn_all
    return {'x': x, 'ctx_1024': ctx_1024, 'mask_Bx1xSxS2_ik1': mask_Bx1xSxS2_ik1, 'L0_xattn_Wq': _L0_xattn_in['Wq'], 'L0_xattn_Wk': _L0_xattn_in['Wk'], 'L0_xattn_Wv': _L0_xattn_in['Wv'], 'L0_ffn_wqkv': _L0_ffn_in['wqkv'], 'L0_ffn_q_scale': _L0_ffn_in['q_scale'], 'L0_ffn_k_scale': _L0_ffn_in['k_scale'], 'L0_ffn_wo': _L0_ffn_in['wo'], 'L0_ffn_ln_g': _L0_ffn_in['ln_g'], 'L0_ffn_ln_b': _L0_ffn_in['ln_b'], 'L0_ffn_w1': _L0_ffn_in['w1'], 'L0_ffn_b1': _L0_ffn_in['b1'], 'L0_ffn_w2': _L0_ffn_in['w2'], 'L0_ffn_b2': _L0_ffn_in['b2'], 'L1_xattn_Wq': _L1_xattn_in['Wq'], 'L1_xattn_bq': _L1_xattn_in['bq'], 'L1_xattn_Wk': _L1_xattn_in['Wk'], 'L1_xattn_bk': _L1_xattn_in['bk'], 'L1_xattn_Wv': _L1_xattn_in['Wv'], 'L1_xattn_bv': _L1_xattn_in['bv'], 'L1_xattn_Wo': _L1_xattn_in['Wo'], 'L1_ffn_gate_W': _L1_ffn_in['gate_W'], 'L1_ffn_w1_e': _L1_ffn_in['w1_e'], 'L1_ffn_w3_e': _L1_ffn_in['w3_e'], 'L1_ffn_w2_e': _L1_ffn_in['w2_e'], 'L1_ffn_w1_s': _L1_ffn_in['w1_s'], 'L1_ffn_w3_s': _L1_ffn_in['w3_s'], 'L1_ffn_w2_s': _L1_ffn_in['w2_s'], 'L2_xattn_Wq': _L2_xattn_in['Wq'], 'L2_xattn_Wk': _L2_xattn_in['Wk'], 'L2_xattn_Wv': _L2_xattn_in['Wv'], 'L2_xattn_Wo': _L2_xattn_in['Wo'], 'L2_xattn_bo': _L2_xattn_in['bo'], 'L2_ffn_router_w': _L2_ffn_in['router_w'], 'L2_ffn_experts_bias': _L2_ffn_in['experts_bias'], 'L2_ffn_w1': _L2_ffn_in['w1'], 'L2_ffn_w3': _L2_ffn_in['w3'], 'L2_ffn_w2': _L2_ffn_in['w2'], 'L2_ffn_sw1': _L2_ffn_in['sw1'], 'L2_ffn_sw3': _L2_ffn_in['sw3'], 'L2_ffn_sw2': _L2_ffn_in['sw2'], 'L3_xattn_Wq': _L3_xattn_in['Wq'], 'L3_xattn_bq': _L3_xattn_in['bq'], 'L3_xattn_Wk': _L3_xattn_in['Wk'], 'L3_xattn_bk': _L3_xattn_in['bk'], 'L3_xattn_Wv': _L3_xattn_in['Wv'], 'L3_xattn_bv': _L3_xattn_in['bv'], 'L3_ffn_Wg': _L3_ffn_in['Wg'], 'L3_ffn_W_in': _L3_ffn_in['W_in'], 'L3_ffn_W_out': _L3_ffn_in['W_out']}

def reference(x, ctx_1024, mask_Bx1xSxS2_ik1, L0_xattn_Wq, L0_xattn_Wk, L0_xattn_Wv, L0_ffn_wqkv, L0_ffn_q_scale, L0_ffn_k_scale, L0_ffn_wo, L0_ffn_ln_g, L0_ffn_ln_b, L0_ffn_w1, L0_ffn_b1, L0_ffn_w2, L0_ffn_b2, L1_xattn_Wq, L1_xattn_bq, L1_xattn_Wk, L1_xattn_bk, L1_xattn_Wv, L1_xattn_bv, L1_xattn_Wo, L1_ffn_gate_W, L1_ffn_w1_e, L1_ffn_w3_e, L1_ffn_w2_e, L1_ffn_w1_s, L1_ffn_w3_s, L1_ffn_w2_s, L2_xattn_Wq, L2_xattn_Wk, L2_xattn_Wv, L2_xattn_Wo, L2_xattn_bo, L2_ffn_router_w, L2_ffn_experts_bias, L2_ffn_w1, L2_ffn_w3, L2_ffn_w2, L2_ffn_sw1, L2_ffn_sw3, L2_ffn_sw2, L3_xattn_Wq, L3_xattn_bq, L3_xattn_Wk, L3_xattn_bk, L3_xattn_Wv, L3_xattn_bv, L3_ffn_Wg, L3_ffn_W_in, L3_ffn_W_out):
    import jax
    import jax.numpy as jnp

    def _L0_xattn_ref(q, k, v, Wq, Wk, Wv):
        import jax, jax.numpy as jnp
        import numpy as np
        BETA = 256
        NUM_HEADS = 16
        NORM = (BETA // NUM_HEADS) ** (-0.5)
        qp = jax.nn.relu(jnp.einsum('bnd,od->bno', q, Wq))
        kp = jax.nn.relu(jnp.einsum('bnd,od->bno', k, Wk))
        vp = jax.nn.relu(jnp.einsum('bnd,od->bno', v, Wv))
        B, N, D = qp.shape
        dh = D // NUM_HEADS
        qh = qp.reshape(B, N, NUM_HEADS, dh)
        kh = kp.reshape(B, N, NUM_HEADS, dh)
        vh = vp.reshape(B, N, NUM_HEADS, vp.shape[-1] // NUM_HEADS)
        E = NORM * jnp.einsum('bqhd,bkhd->bhqk', qh, kh)
        A = jax.nn.softmax(E, axis=-1)
        out = jnp.einsum('bhqk,bkhd->bqhd', A, vh)
        return out.reshape(B, N, -1)

    def _L0_ffn_ref(x, wqkv, q_scale, k_scale, wo, ln_g, ln_b, w1, b1, w2, b2):
        import jax, jax.numpy as jnp
        import numpy as np
        DIM = 256
        DEPTH = 2
        HEADS = 8
        DIM_HEAD = 64
        WINDOW = 128
        INNER = HEADS * DIM_HEAD
        HID = int(DIM * 4 * 2 / 3)
        B, N = (2, 2048)
        QK_SCALE = 8.0

        def shift_token(t):
            t1, t2 = jnp.split(t, 2, axis=-1)
            t2 = jnp.pad(t2, ((0, 0), (1, 0), (0, 0)))[:, :-1]
            return jnp.concatenate([t1, t2], axis=-1)

        def l2norm(t):
            return t / jnp.clip(jnp.linalg.norm(t, axis=-1, keepdims=True), 1e-12)

        def rotate_half(x):
            x1, x2 = jnp.split(x, 2, axis=-1)
            return jnp.concatenate([-x2, x1], axis=-1)

        def rotary_xpos(q, k):
            n = q.shape[-2]
            half_idx = jnp.arange(0, DIM_HEAD, 2, dtype=jnp.float32)
            inv_freq = 1.0 / 10000.0 ** (half_idx / DIM_HEAD)
            t = jnp.arange(n, dtype=jnp.float32)
            freqs = t[:, None] * inv_freq[None, :]
            freqs = jnp.concatenate([freqs, freqs], axis=-1)
            base = (half_idx + 0.4 * DIM_HEAD) / (1.4 * DIM_HEAD)
            power = (t - n // 2) / float(WINDOW // 2)
            scale = base[None, :] ** power[:, None]
            scale = jnp.concatenate([scale, scale], axis=-1)
            cos, sin = (jnp.cos(freqs), jnp.sin(freqs))
            q = q * cos * scale + rotate_half(q) * sin * scale
            k = k * cos / scale + rotate_half(k) * sin / scale
            return (q, k)

        def local_attention(q, k, v):
            b, h, n, d = q.shape
            w = n // WINDOW
            bq = q.reshape(b, h, w, WINDOW, d) * QK_SCALE
            bk = k.reshape(b, h, w, WINDOW, d)
            bv = v.reshape(b, h, w, WINDOW, d)

            def look_around(t):
                p = jnp.pad(t, ((0, 0), (0, 0), (1, 0), (0, 0), (0, 0)))
                return jnp.concatenate([p[:, :, :w], p[:, :, 1:]], axis=3)
            bk, bv = (look_around(bk), look_around(bv))
            bt = jnp.arange(n).reshape(w, WINDOW)
            btp = jnp.pad(bt, ((1, 0), (0, 0)), constant_values=-1)
            btk = jnp.concatenate([btp[:w], btp[1:]], axis=1)
            sim = jnp.einsum('bhwid,bhwjd->bhwij', bq, bk)
            i = bt[:, :, None]
            j = btk[:, None, :]
            mask = (i < j) | (i > j + WINDOW) | (j == -1)
            sim = jnp.where(mask, -jnp.finfo(sim.dtype).max, sim)
            attn = jax.nn.softmax(sim, axis=-1)
            out = jnp.einsum('bhwij,bhwjd->bhwid', attn, bv)
            return out.reshape(b, h, n, d)

        def _layer(x, wqkv, qs, ksc, wo, lg, lb, w1, b1, w2, b2):
            b, n, _ = x.shape
            h = shift_token(x)
            qkv = h @ wqkv
            q, k, v = jnp.split(qkv, 3, axis=-1)
            to_heads = lambda t: t.reshape(b, n, HEADS, DIM_HEAD).transpose(0, 2, 1, 3)
            q, k, v = (to_heads(q), to_heads(k), to_heads(v))
            q = l2norm(q) * qs
            k = l2norm(k) * ksc
            q, k = rotary_xpos(q, k)
            o = local_attention(q, k, v)
            o = o.transpose(0, 2, 1, 3).reshape(b, n, INNER)
            x = x + o @ wo
            h = shift_token(x)
            mu = h.mean(-1, keepdims=True)
            var = h.var(-1, keepdims=True)
            h = (h - mu) / jnp.sqrt(var + 1e-05) * lg + lb
            h = h @ w1 + b1
            a, g = jnp.split(h, 2, axis=-1)
            h = a * jax.nn.gelu(g, approximate=False)
            x = x + h @ w2 + b2
            return x
        for l in range(DEPTH):
            x = _layer(x, wqkv[l], q_scale[l], k_scale[l], wo[l], ln_g[l], ln_b[l], w1[l], b1[l], w2[l], b2[l])
        return x

    def _L1_xattn_ref(query, key, value, mask, Wq, bq, Wk, bk, Wv, bv, Wo):
        import jax, jax.numpy as jnp
        import numpy as np
        HIDDEN = 256
        HEADS = 16
        HEAD_DIM = HIDDEN // HEADS
        SCALE = HEAD_DIM ** (-0.5)
        NEG_INF = -1000000000.0

        def _split_heads(x):
            B, S, _ = x.shape
            return x.reshape(B, S, HEADS, HEAD_DIM).transpose(0, 2, 1, 3)
        B, Sq, _ = query.shape
        q = _split_heads(query @ Wq.T + bq)
        k = _split_heads(key @ Wk.T + bk)
        v = _split_heads(value @ Wv.T + bv)
        scores = jnp.einsum('bhqd,bhkd->bhqk', q, k) * SCALE
        scores = jnp.where(mask == 0, NEG_INF, scores)
        attn = jax.nn.silu(scores)
        out = jnp.einsum('bhqk,bhkd->bhqd', attn, v)
        out = out.transpose(0, 2, 1, 3).reshape(B, Sq, HIDDEN)
        return out @ Wo.T

    def _L1_ffn_ref(hidden_states, gate_W, w1_e, w3_e, w2_e, w1_s, w3_s, w2_s):
        import jax, jax.numpy as jnp
        import numpy as np
        B, S, D, F, E, NS, K = (2, 256, 256, 1024, 8, 8, 2)
        FS = F // NS
        b, s, d = hidden_states.shape
        e = gate_W.shape[0]
        flat = hidden_states.reshape(-1, d)
        T = flat.shape[0]
        logits = (flat @ gate_W.T).astype(jnp.float32)
        probs = jax.nn.softmax(logits, axis=-1)
        top_v, top_i = jax.lax.top_k(probs, K)
        gates = jnp.zeros((T, e), probs.dtype).at[jnp.arange(T)[:, None], top_i].set(top_v)
        g = jax.nn.silu(jnp.einsum('td,edf->etf', flat, w1_e))
        u = jnp.einsum('td,edf->etf', flat, w3_e)
        out_e = jnp.einsum('etf,efd->etd', g * u, w2_e)
        routed = jnp.einsum('te,etd->td', gates, out_e).reshape(b, s, d)
        gs = jax.nn.silu(jnp.einsum('bsd,ndf->nbsf', hidden_states, w1_s))
        us = jnp.einsum('bsd,ndf->nbsf', hidden_states, w3_s)
        shared = jnp.einsum('nbsf,nfd->bsd', gs * us, w2_s) / w1_s.shape[0]
        alpha = 0.5
        return alpha * shared + (1.0 - alpha) * routed

    def _L2_xattn_ref(x, context, Wq, Wk, Wv, Wo, bo):
        import jax, jax.numpy as jnp
        import numpy as np
        DIM = 256
        NUM_HEADS = 8
        HEAD_DIM = 64
        INNER = NUM_HEADS * HEAD_DIM
        B, N, _ = x.shape
        M = context.shape[1]
        scale = HEAD_DIM ** (-0.5)
        q = (x @ Wq).reshape(B, N, NUM_HEADS, HEAD_DIM).transpose(0, 2, 1, 3)
        k = (context @ Wk).reshape(B, M, NUM_HEADS, HEAD_DIM).transpose(0, 2, 1, 3)
        v = (context @ Wv).reshape(B, M, NUM_HEADS, HEAD_DIM).transpose(0, 2, 1, 3)
        attn = jax.nn.softmax(jnp.einsum('bhnd,bhmd->bhnm', q, k) * scale, axis=-1)
        out = jnp.einsum('bhnm,bhmd->bhnd', attn, v)
        out = out.transpose(0, 2, 1, 3).reshape(B, N, INNER)
        return out @ Wo + bo

    def _L2_ffn_ref(x, router_w, experts_bias, w1, w3, w2, sw1, sw3, sw2):
        import jax, jax.numpy as jnp
        import numpy as np
        D, H, E, K, S = (256, 512, 8, 2, 1)
        B, L = (4, 512)
        b, l, d = x.shape
        xf = x.reshape(-1, d)
        sg = jnp.einsum('td,sdh->tsh', xf, sw1)
        su = jnp.einsum('td,sdh->tsh', xf, sw3)
        shared_out = jnp.einsum('tsh,shd->td', jax.nn.silu(sg) * su, sw2)
        logits = xf @ router_w.T + experts_bias
        rw, sel = jax.lax.top_k(logits, K)
        rw = jax.nn.softmax(rw.astype(jnp.float32), axis=-1).astype(x.dtype)
        cw = (jax.nn.one_hot(sel, E, dtype=x.dtype) * rw[..., None]).sum(axis=1)
        g = jnp.einsum('td,edh->teh', xf, w1)
        u = jnp.einsum('td,edh->teh', xf, w3)
        eo = jax.nn.silu(g) * u
        moe_out = jnp.einsum('te,teh,ehd->td', cw, eo, w2)
        return (moe_out + shared_out).reshape(b, l, d)

    def _L3_xattn_ref(q, k, v, Wq, bq, Wk, bk, Wv, bv):
        import jax, jax.numpy as jnp
        import numpy as np
        B, S, D_IN, D_MODEL = (4, 512, 256, 256)
        qp = jnp.einsum('bsd,de->bse', q, Wq) + bq
        kp = jnp.einsum('bsd,de->bse', k, Wk) + bk
        vp = jnp.einsum('bsd,de->bse', v, Wv) + bv
        scale = 1.0 / jnp.sqrt(jnp.asarray(kp.shape[-1], jnp.float32))
        logits = jnp.einsum('bqe,bke->bqk', qp, kp) * scale
        attn = jax.nn.softmax(logits, axis=-1)
        return jnp.einsum('bqk,bke->bqe', attn, vp)

    def _L3_ffn_ref(x, Wg, W_in, W_out):
        import math
        import jax, jax.numpy as jnp
        import numpy as np
        B, T, H = (4, 512, 256)
        E, K, F = (8, 2, 512)
        CAP_FACTOR = 1.25

        def _moe_forward(x, Wg, W_in, W_out):
            b, t, h = x.shape
            xf = x.reshape(-1, h)
            S = xf.shape[0]
            C = int(math.ceil(K * S / E * CAP_FACTOR))
            logits = xf @ Wg
            probs = jax.nn.softmax(logits, axis=-1)
            top_vals, top_idx = jax.lax.top_k(probs, K)
            flat_idx = top_idx.T.reshape(-1)
            onehot = jax.nn.one_hot(flat_idx, E, dtype=jnp.int32)
            cum = jnp.cumsum(onehot, axis=0) - 1
            loc = jnp.take_along_axis(cum, flat_idx[:, None], axis=1)[:, 0]
            loc = loc.reshape(K, S).T
            keep = loc < C
            gates = top_vals * keep.astype(top_vals.dtype)
            denom = jnp.maximum(gates.sum(-1, keepdims=True), 1e-09)
            gates = gates / denom
            loc_c = jnp.where(keep, loc, C)
            e_flat = top_idx.reshape(-1)
            l_flat = loc_c.reshape(-1)
            xk = jnp.broadcast_to(xf[:, None, :], (S, K, h)).reshape(-1, h)
            xk = jnp.where(keep.reshape(-1, 1), xk, 0.0)
            buf = jnp.zeros((E, C + 1, h), x.dtype).at[e_flat, l_flat].set(xk)
            inp = buf[:, :C]
            hid = jnp.einsum('ech,ehf->ecf', inp, W_in)
            a, g = jnp.split(hid, 2, axis=-1)
            hid = jax.nn.gelu(a, approximate=False) * g
            out_e = jnp.einsum('ecf,efh->ech', hid, W_out)
            out_pad = jnp.concatenate([out_e, jnp.zeros((E, 1, h), out_e.dtype)], axis=1)
            gathered = out_pad[e_flat, l_flat].reshape(S, K, h)
            y = (gathered * gates[..., None]).sum(axis=1)
            return y.reshape(b, t, h)
        return _moe_forward(x, Wg, W_in, W_out)
    x = x + _L0_xattn_ref(_layernorm(x, axis=-1), ctx_1024, ctx_1024, L0_xattn_Wq, L0_xattn_Wk, L0_xattn_Wv)
    x = x + _L0_ffn_ref(_layernorm(x, axis=-1), L0_ffn_wqkv, L0_ffn_q_scale, L0_ffn_k_scale, L0_ffn_wo, L0_ffn_ln_g, L0_ffn_ln_b, L0_ffn_w1, L0_ffn_b1, L0_ffn_w2, L0_ffn_b2)
    x = x + _L1_xattn_ref(_layernorm(x, axis=-1), ctx_1024, ctx_1024, mask_Bx1xSxS2_ik1, L1_xattn_Wq, L1_xattn_bq, L1_xattn_Wk, L1_xattn_bk, L1_xattn_Wv, L1_xattn_bv, L1_xattn_Wo)
    x = x + _L1_ffn_ref(_layernorm(x, axis=-1), L1_ffn_gate_W, L1_ffn_w1_e, L1_ffn_w3_e, L1_ffn_w2_e, L1_ffn_w1_s, L1_ffn_w3_s, L1_ffn_w2_s)
    x = x + _L2_xattn_ref(_layernorm(x, axis=-1), ctx_1024, L2_xattn_Wq, L2_xattn_Wk, L2_xattn_Wv, L2_xattn_Wo, L2_xattn_bo)
    x = x + _L2_ffn_ref(_layernorm(x, axis=-1), L2_ffn_router_w, L2_ffn_experts_bias, L2_ffn_w1, L2_ffn_w3, L2_ffn_w2, L2_ffn_sw1, L2_ffn_sw3, L2_ffn_sw2)
    x = x + _L3_xattn_ref(_layernorm(x, axis=-1), ctx_1024, ctx_1024, L3_xattn_Wq, L3_xattn_bq, L3_xattn_Wk, L3_xattn_bk, L3_xattn_Wv, L3_xattn_bv)
    x = x + _L3_ffn_ref(_layernorm(x, axis=-1), L3_ffn_Wg, L3_ffn_W_in, L3_ffn_W_out)
    return x

_drawn_inputs = setup_inputs


def setup_inputs(seed=0):
    import zlib

    import numpy as np

    out = dict(_drawn_inputs(seed))
    spreads = {'L0_ffn_q_scale': (1.0, 0.6),
     'L0_ffn_k_scale': (1.0, 0.6),
     'L0_ffn_ln_g': (1.0, 0.6),
     'L0_ffn_ln_b': (0.0, 0.607),
     'L0_ffn_b1': (0.0, 0.378),
     'L0_ffn_b2': (0.0, 0.1),
     'L2_ffn_experts_bias': (0.0, 0.636)}
    factors = {'L1_ffn_gate_W': 7.626,
     'L1_ffn_w1_e': 6.681,
     'L1_ffn_w3_e': 6.71,
     'L1_ffn_w2_e': 7.98,
     'L1_ffn_w1_s': 8.0,
     'L1_ffn_w3_s': 7.48,
     'L1_ffn_w2_s': 7.663,
     'L2_xattn_bo': 19.601,
     'L2_ffn_router_w': 3.649,
     'L2_ffn_w1': 3.468,
     'L2_ffn_w3': 3.279,
     'L2_ffn_w2': 3.344,
     'L2_ffn_sw3': 2.847,
     'L2_ffn_sw2': 2.93,
     'L3_xattn_Wq': 5.524,
     'L3_xattn_bq': 64.0,
     'L3_xattn_Wk': 6.53,
     'L3_xattn_bk': 64.0,
     'L3_xattn_bv': 15.483}
    for name, (base, spread) in spreads.items():
        noise = np.random.default_rng([zlib.crc32(name.encode()), seed]).standard_normal(out[name].shape)
        drawn = base * np.exp(spread * noise) if base else spread * noise
        out[name] = jnp.asarray(drawn.astype(out[name].dtype))
    for name, factor in factors.items():
        out[name] = (out[name] * factor).astype(out[name].dtype)
    return out
```

```python
from collections import namedtuple
from contextlib import ExitStack, contextmanager

import numpy as np

import concourse.bass as bass
from concourse import mybir

F32 = mybir.dt.float32
I32 = mybir.dt.int32
ALU = mybir.AluOpType
ACT = mybir.ActivationFunctionType
AX = mybir.AxisListType

P = 128
B, N, D = 4, 512, 256
TOK = B * N
NT = N // P
TT = TOK // P
DC = D // P
BANK = 512
EPS = 1e-5
HID = 682
HC = -(-HID // P)
E = 8
TS = 256
ROUTED = 24
SHARED = TOK // TS
CAPACITY = 640
NEG = -1.0e30

Moe = namedtuple("Moe", "gates hidden func shared w13 w2 own_scale shared_scale")


@contextmanager
def stage(nc, tag, *names):
    with ExitStack() as es:
        sems = [es.enter_context(nc.semaphore(f"{tag}_{n}")) for n in names]
        with nc.Block() as block:
            yield [block] + sems
        for s in sems:
            nc.sync.sem_clear(s)
        nc.all_engine_barrier()


class Names:

    def __init__(self):
        self.n = 0

    def next(self, what):
        self.n += 1
        return f"{what}{self.n}"


def load_stage(nc, names, pairs):
    with stage(nc, names.next("load"), "landed") as (block, landed):
        @block.sync
        def _(sp):
            for dst, src in pairs:
                sp.dma_start(dst, src).then_inc(landed, 16)
            sp.wait_ge(landed, 16 * len(pairs))


def layer_norm(nc, names, ident, X, XN, XNT):
    tag = names.next("ln")
    with ExitStack() as es:
        stats = es.enter_context(nc.sbuf_tensor(tag + "_stats", [P, NT, 6], F32))
        mv = es.enter_context(nc.sbuf_tensor(tag + "_mv", [P, NT, 2], F32))
        std = es.enter_context(nc.sbuf_tensor(tag + "_std", [P, NT], F32))
        rstd = es.enter_context(nc.sbuf_tensor(tag + "_rstd", [P, NT], F32))
        eps = es.enter_context(nc.sbuf_tensor(tag + "_eps", [P, 1], F32))
        turned = [es.enter_context(nc.psum_tensor(f"{tag}_turned{c}", [P, N], F32)) for c in range(DC)]
        with stage(nc, tag, "eps_set", "stats_done", "moments_done", "std_done", "rstd_done", "normed", "transposed") as (
                block, eps_set, stats_done, moments_done, std_done, rstd_done, normed, transposed):
            @block.vector
            def _(dve):
                nc.vector.memset(eps[:], EPS).then_inc(eps_set, 1)
                for t in range(NT):
                    nc.vector.bn_stats(stats[:, t, :], X[:, t, :]).then_inc(stats_done, 1)
                dve.wait_ge(stats_done, NT)
                for t in range(NT):
                    nc.vector.bn_aggr(mv[:, t, :], stats[:, t, :]).then_inc(moments_done, 1)
                dve.wait_ge(std_done, 1)
                nc.vector.reciprocal(rstd[:], std[:]).then_inc(rstd_done, 1)
                dve.wait_ge(rstd_done, 1)
                dve.wait_ge(moments_done, NT)
                for t in range(NT):
                    nc.vector.tensor_scalar(XN[:, t, :], X[:, t, :], mv[:, t, 0:1], rstd[:, t:t + 1],
                                            ALU.subtract, ALU.mult).then_inc(normed, 1)
                if XNT is not None:
                    dve.wait_ge(transposed, 2)
                    nc.vector.tensor_copy(XNT[:, 1, :], turned[1][:])

            @block.scalar
            def _(act):
                act.wait_ge(eps_set, 1)
                act.wait_ge(moments_done, NT)
                nc.scalar.activation(std[:], mv[:, :, 1], ACT.Sqrt, bias=eps[:, 0:1]).then_inc(std_done, 1)
                if XNT is not None:
                    act.wait_ge(transposed, 1)
                    nc.scalar.activation(XNT[:, 0, :], turned[0][:], ACT.Copy)

            if XNT is not None:
                @block.tensor
                def _(pe):
                    for c in range(DC):
                        for t in range(NT):
                            pe.wait_ge(normed, t + 1)
                            last = nc.tensor.transpose(turned[c][:, t * P:(t + 1) * P],
                                                       XN[:, t, c * P:(c + 1) * P], ident[:])
                        last.then_inc(transposed, 1)


Job = namedtuple("Job", "dst terms turns relu scale bias add", defaults=((), (), False, 1.0, None, False))


def products(nc, names, ident, jobs):
    tag = names.next("prod")
    on_dve, nth, count = [], [], [0, 0]
    for j, job in enumerate(jobs):
        d = job.bias is not None or job.add or j % 2 == 0
        on_dve.append(d)
        count[d] += 1
        nth.append(count[d])
    with ExitStack() as es:
        banks = [es.enter_context(nc.psum_tensor(f"{tag}_bank{i}", [P, BANK], F32)) for i in range(8)]
        with stage(nc, tag, "filled", "emptied_by_act", "emptied_by_dve") as (
                block, filled, emptied_by_act, emptied_by_dve):
            def bank(j):
                rows, cols = jobs[j].dst.shape[0], jobs[j].dst.shape[-1]
                return banks[j % 8][0:rows, 0:cols]

            @block.tensor
            def _(pe):
                for j, job in enumerate(jobs):
                    if j >= 8:
                        pe.wait_ge(emptied_by_dve if on_dve[j - 8] else emptied_by_act, nth[j - 8])
                    for i, (lhsT, rhs) in enumerate(job.terms):
                        last = nc.tensor.matmul(bank(j), lhsT, rhs, start=(i == 0), stop=(i == len(job.terms) - 1))
                    for i, src in enumerate(job.turns):
                        last = nc.tensor.transpose(banks[j % 8][:, i * P:(i + 1) * P], src, ident[:])
                    last.then_inc(filled, 1)

            @block.scalar
            def _(act):
                for j, job in enumerate(jobs):
                    if not on_dve[j]:
                        act.wait_ge(filled, j + 1)
                        nc.scalar.activation(job.dst, bank(j), ACT.Relu if job.relu else ACT.Copy,
                                             scale=job.scale).then_inc(emptied_by_act, 1)

            @block.vector
            def _(dve):
                for j, job in enumerate(jobs):
                    if on_dve[j]:
                        dve.wait_ge(filled, j + 1)
                        if job.add:
                            ins = nc.vector.tensor_tensor(job.dst, bank(j), job.dst, ALU.add)
                        elif job.bias is not None:
                            ins = nc.vector.tensor_scalar(job.dst, bank(j), job.bias, job.scale, ALU.add, ALU.mult)
                        elif job.relu:
                            ins = nc.vector.tensor_scalar(job.dst, bank(j), job.scale, 0.0, ALU.mult, ALU.max)
                        elif job.scale != 1.0:
                            ins = nc.vector.tensor_scalar(job.dst, bank(j), job.scale, None, ALU.mult)
                        else:
                            ins = nc.vector.tensor_copy(job.dst, bank(j))
                        ins.then_inc(emptied_by_dve, 1)


Unit = namedtuple("Unit", "terms n mask values qt head")


def softmax_attention(nc, names, ident, units, heads, dv, out, residual):
    tag = names.next("attn")
    U = len(units)
    width = heads * dv
    masked = units[0].mask is not None
    with ExitStack() as es:
        def sb(name, shape):
            return es.enter_context(nc.sbuf_tensor(f"{tag}_{name}", shape, F32))

        def ps(name):
            return es.enter_context(nc.psum_tensor(f"{tag}_{name}", [P, BANK], F32))

        S = [ps(f"S{i}") for i in range(3)]
        PT = [ps(f"PT{i}") for i in range(3)]
        O = [ps(f"O{i}") for i in range(2)]
        masked_scores = [sb(f"SM{i}", [P, 2 * P]) for i in range(3)] if masked else S
        probs = sb("probs", [P, 3, BANK])
        probsT = sb("probsT", [P, 3, BANK])
        neg_max = sb("neg_max", [P, 4])
        row_sum = sb("row_sum", [P, NT, heads])
        inv_sum = sb("inv_sum", [P, 2, heads])
        with stage(nc, tag, "scores_ready", "mask_added", "max_ready", "probs_ready", "turned", "evac_act", "evac_dve",
                   "pv_done", "inv_ready", "scaled", "tile_done") as (
                block, scores_ready, mask_added, max_ready, probs_ready, turned, evac_act, evac_dve,
                pv_done, inv_ready, scaled, tile_done):
            first = {}
            last_of = {}
            for i, u in enumerate(units):
                first.setdefault(u.qt, i)
                last_of[u.qt] = i

            def wait_evacuated(eng, i):
                eng.wait_ge(evac_act if i % 2 else evac_dve, i // 2 + 1)

            @block.tensor
            def _(pe):
                for step in range(U + 3):
                    i = step
                    if i < U:
                        if i >= 3:
                            pe.wait_ge(probs_ready, i - 2)
                        u = units[i]
                        for k, (lhsT, rhs) in enumerate(u.terms):
                            ins = nc.tensor.matmul(S[i % 3][:, 0:u.n], lhsT, rhs,
                                                   start=(k == 0), stop=(k == len(u.terms) - 1))
                        ins.then_inc(scores_ready, 1)
                    i = step - 2
                    if 0 <= i < U:
                        pe.wait_ge(probs_ready, i + 1)
                        if i >= 3:
                            wait_evacuated(pe, i - 3)
                        for k in range(units[i].n // P):
                            ins = nc.tensor.transpose(PT[i % 3][:, k * P:(k + 1) * P],
                                                      probs[:, i % 3, k * P:(k + 1) * P], ident[:])
                        ins.then_inc(turned, 1)
                    i = step - 3
                    if 0 <= i < U:
                        u = units[i]
                        wait_evacuated(pe, i)
                        if i == first[u.qt] and u.qt >= 2:
                            pe.wait_ge(tile_done, u.qt - 1)
                        for k, v in enumerate(u.values):
                            ins = nc.tensor.matmul(O[u.qt % 2][:, u.head * dv:(u.head + 1) * dv],
                                                   probsT[:, i % 3, k * P:(k + 1) * P], v,
                                                   start=(k == 0), stop=(k == len(u.values) - 1))
                        ins.then_inc(pv_done, 1)

            @block.scalar
            def _(act):
                for step in range(U + 2):
                    i = step
                    if i < U:
                        u = units[i]
                        act.wait_ge(max_ready, i + 1)
                        if i >= 3:
                            act.wait_ge(turned, i - 2)
                        nc.scalar.activation(probs[:, i % 3, 0:u.n], masked_scores[i % 3][:, 0:u.n], ACT.Exp,
                                             bias=neg_max[:, i % 4:i % 4 + 1],
                                             accum_out=row_sum[:, u.qt, u.head:u.head + 1]).then_inc(probs_ready, 1)
                    i = step - 2
                    if 0 <= i < U and i % 2:
                        act.wait_ge(turned, i + 1)
                        if i >= 3:
                            act.wait_ge(pv_done, i - 2)
                        nc.scalar.activation(probsT[:, i % 3, 0:units[i].n], PT[i % 3][:, 0:units[i].n],
                                             ACT.Copy).then_inc(evac_act, 1)

            @block.vector
            def _(dve):
                for step in range(U + 4):
                    i = step - 4
                    if 0 <= i < U and i == last_of[units[i].qt]:
                        qt = units[i].qt
                        dve.wait_ge(pv_done, i + 1)
                        dve.wait_ge(probs_ready, i + 1)
                        nc.vector.reciprocal(inv_sum[:, qt % 2, :], row_sum[:, qt, :]).then_inc(inv_ready, 1)
                        dve.wait_ge(inv_ready, qt + 1)
                        ins = nc.vector.tensor_tensor(
                            out[:, qt, 0:width].rearrange("p (h v) -> p h v", h=heads),
                            O[qt % 2][:, 0:width].rearrange("p (h v) -> p h v", h=heads),
                            inv_sum[:, qt % 2, :].unsqueeze(2).to_broadcast([P, heads, dv]), ALU.mult)
                        if residual is not None:
                            ins.then_inc(scaled, 1)
                            dve.wait_ge(scaled, qt + 1)
                            ins = nc.vector.tensor_tensor(residual[:, qt, :], residual[:, qt, :], out[:, qt, 0:width],
                                                          ALU.add)
                        ins.then_inc(tile_done, 1)
                    i = step
                    if i < U:
                        u = units[i]
                        dve.wait_ge(scores_ready, i + 1)
                        if masked:
                            if i >= 3:
                                dve.wait_ge(probs_ready, i - 2)
                            nc.vector.tensor_tensor(masked_scores[i % 3][:, 0:u.n], S[i % 3][:, 0:u.n], u.mask,
                                                    ALU.add).then_inc(mask_added, 1)
                            dve.wait_ge(mask_added, i + 1)
                        if i >= 4:
                            dve.wait_ge(probs_ready, i - 3)
                        nc.vector.tensor_reduce(neg_max[:, i % 4:i % 4 + 1], masked_scores[i % 3][:, 0:u.n], AX.X,
                                                ALU.max, negate=True).then_inc(max_ready, 1)
                    i = step - 2
                    if 0 <= i < U and i % 2 == 0:
                        dve.wait_ge(turned, i + 1)
                        if i >= 3:
                            dve.wait_ge(pv_done, i - 2)
                        nc.vector.tensor_copy(probsT[:, i % 3, 0:units[i].n], PT[i % 3][:, 0:units[i].n])\
                            .then_inc(evac_dve, 1)


def silu_attention(nc, names, qT, kT, V, mask, out, heads=16, dh=16):
    tag = names.next("silu")
    units = [(h, kt) for h in range(heads) for kt in range(NT)]
    U = len(units)
    with ExitStack() as es:
        S = [es.enter_context(nc.psum_tensor(f"{tag}_S{i}", [P, N], F32)) for i in range(4)]
        O = [es.enter_context(nc.psum_tensor(f"{tag}_O{i}", [P, BANK], F32)) for i in range(NT)]
        A = es.enter_context(nc.sbuf_tensor(f"{tag}_A", [P, 3, N], F32))
        W = es.enter_context(nc.sbuf_tensor(f"{tag}_W", [P, 3, N], F32))
        with stage(nc, tag, "scores_ready", "silu_done", "masked", "pv_done") as (
                block, scores_ready, silu_done, masked, pv_done):
            @block.tensor
            def _(pe):
                for step in range(U + 2):
                    if step < U:
                        h, kt = units[step]
                        if step >= 4:
                            pe.wait_ge(silu_done, step - 3)
                        r, g = 32 * (h % 4), h // 4
                        nc.tensor.matmul(S[step % 4][:], kT[r:r + dh, g, kt * P:(kt + 1) * P],
                                         qT[r:r + dh, g, :], start=True, stop=True).then_inc(scores_ready, 1)
                    i = step - 2
                    if 0 <= i < U:
                        h, kt = units[i]
                        pe.wait_ge(masked, i + 1)
                        for qt in range(NT):
                            ins = nc.tensor.matmul(O[qt][:, h * dh:(h + 1) * dh], W[:, i % 3, qt * P:(qt + 1) * P],
                                                   V[:, kt, h * dh:(h + 1) * dh], start=(kt == 0), stop=(kt == NT - 1))
                        ins.then_inc(pv_done, 1)

            @block.scalar
            def _(act):
                for i in range(U):
                    act.wait_ge(scores_ready, i + 1)
                    if i >= 3:
                        act.wait_ge(masked, i - 2)
                    nc.scalar.activation(A[:, i % 3, :], S[i % 4][:], ACT.Silu).then_inc(silu_done, 1)

            @block.vector
            def _(dve):
                for i, (h, kt) in enumerate(units):
                    dve.wait_ge(silu_done, i + 1)
                    if i >= 3:
                        dve.wait_ge(pv_done, i - 2)
                    nc.vector.tensor_tensor(W[:, i % 3, :], A[:, i % 3, :], mask[:, kt, :], ALU.mult)\
                        .then_inc(masked, 1)
                dve.wait_ge(pv_done, U)
                for qt in range(NT):
                    nc.vector.tensor_copy(out[:, qt, 0:D], O[qt][:, 0:D])


def turn_jobs(src, dst, chunks):
    return [Job(dst[:, c, :], turns=tuple(src[:, t, c * P:(c + 1) * P] for t in range(NT))) for c in range(chunks)]


def out_projection_jobs(srcT, chunks, weight, residual, ones_row, bias_row):
    jobs = []
    for t in range(NT):
        terms = [(srcT[:, c, t * P:(t + 1) * P], weight[:, c, :]) for c in range(chunks)]
        if bias_row is not None:
            terms.append((ones_row, bias_row))
        jobs.append(Job(residual[:, t, :], terms=tuple(terms), add=True))
    return jobs


def head_major_jobs(dst, xT, weight, groups, relu=False, scale=1.0, bias=None):
    return [Job(dst[:, g, :], terms=tuple((weight[:, c, g * P:(g + 1) * P], xT[:, c, :]) for c in range(DC)),
                relu=relu, scale=scale, bias=None if bias is None else bias[:, g:g + 1]) for g in range(groups)]


def token_major_jobs(dst_of, xT, weight, lo, hi, relu=False, ones_row=None, bias_row=None):
    jobs = []
    for t in range(NT):
        terms = [(xT[:, c, t * P:(t + 1) * P], weight[:, c, lo:hi]) for c in range(DC)]
        if bias_row is not None:
            terms.append((ones_row, bias_row))
        jobs.append(Job(dst_of(t), terms=tuple(terms), relu=relu))
    return jobs


def tiles_of(dram, row, rows):
    return dram[bass.ds(row, rows), :].rearrange("(t p) d -> p t d", p=P)


def store_stage(nc, names, pairs):
    with stage(nc, names.next("store"), "stored") as (block, stored):
        @block.sync
        def _(sp):
            for dst, src in pairs:
                sp.dma_start(dst, src).then_inc(stored, 16)
            sp.wait_ge(stored, 16 * len(pairs))


def rope(nc, names, QK, table_c, table_s, out):
    tag = names.next("rope")
    H, DH = 8, 64
    R = DH // 2
    with ExitStack() as es:
        def sb(name, shape):
            return es.enter_context(nc.sbuf_tensor(f"{tag}_{name}", shape, F32))

        sq = sb("sq", [P, 2, 1024])
        norm = sb("norm", [P, NT, 2 * H])
        root = sb("root", [P, NT, 2 * H])
        inv = sb("inv", [P, NT, 2 * H])
        rot = sb("rot", [P, 2, 1024])
        with stage(nc, tag, "squared", "summed", "rooted", "clipped", "inverted", "scaled", "turned_part",
                   "straight", "done") as (
                block, squared, summed, rooted, clipped, inverted, scaled, turned_part, straight, done):
            def heads(ap):
                return ap.rearrange("p (z h f) -> p z h f", z=2, h=H)

            @block.scalar
            def _(act):
                for t in range(NT):
                    if t >= 2:
                        act.wait_ge(summed, t - 1)
                    nc.scalar.activation(sq[:, t % 2, :], QK[:, t, :], ACT.Square).then_inc(squared, 1)
                act.wait_ge(summed, NT)
                nc.scalar.activation(root[:], norm[:], ACT.Sqrt).then_inc(rooted, 1)

            @block.vector
            def _(dve):
                for t in range(NT):
                    dve.wait_ge(squared, t + 1)
                    nc.vector.tensor_reduce(norm[:, t, :], sq[:, t % 2, :].rearrange("p (h f) -> p h f", f=DH),
                                            AX.X, ALU.add).then_inc(summed, 1)
                dve.wait_ge(rooted, 1)
                nc.vector.tensor_scalar(root[:], root[:], 1e-12, None, ALU.max).then_inc(clipped, 1)
                dve.wait_ge(clipped, 1)
                nc.vector.reciprocal(inv[:], root[:]).then_inc(inverted, 1)
                dve.wait_ge(inverted, 1)
                for t in range(NT):
                    x = QK[:, t, :].rearrange("p (h f) -> p h f", f=DH)
                    nc.vector.tensor_tensor(x, x, inv[:, t, :].unsqueeze(2).to_broadcast([P, 2 * H, DH]),
                                            ALU.mult).then_inc(scaled, 1)
                    dve.wait_ge(scaled, t + 1)
                    for lo in (0, R):
                        for z in range(2):
                            src = heads(QK[:, t, :])[:, z, :, R - lo:DH - lo]
                            dst = heads(rot[:, t % 2, :])[:, z, :, lo:lo + R]
                            tab = table_s[:, t, z, lo:lo + R].unsqueeze(1).to_broadcast([P, H, R])
                            nc.vector.tensor_tensor(dst, src, tab, ALU.mult).then_inc(turned_part, 1)
                    dve.wait_ge(turned_part, 4 * (t + 1))
                    dve.wait_ge(straight, 2 * (t + 1))
                    nc.vector.tensor_tensor(out[:, t, :], out[:, t, :], rot[:, t % 2, :], ALU.add).then_inc(done, 1)
                    dve.wait_ge(done, t + 1)

            @block.gpsimd
            def _(pool):
                for t in range(NT):
                    pool.wait_ge(scaled, t + 1)
                    for z in range(2):
                        tab = table_c[:, t, z, :].unsqueeze(1).to_broadcast([P, H, DH])
                        nc.gpsimd.tensor_tensor(heads(out[:, t, :])[:, z], heads(QK[:, t, :])[:, z], tab,
                                                ALU.mult).then_inc(straight, 1)


def norm_shifted(nc, names, mean_mat, HT, HN, gain, shift):
    tag = names.next("nsh")
    with ExitStack() as es:
        MU = es.enter_context(nc.psum_tensor(f"{tag}_mu", [P, N], F32))
        VAR = es.enter_context(nc.psum_tensor(f"{tag}_var", [P, N], F32))
        dev = es.enter_context(nc.sbuf_tensor(f"{tag}_dev", [P, DC, N], F32))
        sq = es.enter_context(nc.sbuf_tensor(f"{tag}_sq", [P, DC, N], F32))
        std = es.enter_context(nc.sbuf_tensor(f"{tag}_std", [P, N], F32))
        eps = es.enter_context(nc.sbuf_tensor(f"{tag}_eps", [P, 1], F32))
        with stage(nc, tag, "mean_ready", "dev_ready", "squared", "var_ready", "std_ready", "inverted", "scaled",
                   "eps_set") as (
                block, mean_ready, dev_ready, squared, var_ready, std_ready, inverted, scaled, eps_set):
            @block.tensor
            def _(pe):
                for c in range(DC):
                    ins = nc.tensor.matmul(MU[:], mean_mat[:], HT[:, c, 0:N], start=(c == 0), stop=(c == DC - 1))
                ins.then_inc(mean_ready, 1)
                for c in range(DC):
                    pe.wait_ge(squared, c + 1)
                    ins = nc.tensor.matmul(VAR[:], mean_mat[:], sq[:, c, :], start=(c == 0), stop=(c == DC - 1))
                ins.then_inc(var_ready, 1)

            @block.vector
            def _(dve):
                nc.vector.memset(eps[:], EPS).then_inc(eps_set, 1)
                dve.wait_ge(mean_ready, 1)
                for c in range(DC):
                    nc.vector.tensor_tensor(dev[:, c, :], HT[:, c, 0:N], MU[:], ALU.subtract).then_inc(dev_ready, 1)
                dve.wait_ge(std_ready, 1)
                nc.vector.reciprocal(std[:], std[:]).then_inc(inverted, 1)
                dve.wait_ge(inverted, 1)
                dve.wait_ge(squared, DC)
                for c in range(DC):
                    nc.vector.tensor_tensor(sq[:, c, :], dev[:, c, :], std[:], ALU.mult).then_inc(scaled, 1)

            @block.scalar
            def _(act):
                for c in range(DC):
                    act.wait_ge(dev_ready, c + 1)
                    nc.scalar.activation(sq[:, c, :], dev[:, c, :], ACT.Square).then_inc(squared, 1)
                act.wait_ge(var_ready, 1)
                act.wait_ge(eps_set, 1)
                nc.scalar.activation(std[:], VAR[:], ACT.Sqrt, bias=eps[:, 0:1]).then_inc(std_ready, 1)
                for c in range(DC):
                    act.wait_ge(scaled, c + 1)
                    nc.scalar.activation(HN[:, c, :], sq[:, c, :], ACT.Identity, bias=shift[:, c:c + 1],
                                         scale=gain[:, c:c + 1])


def gated_mlp(nc, names, HN, w1, b1a, b1g, w2, ones_row, b2_row, hidden, Y):
    tag = names.next("mlp")
    with ExitStack() as es:
        G = [es.enter_context(nc.psum_tensor(f"{tag}_G{i}", [P, N], F32)) for i in range(3)]
        A = [es.enter_context(nc.psum_tensor(f"{tag}_A{i}", [P, N], F32)) for i in range(3)]
        O = [es.enter_context(nc.psum_tensor(f"{tag}_O{i}", [P, BANK], F32)) for i in range(2)]
        gate = es.enter_context(nc.sbuf_tensor(f"{tag}_gate", [P, 2, N], F32))
        with stage(nc, tag, "pair_ready", "gate_ready", "hidden_ready", "out_ready", "added") as (
                block, pair_ready, gate_ready, hidden_ready, out_ready, added):
            rows = [min(P, HID - f * P) for f in range(HC)]

            @block.tensor
            def _(pe):
                for f, m in enumerate(rows):
                    if f >= 3:
                        pe.wait_ge(hidden_ready, f - 2)
                    for bank, lo in ((G[f % 3], HID + f * P), (A[f % 3], f * P)):
                        for c in range(DC):
                            ins = nc.tensor.matmul(bank[0:m, :], w1[:, c, lo:lo + m], HN[:, c, :],
                                                   start=(c == 0), stop=(c == DC - 1))
                    ins.then_inc(pair_ready, 1)
                for t in range(NT):
                    if t == 0:
                        pe.wait_ge(hidden_ready, HC)
                    if t >= 2:
                        pe.wait_ge(added, t - 1)
                    o = O[t % 2][:, 0:D]
                    for f, m in enumerate(rows):
                        nc.tensor.matmul(o, hidden[0:m, f, t * P:(t + 1) * P], w2[0:m, f, :],
                                         start=(f == 0), stop=False)
                    nc.tensor.matmul(o, ones_row, b2_row, start=False, stop=True).then_inc(out_ready, 1)

            @block.scalar
            def _(act):
                for f, m in enumerate(rows):
                    act.wait_ge(pair_ready, f + 1)
                    if f >= 2:
                        act.wait_ge(hidden_ready, f - 1)
                    nc.scalar.activation(gate[0:m, f % 2, :], G[f % 3][0:m, :], ACT.Gelu,
                                         bias=b1g[0:m, f:f + 1]).then_inc(gate_ready, 1)

            @block.vector
            def _(dve):
                for f, m in enumerate(rows):
                    dve.wait_ge(gate_ready, f + 1)
                    nc.vector.scalar_tensor_tensor(hidden[0:m, f, :], A[f % 3][0:m, :], b1a[0:m, f:f + 1],
                                                   gate[0:m, f % 2, :], ALU.add, ALU.mult).then_inc(hidden_ready, 1)
                for t in range(NT):
                    dve.wait_ge(out_ready, t + 1)
                    nc.vector.tensor_tensor(Y[:, t, :], Y[:, t, :], O[t % 2][:, 0:D], ALU.add).then_inc(added, 1)


def route(nc, names, C, moe, logits_dram, bias_bc, slot, gate, tile_expert):
    tag = names.next("route")
    TE = TT * E
    with ExitStack() as es:
        def sb(name, shape):
            return es.enter_context(nc.sbuf_tensor(f"{tag}_{name}", shape, F32))

        L = sb("L", [P, TT, E])
        L2 = sb("L2", [P, TT, E])
        prio = sb("prio", [P, TT, E])
        top = sb("top", [P, TT])
        best = sb("best", [P, TT])
        sel = sb("sel", [P, 2, TT, E])
        expo = sb("expo", [P, TT, E])
        work = sb("work", [P, 2, TT, E])
        s = sb("s", [P, 2, TT])
        den = sb("den", [P, TT])
        inv = sb("inv", [P, TT])
        loc = sb("loc", [P, 2, TT])
        keep = sb("keep", [P, 2, TT])
        scan = [sb(f"scan{i}", [P, 3, TT, E]) for i in range(2)]
        tiles = sb("tiles", [P, E])
        tcmp = sb("tcmp", [P, E, E])
        start_t = sb("start_t", [P, E])
        end_t = sb("end_t", [P, E])
        place = sb("place", [P, 2, TT])
        te = sb("te", [P, ROUTED + SHARED])
        tecmp = sb("tecmp", [P, ROUTED, E])
        prefix = es.enter_context(nc.psum_tensor(f"{tag}_prefix", [P, BANK], F32))
        total = es.enter_context(nc.psum_tensor(f"{tag}_total", [P, BANK], F32))
        with stage(nc, tag, "landed", "chain", "shifted", "expo_done", "selected", "counted") as (
                block, landed, chain, shifted, expo_done, selected, counted):
            flat_sel = sel[:].rearrange("p c t e -> p (c t e)")

            @block.sync
            def _(sp):
                sp.dma_start(L[:], logits_dram.rearrange("(t p) e -> p t e", p=P)).then_inc(landed, 16)
                sp.wait_ge(landed, 16)

            @block.scalar
            def _(act):
                act.wait_ge(shifted, 1)
                nc.scalar.activation(expo[:], L2[:], ACT.Exp).then_inc(expo_done, 1)

            @block.tensor
            def _(pe):
                pe.wait_ge(selected, 1)
                nc.tensor.matmul(prefix[:, 0:2 * TE], C["upper"], flat_sel, start=True, stop=True)
                nc.tensor.matmul(total[:, 0:2 * TE], C["ones"], flat_sel, start=True, stop=True).then_inc(counted, 1)

            @block.vector
            def _(dve):
                done = [0]

                def link(ins):
                    done[0] += 1
                    ins.then_inc(chain, 1)
                    dve.wait_ge(chain, done[0])

                def over_e(ap):
                    return ap.unsqueeze(2).to_broadcast([P, TT, E])

                v = nc.vector
                dve.wait_ge(landed, 16)
                if bias_bc is not None:
                    link(v.tensor_tensor(L[:], L[:], bias_bc.unsqueeze(1).to_broadcast([P, TT, E]), ALU.add))
                link(v.tensor_reduce(top[:], L[:], AX.X, ALU.max))
                link(v.tensor_tensor(L2[:], L[:], over_e(top[:]), ALU.subtract))
                link(v.tensor_copy(L[:], L2[:]))
                v.sem_inc(shifted, 1)
                countdown = C["countdown"].unsqueeze(1).to_broadcast([P, TT, E])
                for c in range(2):
                    if c:
                        link(v.tensor_reduce(top[:], L[:], AX.X, ALU.max))
                    else:
                        link(v.memset(top[:], 0.0))
                    link(v.tensor_tensor(prio[:], L[:], over_e(top[:]), ALU.is_equal))
                    link(v.tensor_tensor(prio[:], prio[:], countdown, ALU.mult))
                    link(v.tensor_reduce(best[:], prio[:], AX.X, ALU.max))
                    link(v.tensor_tensor(sel[:, c], prio[:], over_e(best[:]), ALU.is_equal))
                    if c == 0:
                        link(v.scalar_tensor_tensor(L[:], sel[:, 0], NEG, L[:], ALU.mult, ALU.add))
                v.sem_inc(selected, 1)
                dve.wait_ge(expo_done, 1)
                for c in range(2):
                    link(v.tensor_tensor(work[:, c], sel[:, c], expo[:], ALU.mult))
                link(v.tensor_reduce(s[:], work[:], AX.X, ALU.add))
                if moe.gates == "top2":
                    link(v.tensor_tensor(den[:], s[:, 0], s[:, 1], ALU.add))
                else:
                    link(v.tensor_reduce(den[:], expo[:], AX.X, ALU.add))
                link(v.reciprocal(inv[:], den[:]))
                for c in range(2):
                    link(v.tensor_tensor(s[:, c], s[:, c], inv[:], ALU.mult))
                dve.wait_ge(counted, 1)
                for i in range(2):
                    link(v.memset(scan[i][:], 0.0))
                link(v.tensor_copy(scan[0][:, 1:3].rearrange("p c t e -> p (c t e)"), total[:, 0:2 * TE]))
                a, b = scan
                hop = 1
                while hop < 2 * TT:
                    fa, fb = (x[:].rearrange("p c t e -> p (c t e)") for x in (a, b))
                    link(v.tensor_tensor(fb[:, TE:3 * TE], fa[:, TE:3 * TE],
                                         fa[:, TE - hop * E:3 * TE - hop * E], ALU.add))
                    a, b = b, a
                    hop *= 2
                fa, fb = (x[:].rearrange("p c t e -> p (c t e)") for x in (a, b))
                count = fa[:, 3 * TE - E:3 * TE]
                fw = work[:].rearrange("p c t e -> p (c t e)")
                link(v.tensor_tensor(fb[:, TE:3 * TE], fa[:, TE - E:3 * TE - E], prefix[:, 0:2 * TE], ALU.add))
                link(v.tensor_tensor(fw, fb[:, TE:3 * TE], flat_sel, ALU.mult))
                link(v.tensor_reduce(loc[:], work[:], AX.X, ALU.add))
                if moe.gates == "capacity":
                    link(v.tensor_scalar(keep[:], loc[:], float(CAPACITY), None, ALU.is_lt))
                    link(v.tensor_tensor(s[:], s[:], keep[:], ALU.mult))
                    link(v.tensor_tensor(den[:], s[:, 0], s[:, 1], ALU.add))
                    link(v.tensor_scalar(den[:], den[:], 1e-9, None, ALU.max))
                    link(v.reciprocal(inv[:], den[:]))
                    for c in range(2):
                        link(v.tensor_tensor(s[:, c], s[:, c], inv[:], ALU.mult))
                link(v.tensor_scalar(gate, s[:], moe.own_scale, None, ALU.mult))
                link(v.tensor_tensor(tcmp[:], count.unsqueeze(2).to_broadcast([P, E, E]),
                                     C["tile_steps"].unsqueeze(1).to_broadcast([P, E, E]), ALU.is_gt))
                link(v.tensor_reduce(tiles[:], tcmp[:], AX.X, ALU.add))
                link(v.tensor_tensor(tcmp[:], tiles[:].unsqueeze(1).to_broadcast([P, E, E]), C["before"], ALU.mult))
                link(v.tensor_reduce(start_t[:], tcmp[:], AX.X, ALU.add))
                link(v.tensor_tensor(end_t[:], start_t[:], tiles[:], ALU.add))
                link(v.tensor_scalar(start_t[:], start_t[:], float(TS), None, ALU.mult))
                for c in range(2):
                    link(v.tensor_tensor(work[:, c], sel[:, c], start_t[:].unsqueeze(1).to_broadcast([P, TT, E]),
                                         ALU.mult))
                link(v.tensor_reduce(place[:], work[:], AX.X, ALU.add))
                link(v.tensor_tensor(place[:], place[:], loc[:], ALU.add))
                link(v.tensor_copy(slot, place[:]))
                link(v.memset(te[:], float(E)))
                link(v.tensor_tensor(tecmp[:], end_t[:].unsqueeze(1).to_broadcast([P, ROUTED, E]),
                                     C["tile_ids"].unsqueeze(2).to_broadcast([P, ROUTED, E]), ALU.is_le))
                link(v.tensor_reduce(te[:, 0:ROUTED], tecmp[:], AX.X, ALU.add))
                link(v.tensor_scalar(te[:, 0:ROUTED], te[:, 0:ROUTED], float(E - 1), None, ALU.min))
                link(v.tensor_copy(tile_expert, te[:]))


def scatter_rows(nc, names, xs, slot):
    tag = names.next("scat")
    with ExitStack() as es:
        rows = es.enter_context(nc.sbuf_tensor(f"{tag}_rows", [P, TT, D], F32))
        with stage(nc, tag, "landed", "scattered") as (block, landed, scattered):
            @block.sync
            def _(sp):
                sp.dma_start(rows[:], xs[ROUTED * TS:ROUTED * TS + TOK, :].rearrange("(t p) d -> p t d", p=P))\
                    .then_inc(landed, 16)
                sp.wait_ge(landed, 16)

            @block.gpsimd
            def _(pool):
                pool.wait_ge(landed, 16)
                for t in range(TT):
                    for c in range(2):
                        pool.indirect_dma_start(xs, bass.IndirectOffsetOnAxis(ap=slot[:, c, t:t + 1], axis=0),
                                                rows[:, t, :], None).then_inc(scattered, 16)
                pool.wait_ge(scattered, 2 * TT * 16)


def expert_tiles(nc, names, ident, moe, xs, os_, tile_expert):
    tag = names.next("exp")
    NF = moe.hidden // P
    TILES = ROUTED + (SHARED if moe.shared else 0)
    PAIRS = TILES // 2
    HALF = TS // P
    RING, ORING = 4, 2
    assert NF % RING == 0
    with ExitStack() as es:
        def sb(name, shape):
            return es.enter_context(nc.sbuf_tensor(f"{tag}_{name}", shape, F32))

        def ps(name):
            return es.enter_context(nc.psum_tensor(f"{tag}_{name}", [P, BANK], F32))

        w13 = [sb(f"w13_{u}", [P, 2, DC, moe.hidden]) for u in range(2)]
        w2 = [sb(f"w2_{u}", [P, NF, D]) for u in range(2)]
        X = [sb(f"X{u}", [P, HALF, D]) for u in range(2)]
        XT = [sb(f"XT{u}", [P, DC, TS]) for u in range(2)]
        hidden = [sb(f"hidden{u}", [P, NF, TS]) for u in range(2)]
        gated = sb("gated", [P, 2, TS])
        Y = [sb(f"Y{u}", [P, HALF, D]) for u in range(2)]
        turned = ps("turned")
        H = [ps(f"H{i}") for i in range(RING)]
        O = [ps(f"O{i}") for i in range(ORING)]
        names_ = ["weights0", "weights1", "rows0", "rows1", "rows_turned", "turned_copied", "pair_ready", "gate_ready",
                  "hidden_ready", "out_ready", "out_copied", "stored0", "stored1"]
        with stage(nc, tag, *names_) as (block, weights0, weights1, rows0, rows1, rows_turned, turned_copied,
                                         pair_ready, gate_ready, hidden_ready, out_ready, out_copied,
                                         stored0, stored1):
            weights, rows, stored = (weights0, weights1), (rows0, rows1), (stored0, stored1)

            @block.sync
            def _(sp):
                def load(i, u):
                    e = sp.value_load(tile_expert[0:1, bass.ds(i, 1)], min_val=0,
                                      max_val=E if moe.shared else E - 1)
                    sp.dma_start(X[u][:], xs[bass.ds(i * TS, TS), :].rearrange("(s p) d -> p s d", p=P))\
                        .then_inc(rows[u], 16)
                    sp.dma_start(w13[u][:].rearrange("p a c f -> p (a c f)"),
                                 moe.w13[bass.ds(e, 1)].rearrange("o p f -> (o p) f")).then_inc(weights[u], 16)
                    sp.dma_start(w2[u][:].rearrange("p k d -> p (k d)"),
                                 moe.w2[bass.ds(e, 1)].rearrange("o p f -> (o p) f")).then_inc(weights[u], 16)

                def store(i, u):
                    sp.wait_ge(out_copied, ORING + HALF * (i + 1))
                    sp.dma_start(os_[bass.ds(i * TS, TS), :].rearrange("(s p) d -> p s d", p=P), Y[u][:])\
                        .then_inc(stored[u], 16)

                for u in range(2):
                    sp.sem_inc(stored[u], 16)
                    load(u, u)
                with sp.Fori(0, PAIRS - 1) as pair:
                    for u in range(2):
                        store(2 * pair + u, u)
                        load(2 * pair + u + 2, u)
                for u in range(2):
                    store(TILES - 2 + u, u)
                for u in range(2):
                    sp.wait_ge(stored[u], 16 * (PAIRS + 1))

            @block.tensor
            def _(pe):
                def turn_rows(i, u, nth):
                    pe.wait_ge(rows[u], 16 * nth)
                    for c in range(DC):
                        for s in range(HALF):
                            ins = nc.tensor.transpose(turned[:, c * TS + s * P:c * TS + (s + 1) * P],
                                                      X[u][:, s, c * P:(c + 1) * P], ident[:])
                    ins.then_inc(rows_turned, 1)

                def tile(pair, u, last):
                    i = 2 * pair + u
                    pe.wait_ge(turned_copied, i + 1)
                    pe.wait_ge(weights[u], 32 * (pair + 1))
                    for f in range(NF):
                        pe.wait_ge(hidden_ready, i * NF + f + 1)
                        for a in range(2):
                            for c in range(DC):
                                ins = nc.tensor.matmul(H[f % RING][:, a * TS:(a + 1) * TS],
                                                       w13[u][:, a, c, f * P:(f + 1) * P], XT[u][:, c, :],
                                                       start=(c == 0), stop=(c == DC - 1))
                        ins.then_inc(pair_ready, 1)
                    if not last:
                        turn_rows(i + 1, 1 - u, pair + 1 + u)
                    for s in range(HALF):
                        if s == 0:
                            pe.wait_ge(hidden_ready, (i + 1) * NF + RING)
                        pe.wait_ge(out_copied, HALF * i + s + 1)
                        for f in range(NF):
                            ins = nc.tensor.matmul(O[s][:, 0:D], hidden[u][:, f, s * P:(s + 1) * P], w2[u][:, f, :],
                                                   start=(f == 0), stop=(f == NF - 1))
                        ins.then_inc(out_ready, 1)

                turn_rows(0, 0, 1)
                with pe.Fori(0, PAIRS - 1) as pair:
                    for u in range(2):
                        tile(pair, u, False)
                tile(PAIRS - 1, 0, False)
                tile(PAIRS - 1, 1, True)

            @block.scalar
            def _(act):
                act.sem_inc(out_copied, ORING)
                with act.Fori(0, PAIRS) as pair:
                    for u in range(2):
                        i = 2 * pair + u
                        for f in range(NF):
                            act.wait_ge(pair_ready, i * NF + f + 1)
                            act.wait_ge(hidden_ready, i * NF + f + RING - 1)
                            nc.scalar.activation(gated[:, f % 2, :], H[f % RING][:, 0:TS], moe.func)\
                                .then_inc(gate_ready, 1)
                        for s in range(HALF):
                            act.wait_ge(out_ready, HALF * i + s + 1)
                            act.wait_ge(stored[u], 16 * (pair + 1))
                            nc.scalar.activation(Y[u][:, s, :], O[s][:, 0:D], ACT.Copy).then_inc(out_copied, 1)

            @block.vector
            def _(dve):
                def copy_turned(i, u):
                    dve.wait_ge(rows_turned, i + 1)
                    nc.vector.tensor_copy(XT[u][:], turned[:].rearrange("p (c n) -> p c n", c=DC))\
                        .then_inc(turned_copied, 1)

                def tile(pair, u, last):
                    i = 2 * pair + u
                    for f in range(NF):
                        dve.wait_ge(gate_ready, i * NF + f + 1)
                        nc.vector.tensor_tensor(hidden[u][:, f, :], gated[:, f % 2, :], H[f % RING][:, TS:2 * TS],
                                                ALU.mult).then_inc(hidden_ready, 1)
                    if not last:
                        copy_turned(i + 1, 1 - u)

                dve.sem_inc(hidden_ready, RING)
                copy_turned(0, 0)
                with dve.Fori(0, PAIRS - 1) as pair:
                    for u in range(2):
                        tile(pair, u, False)
                tile(PAIRS - 1, 0, False)
                tile(PAIRS - 1, 1, True)


def combine(nc, names, moe, xres, os_, slot, gate, dst):
    tag = names.next("comb")
    G = 4
    with ExitStack() as es:
        X = es.enter_context(nc.sbuf_tensor(f"{tag}_X", [P, TT, D], F32))
        S = es.enter_context(nc.sbuf_tensor(f"{tag}_S", [P, TT, D], F32))
        R = es.enter_context(nc.sbuf_tensor(f"{tag}_R", [P, G, 2, D], F32))
        with stage(nc, tag, "landed", "gathered0", "gathered1", "gathered2", "gathered3", "added", "row_done",
                   "stored") as (
                block, landed, g0, g1, g2, g3, added, row_done, stored):
            gathered = (g0, g1, g2, g3)
            loads = 2 if moe.shared else 1

            @block.sync
            def _(sp):
                sp.dma_start(X[:], xres.rearrange("(t p) d -> p t d", p=P)).then_inc(landed, 16)
                if moe.shared:
                    sp.dma_start(S[:], os_[ROUTED * TS:ROUTED * TS + TOK, :].rearrange("(t p) d -> p t d", p=P))\
                        .then_inc(landed, 16)
                sp.wait_ge(landed, 16 * loads)
                sp.wait_ge(row_done, TT)
                sp.dma_start(dst.rearrange("(t p) d -> p t d", p=P), X[:]).then_inc(stored, 16)
                sp.wait_ge(stored, 16)

            @block.gpsimd
            def _(pool):
                for t in range(TT):
                    if t >= G:
                        pool.wait_ge(row_done, t - G + 1)
                    for c in range(2):
                        pool.indirect_dma_start(R[:, t % G, c, :], None, os_,
                                                bass.IndirectOffsetOnAxis(ap=slot[:, c, t:t + 1], axis=0))\
                            .then_inc(gathered[t % G], 16)

            @block.vector
            def _(dve):
                done = 0
                dve.wait_ge(landed, 16 * loads)
                for t in range(TT):
                    dve.wait_ge(gathered[t % G], 32 * (t // G + 1))
                    terms = [(R[:, t % G, c, :], gate[:, c, t:t + 1]) for c in range(2)]
                    if moe.shared:
                        terms.append((S[:, t, :], moe.shared_scale))
                    for k, (row, g) in enumerate(terms):
                        ins = nc.vector.scalar_tensor_tensor(X[:, t, :], row, g, X[:, t, :], ALU.mult, ALU.add)
                        if k < len(terms) - 1:
                            done += 1
                            ins.then_inc(added, 1)
                            dve.wait_ge(added, done)
                    ins.then_inc(row_done, 1)


def program(nc, A, out, stop):
    names = Names()
    xres = nc.dram_tensor("xres", [TOK, D], F32, kind="Internal").ap()
    yres = nc.dram_tensor("yres", [TOK, D], F32, kind="Internal").ap()
    xs = nc.dram_tensor("xs", [(ROUTED + SHARED) * TS, D], F32, kind="Internal").ap()
    os_ = nc.dram_tensor("os", [(ROUTED + SHARED) * TS, D], F32, kind="Internal").ap()
    logits = nc.dram_tensor("logits", [TOK, E], F32, kind="Internal").ap()
    with ExitStack() as outer:
        def sbo(name, shape, dt=F32):
            return outer.enter_context(nc.sbuf_tensor(name, shape, dt))

        const_sb = sbo("const_sb", [P, A["consts"].shape[1]])
        slot = sbo("slot", [P, 2, TT], I32)
        gate = sbo("gate", [P, 2, TT])
        tile_expert = sbo("tile_expert", [P, ROUTED + SHARED], I32)
        C, at = {}, 0
        for name, n in CONSTS:
            C[name] = const_sb[:, at:at + n]
            at += n
        ident = C["ident"]
        C["before"] = C["before"].rearrange("p (a b) -> p a b", a=E)
        ones_row = C["ones"][0:1, :]
        load_stage(nc, names, [(const_sb[:], A["consts"])])

        with ExitStack() as es:
            zeros = es.enter_context(nc.sbuf_tensor("zeros", [P, 8 * D], F32))
            with stage(nc, "zero", "set", "stored") as (block, zeros_set, stored):
                @block.vector
                def _(dve):
                    nc.vector.memset(zeros[:], 0.0).then_inc(zeros_set, 1)

                @block.sync
                def _(sp):
                    sp.wait_ge(zeros_set, 1)
                    for i in range(ROUTED * TS // (8 * P)):
                        sp.dma_start(xs[i * 8 * P:(i + 1) * 8 * P, :].rearrange("(p t) d -> p (t d)", p=P),
                                     zeros[:]).then_inc(stored, 16)
                    sp.wait_ge(stored, 16 * (ROUTED * TS // (8 * P)))

        def finish(src):
            with ExitStack() as es:
                t = es.enter_context(nc.sbuf_tensor(names.next("fin"), [P, TT, D], F32))
                load_stage(nc, names, [(t[:], src.rearrange("(t p) d -> p t d", p=P))])
                store_stage(nc, names, [(out.rearrange("(t p) d -> p t d", p=P), t[:])])

        def batch_phase(weights, work, body):
            with ExitStack() as es:
                W = {n: es.enter_context(nc.sbuf_tensor(names.next("w_" + n), list(A[n].shape), F32)) for n in weights}
                if weights:
                    load_stage(nc, names, [(W[n][:], A[n]) for n in weights])
                T = {n: es.enter_context(nc.sbuf_tensor(names.next("t_" + n), shape, dt))
                     for n, (shape, dt) in work.items()}
                with nc.Fori(0, B) as b:
                    body(b, W, T)

        tok = ([P, NT, D], F32)
        wid = ([P, DC, N], F32)
        quad = ([P, 4, N], F32)

        def l0_cross(b, W, T):
            load_stage(nc, names, [(T["X"][:], tiles_of(A["x"], b * N, N)),
                                   (T["ctxT"][:].rearrange("p c n -> p (c n)"),
                                    A["ctxT"][bass.ds(b, 1)].rearrange("o p f -> (o p) f"))])
            layer_norm(nc, names, ident, T["X"], T["XN"], T["XNT"])
            V = T["V"]
            products(nc, names, ident,
                     head_major_jobs(T["qT"], T["XNT"], W["L0_xattn_Wq"], 4, relu=True, scale=0.25)
                     + head_major_jobs(T["kT"], T["ctxT"], W["L0_xattn_Wk"], 4, relu=True)
                     + token_major_jobs(lambda t: V[:, t, 0:D], T["ctxT"], W["L0_xattn_Wv"], 0, D, relu=True))
            units = []
            for qt in range(NT):
                for h in range(16):
                    r, g = 32 * (h % 4), h // 4
                    units.append(Unit([(T["qT"][r:r + 16, g, qt * P:(qt + 1) * P], T["kT"][r:r + 16, g, :])], N, None,
                                      [V[:, kt, h * 16:(h + 1) * 16] for kt in range(NT)], qt, h))
            softmax_attention(nc, names, ident, units, 16, 16, T["ON"], T["X"])
            layer_norm(nc, names, ident, T["X"], T["XN"], None)
            store_stage(nc, names, [(tiles_of(xres, b * N, N), T["X"][:]), (tiles_of(yres, b * N, N), T["XN"][:])])

        batch_phase(["L0_xattn_Wq", "L0_xattn_Wk", "L0_xattn_Wv"],
                    {"X": tok, "XN": tok, "XNT": wid, "ctxT": wid, "qT": quad, "kT": quad, "V": quad, "ON": quad},
                    l0_cross)
        if stop == 0:
            return finish(xres)

        ffn_weights = ["wqkv", "wo", "w1", "b1a", "b1g", "w2", "b2", "ln_g", "ln_b", "qk", "qk_sw"]
        with ExitStack() as es:
            W = {n: es.enter_context(nc.sbuf_tensor("w0_" + n, list(A["f_" + n].shape[1:]), F32)) for n in ffn_weights}
            T = {n: es.enter_context(nc.sbuf_tensor("t0_" + n, shape, F32)) for n, shape in {
                "Y": [P, NT, D], "HT": [P, DC, N + 1], "QK": [P, NT, 1024], "QKR": [P, NT, 1024], "V": [P, NT, 512],
                "qT": [P, 4, N], "kT": [P, 4, N], "ON": [P, NT, 512], "ONT": [P, 4, N], "HN": [P, DC, N],
                "hidden": [P, HC, N], "tab_c": [P, NT, 2, 64], "tab_s": [P, NT, 2, 64]}.items()}
            rope_c = C["rope_c"].rearrange("p (t z f) -> p t z f", t=NT, z=2)
            rope_s = C["rope_s"].rearrange("p (t z f) -> p t z f", t=NT, z=2)
            with nc.Fori(0, 2) as depth:
                pairs = []
                for n in ffn_weights:
                    dst, src = W[n][:], A["f_" + n]
                    if len(dst.shape) == 3:
                        dst = dst.rearrange("p a b -> p (a b)")
                    if len(src.shape) == 4:
                        src = src.rearrange("l p a b -> l p (a b)")
                    pairs.append((dst, src[bass.ds(depth, 1)].rearrange("o p f -> (o p) f")))
                load_stage(nc, names, pairs)
                with stage(nc, names.next("tab"), "tables") as (block, tables):
                    @block.vector
                    def _(dve):
                        nc.vector.memset(T["HT"][:, 1, 0:1], 0.0)
                        for t in range(NT):
                            nc.vector.tensor_tensor(T["tab_c"][:, t], rope_c[:, t],
                                                    W["qk"][:].rearrange("p (z f) -> p z f", z=2), ALU.mult)
                            nc.vector.tensor_tensor(T["tab_s"][:, t], rope_s[:, t],
                                                    W["qk_sw"][:].rearrange("p (z f) -> p z f", z=2), ALU.mult)
                with nc.Fori(0, B) as b:
                    Y, HT, QK, V = T["Y"], T["HT"], T["QK"], T["V"]
                    shifted_jobs = [Job(HT[:, c, c:c + N], turns=tuple(Y[:, t, c * P:(c + 1) * P] for t in range(NT)))
                                    for c in range(DC)]
                    load_stage(nc, names, [(Y[:], tiles_of(yres, b * N, N))])
                    products(nc, names, ident, shifted_jobs)
                    xT = HT[:, :, 0:N]
                    products(nc, names, ident,
                             token_major_jobs(lambda t: QK[:, t, 0:512], xT, W["wqkv"], 0, 512)
                             + token_major_jobs(lambda t: QK[:, t, 512:1024], xT, W["wqkv"], 512, 1024)
                             + token_major_jobs(lambda t: V[:, t, :], xT, W["wqkv"], 1024, 1536))
                    rope(nc, names, QK, T["tab_c"], T["tab_s"], T["QKR"])
                    products(nc, names, ident, turn_jobs(T["QKR"], T["qT"], 4)
                             + turn_jobs(T["QKR"][:, :, 512:1024], T["kT"], 4))
                    units = []
                    for w in range(NT):
                        for h in range(8):
                            r, g = 64 * (h % 2), h // 2
                            lo = max(w - 1, 0)
                            units.append(Unit([(T["qT"][r:r + 64, g, w * P:(w + 1) * P],
                                                T["kT"][r:r + 64, g, lo * P:(w + 1) * P])], (w + 1 - lo) * P,
                                              C["mask"] if w else C["mask"][:, P:2 * P],
                                              [V[:, kt, h * 64:(h + 1) * 64] for kt in range(lo, w + 1)], w, h))
                    softmax_attention(nc, names, ident, units, 8, 64, T["ON"], None)
                    products(nc, names, ident, turn_jobs(T["ON"], T["ONT"], 4))
                    products(nc, names, ident, out_projection_jobs(T["ONT"], 4, W["wo"], Y, None, None))
                    products(nc, names, ident, shifted_jobs)
                    norm_shifted(nc, names, C["mean"], HT, T["HN"], W["ln_g"], W["ln_b"])
                    gated_mlp(nc, names, T["HN"], W["w1"], W["b1a"], W["b1g"], W["w2"], ones_row,
                              W["b2"][0:1, :], T["hidden"], Y)
                    store_stage(nc, names, [(tiles_of(yres, b * N, N), Y[:])])

        def add_stage(X, Y):
            with stage(nc, names.next("add"), "unused") as (block, _unused):
                @block.vector
                def _(dve):
                    nc.vector.tensor_tensor(X[:], X[:], Y[:], ALU.add)

        if stop == 1:
            with ExitStack() as es:
                X = es.enter_context(nc.sbuf_tensor("dbgX", [P, TT, D], F32))
                Y = es.enter_context(nc.sbuf_tensor("dbgY", [P, TT, D], F32))
                load_stage(nc, names, [(X[:], xres.rearrange("(t p) d -> p t d", p=P)),
                                       (Y[:], yres.rearrange("(t p) d -> p t d", p=P))])
                add_stage(X, Y)
                store_stage(nc, names, [(out.rearrange("(t p) d -> p t d", p=P), X[:])])
            return

        def router_tail(b, T, router):
            layer_norm(nc, names, ident, T["X"], T["XN"], T["XNT"])
            LG = T["LG"]
            products(nc, names, ident, token_major_jobs(lambda t: LG[:, t, :], T["XNT"], router, 0, E))
            store_stage(nc, names, [(tiles_of(xres, b * N, N), T["X"][:]),
                                    (tiles_of(xs, ROUTED * TS + b * N, N), T["XN"][:]),
                                    (tiles_of(logits, b * N, N), LG[:])])

        def experts(moe, bias_bc, dst):
            route(nc, names, C, moe, logits, bias_bc, slot[:], gate[:], tile_expert[:])
            scatter_rows(nc, names, xs, slot)
            expert_tiles(nc, names, ident, moe, xs, os_, tile_expert)
            combine(nc, names, moe, xres, os_, slot, gate, dst)

        def load_x_ctx(b, T, more=()):
            load_stage(nc, names, [(T["X"][:], tiles_of(xres, b * N, N)),
                                   (T["ctxT"][:].rearrange("p c n -> p (c n)"),
                                    A["ctxT"][bass.ds(b, 1)].rearrange("o p f -> (o p) f"))] + list(more))

        base = {"X": tok, "XN": tok, "XNT": wid, "ctxT": wid, "LG": ([P, NT, E], F32)}

        def l1_cross(b, W, T):
            load_x_ctx(b, T, [(T["XN"][:], tiles_of(yres, b * N, N)),
                              (T["mask_int"][:].rearrange("p k q -> p (k q)"),
                               A["maskT"][bass.ds(b, 1)].rearrange("o p f -> (o p) f"))])
            with stage(nc, names.next("add"), "unused") as (block, _unused):
                @block.vector
                def _(dve):
                    nc.vector.tensor_tensor(T["X"][:], T["X"][:], T["XN"][:], ALU.add)
                    nc.vector.tensor_scalar(T["mask"][:], T["mask_int"][:], 0.0, None, ALU.not_equal)
            layer_norm(nc, names, ident, T["X"], T["XN"], T["XNT"])
            V = T["V"]
            products(nc, names, ident,
                     head_major_jobs(T["qT"], T["XNT"], W["L1_xattn_Wq"], 4, scale=0.25, bias=W["L1_xattn_bq"])
                     + head_major_jobs(T["kT"], T["ctxT"], W["L1_xattn_Wk"], 4, bias=W["L1_xattn_bk"])
                     + token_major_jobs(lambda t: V[:, t, 0:D], T["ctxT"], W["L1_xattn_Wv"], 0, D,
                                        ones_row=ones_row, bias_row=W["L1_xattn_bv"][0:1, :]))
            silu_attention(nc, names, T["qT"], T["kT"], V, T["mask"], T["ON"])
            products(nc, names, ident, turn_jobs(T["ON"], T["ONT"], DC))
            products(nc, names, ident, out_projection_jobs(T["ONT"], DC, W["L1_xattn_Wo"], T["X"], None, None))
            router_tail(b, T, W["L1_ffn_gate_W"])

        batch_phase(["L1_xattn_Wq", "L1_xattn_bq", "L1_xattn_Wk", "L1_xattn_bk", "L1_xattn_Wv", "L1_xattn_bv",
                     "L1_xattn_Wo", "L1_ffn_gate_W"],
                    dict(base, qT=quad, kT=quad, V=quad, ON=quad, ONT=quad, mask_int=([P, NT, N], I32), mask=quad),
                    l1_cross)
        if stop == 2:
            return finish(xres)
        experts(Moe("softmax", 1024, ACT.Silu, True, A["L1_w13"], A["L1_w2"], 0.5, 0.5 / 8), None,
                xres if stop != 3 else out)
        if stop == 3:
            return

        def l2_cross(b, W, T):
            load_x_ctx(b, T)
            layer_norm(nc, names, ident, T["X"], T["XN"], T["XNT"])
            V = T["V"]
            products(nc, names, ident,
                     head_major_jobs(T["qT"], T["XNT"], W["L2_xattn_Wq"], 4, scale=0.125)
                     + head_major_jobs(T["kT"], T["ctxT"], W["L2_xattn_Wk"], 4)
                     + token_major_jobs(lambda t: V[:, t, :], T["ctxT"], W["L2_xattn_Wv"], 0, 512))
            units = []
            for qt in range(NT):
                for h in range(8):
                    r, g = 64 * (h % 2), h // 2
                    units.append(Unit([(T["qT"][r:r + 64, g, qt * P:(qt + 1) * P], T["kT"][r:r + 64, g, :])], N, None,
                                      [V[:, kt, h * 64:(h + 1) * 64] for kt in range(NT)], qt, h))
            softmax_attention(nc, names, ident, units, 8, 64, T["ON"], None)
            products(nc, names, ident, turn_jobs(T["ON"], T["ONT"], 4))
            products(nc, names, ident, out_projection_jobs(T["ONT"], 4, W["L2_xattn_Wo"], T["X"], ones_row,
                                                           W["L2_xattn_bo"][0:1, :]))
            router_tail(b, T, W["L2_ffn_router_w"])

        batch_phase(["L2_xattn_Wq", "L2_xattn_Wk", "L2_xattn_Wv", "L2_xattn_Wo", "L2_xattn_bo", "L2_ffn_router_w"],
                    dict(base, qT=quad, kT=quad, V=quad, ON=quad, ONT=quad), l2_cross)
        if stop == 4:
            return finish(xres)
        with ExitStack() as es:
            ebias = es.enter_context(nc.sbuf_tensor("expert_bias", [P, E], F32))
            load_stage(nc, names, [(ebias[:], A["L2_ffn_experts_bias"].to_broadcast([P, E]))])
            experts(Moe("top2", 512, ACT.Silu, True, A["L2_w13"], A["L2_w2"], 1.0, 1.0), ebias[:],
                    xres if stop != 5 else out)
        if stop == 5:
            return

        def l3_cross(b, W, T):
            load_x_ctx(b, T)
            layer_norm(nc, names, ident, T["X"], T["XN"], T["XNT"])
            V = T["V"]
            products(nc, names, ident,
                     head_major_jobs(T["qT"], T["XNT"], W["L3_xattn_Wq"], DC, scale=0.0625, bias=W["L3_xattn_bq"])
                     + head_major_jobs(T["kT"], T["ctxT"], W["L3_xattn_Wk"], DC, bias=W["L3_xattn_bk"])
                     + token_major_jobs(lambda t: V[:, t, 0:D], T["ctxT"], W["L3_xattn_Wv"], 0, D,
                                        ones_row=ones_row, bias_row=W["L3_xattn_bv"][0:1, :]))
            units = [Unit([(T["qT"][:, c, qt * P:(qt + 1) * P], T["kT"][:, c, :]) for c in range(DC)], N, None,
                          [V[:, kt, 0:D] for kt in range(NT)], qt, 0) for qt in range(NT)]
            softmax_attention(nc, names, ident, units, 1, D, T["ON"], T["X"])
            router_tail(b, T, W["L3_ffn_Wg"])

        batch_phase(["L3_xattn_Wq", "L3_xattn_bq", "L3_xattn_Wk", "L3_xattn_bk", "L3_xattn_Wv", "L3_xattn_bv",
                     "L3_ffn_Wg"],
                    dict(base, qT=quad, kT=quad, V=quad, ON=quad), l3_cross)
        if stop == 6:
            return finish(xres)
        experts(Moe("capacity", 512, ACT.Gelu, False, A["L3_w13"], A["L3_w2"], 1.0, 0.0), None, out)


CONSTS = [("ident", P), ("ones", P), ("upper", P), ("mean", P), ("mask", 2 * P), ("rope_c", NT * 2 * 64),
          ("rope_s", NT * 2 * 64), ("countdown", E), ("tile_steps", E), ("before", E * E), ("tile_ids", ROUTED)]


def constants():
    p = np.arange(P)
    pos = (np.arange(NT)[None, :] * P + p[:, None]).astype(np.float32)
    half = np.arange(0, 64, 2, dtype=np.float32)
    inv_freq = (np.float32(1.0) / np.float32(10000.0) ** (half / np.float32(64))).astype(np.float32)
    freqs = (pos[..., None] * inv_freq).astype(np.float32).astype(np.float64)
    freqs = np.concatenate([freqs, freqs], -1)
    base = (half.astype(np.float64) + 0.4 * 64) / (1.4 * 64)
    scale = base[None, None, :] ** ((pos[..., None].astype(np.float64) - N // 2) / 64.0)
    scale = np.concatenate([scale, scale], -1)
    sign = np.where(np.arange(64) < 32, -1.0, 1.0)
    rope_c = np.stack([np.cos(freqs) * scale * 8.0, np.cos(freqs) / scale], 2)
    rope_s = np.stack([np.sin(freqs) * scale * 8.0 * sign, np.sin(freqs) / scale * sign], 2)
    prev = np.where(p[:, None] > p[None, :], NEG, 0.0)
    own = np.where(p[:, None] < p[None, :], NEG, 0.0)
    one = np.ones((P, 1))
    tabs = {
        "ident": np.eye(P), "ones": np.ones((P, P)), "upper": (p[:, None] < p[None, :]),
        "mean": np.full((P, P), 1.0 / D), "mask": np.concatenate([prev, own], 1),
        "rope_c": rope_c.reshape(P, -1), "rope_s": rope_s.reshape(P, -1),
        "countdown": one * (E - np.arange(E)), "tile_steps": one * (TS * np.arange(E)),
        "before": one * (np.arange(E)[None, :] < np.arange(E)[:, None]).reshape(1, -1),
        "tile_ids": one * np.arange(ROUTED),
    }
    return np.concatenate([np.asarray(tabs[n], np.float32).reshape(P, k) for n, k in CONSTS], 1)


def rows(w):
    w = np.asarray(w)
    return np.ascontiguousarray(w.reshape(-1, P, w.shape[-1]).transpose(1, 0, 2))


def pad_heads(w):
    w = np.asarray(w).reshape(-1, 16, 16)
    out = np.zeros((w.shape[0], 16, 32), w.dtype)
    out[:, :, :16] = w
    return out.reshape(w.shape[0], 512)


def column(v):
    v = np.asarray(v)
    return np.ascontiguousarray(v.reshape(-1, P).T)


def layout(i):
    i = {k: np.asarray(v) for k, v in i.items()}
    A = {"consts": constants(), "x": i["x"].reshape(TOK, D)}
    A["ctxT"] = np.ascontiguousarray(i["ctx_1024"].reshape(B, N, DC, P).transpose(0, 3, 2, 1)).reshape(B, P, DC * N)
    A["maskT"] = np.ascontiguousarray(i["mask_Bx1xSxS2_ik1"].reshape(B, N, NT, P).transpose(0, 3, 2, 1))\
        .reshape(B, P, NT * N)
    for n in ("Wq", "Wk"):
        A["L0_xattn_" + n] = rows(pad_heads(i["L0_xattn_" + n].T))
        A["L1_xattn_" + n] = rows(pad_heads(i["L1_xattn_" + n].T))
        A["L2_xattn_" + n] = rows(i["L2_xattn_" + n])
        A["L3_xattn_" + n] = rows(i["L3_xattn_" + n])
    for n in ("bq", "bk"):
        A["L1_xattn_" + n] = column(pad_heads(i["L1_xattn_" + n].reshape(1, D)).reshape(-1))
        A["L3_xattn_" + n] = column(i["L3_xattn_" + n])
    A["L0_xattn_Wv"] = rows(i["L0_xattn_Wv"].T)
    A["L1_xattn_Wv"] = rows(i["L1_xattn_Wv"].T)
    A["L1_xattn_Wo"] = rows(i["L1_xattn_Wo"].T)
    A["L2_xattn_Wv"] = rows(i["L2_xattn_Wv"])
    A["L2_xattn_Wo"] = rows(i["L2_xattn_Wo"])
    A["L3_xattn_Wv"] = rows(i["L3_xattn_Wv"])
    for n in ("L1_xattn_bv", "L2_xattn_bo", "L3_xattn_bv"):
        A[n] = i[n].reshape(1, D)
    A["L1_ffn_gate_W"] = rows(i["L1_ffn_gate_W"].T)
    A["L2_ffn_router_w"] = rows(i["L2_ffn_router_w"].T)
    A["L3_ffn_Wg"] = rows(i["L3_ffn_Wg"])
    A["L2_ffn_experts_bias"] = i["L2_ffn_experts_bias"].reshape(1, E)

    f = {n: i["L0_ffn_" + n] for n in ("wqkv", "q_scale", "k_scale", "wo", "ln_g", "ln_b", "w1", "b1", "w2", "b2")}

    def padded(v, n):
        out = np.zeros((n,) + v.shape[1:], v.dtype)
        out[:v.shape[0]] = v
        return out

    A["f_wqkv"] = np.stack([rows(w) for w in f["wqkv"]])
    A["f_wo"] = np.stack([rows(w) for w in f["wo"]])
    A["f_w1"] = np.stack([rows(w) for w in f["w1"]])
    A["f_w2"] = np.stack([rows(padded(w, HC * P)) for w in f["w2"]])
    A["f_b1a"] = np.stack([column(padded(v[:HID], HC * P)) for v in f["b1"]])
    A["f_b1g"] = np.stack([column(padded(v[HID:], HC * P)) for v in f["b1"]])
    A["f_b2"] = f["b2"].reshape(2, 1, D)
    A["f_ln_g"] = np.stack([column(v) for v in f["ln_g"]])
    A["f_ln_b"] = np.stack([column(v) for v in f["ln_b"]])
    qk = np.stack([f["q_scale"], f["k_scale"]], 1)
    swapped = np.concatenate([qk[..., 32:], qk[..., :32]], -1)
    A["f_qk"] = np.ascontiguousarray(np.broadcast_to(qk.reshape(2, 1, 128), (2, P, 128)))
    A["f_qk_sw"] = np.ascontiguousarray(np.broadcast_to(swapped.reshape(2, 1, 128), (2, P, 128)))

    def expert_weights(w1, w3, w2):
        w13 = np.stack([w1, w3], 1).reshape(w1.shape[0], 2, DC, P, -1).transpose(0, 3, 1, 2, 4)
        w2 = w2.reshape(w2.shape[0], -1, P, D).transpose(0, 2, 1, 3)
        return (np.ascontiguousarray(w13).reshape(w13.shape[0], P, -1),
                np.ascontiguousarray(w2).reshape(w2.shape[0], P, -1))

    def beside(w):
        return w.transpose(1, 0, 2).reshape(1, D, -1)

    A["L1_w13"], A["L1_w2"] = expert_weights(
        np.concatenate([i["L1_ffn_w1_e"], beside(i["L1_ffn_w1_s"])]),
        np.concatenate([i["L1_ffn_w3_e"], beside(i["L1_ffn_w3_s"])]),
        np.concatenate([i["L1_ffn_w2_e"], i["L1_ffn_w2_s"].reshape(1, -1, D)]))
    A["L2_w13"], A["L2_w2"] = expert_weights(
        np.concatenate([i["L2_ffn_w1"], i["L2_ffn_sw1"]]), np.concatenate([i["L2_ffn_w3"], i["L2_ffn_sw3"]]),
        np.concatenate([i["L2_ffn_w2"], i["L2_ffn_sw2"]]))
    A["L3_w13"], A["L3_w2"] = expert_weights(i["L3_ffn_W_in"][:, :, :512], i["L3_ffn_W_in"][:, :, 512:],
                                             i["L3_ffn_W_out"])
    return A


STOP = None


def kernel(**inputs):
    import concourse.bacc as _bacc
    from concourse.bass_utils import run_bass_kernel_spmd as _run

    nc = _bacc.Bacc("TRN2", target_bir_lowering=False, num_devices=1)
    arrays, aps = {}, {}
    for name, a in layout(inputs).items():
        arrays["in_" + name] = a
        aps[name] = nc.dram_tensor("in_" + name, a.shape, mybir.dt.from_np(a.dtype), kind="ExternalInput").ap()
    out = nc.dram_tensor("out_x", (TOK, D), F32, kind="ExternalOutput").ap()
    program(nc, aps, out, STOP)
    r = _run(nc, [arrays], core_ids=[0])
    return r.results[0]["out_x"].reshape(B, N, D)
```

```python
from collections import namedtuple
from contextlib import ExitStack, contextmanager

import numpy as np

import concourse.bass as bass
from concourse import mybir

F32 = mybir.dt.float32
I32 = mybir.dt.int32
ALU = mybir.AluOpType
ACT = mybir.ActivationFunctionType
AX = mybir.AxisListType

P = 128
B, N, D = 4, 512, 256
TOK = B * N
NT = N // P
TT = TOK // P
DC = D // P
BANK = 512
EPS = 1e-5
HID = 682
HC = -(-HID // P)
E = 8
TS = 256
ROUTED = 24
SHARED = TOK // TS
CAPACITY = 640
NEG = -1.0e30

Moe = namedtuple("Moe", "gates hidden func shared w13 w2 own_scale shared_scale")


@contextmanager
def stage(nc, tag, *names):
    with ExitStack() as es:
        sems = [es.enter_context(nc.semaphore(f"{tag}_{n}")) for n in names]
        with nc.Block() as block:
            yield [block] + sems
        for s in sems:
            nc.sync.sem_clear(s)
        nc.all_engine_barrier()


class Names:

    def __init__(self):
        self.n = 0

    def next(self, what):
        self.n += 1
        return f"{what}{self.n}"


def load_stage(nc, names, pairs):
    with stage(nc, names.next("load"), "landed") as (block, landed):
        @block.sync
        def _(sp):
            for dst, src in pairs:
                sp.dma_start(dst, src).then_inc(landed, 16)
            sp.wait_ge(landed, 16 * len(pairs))


def layer_norm(nc, names, ident, X, XN, XNT):
    tag = names.next("ln")
    with ExitStack() as es:
        stats = es.enter_context(nc.sbuf_tensor(tag + "_stats", [P, NT, 6], F32))
        mv = es.enter_context(nc.sbuf_tensor(tag + "_mv", [P, NT, 2], F32))
        std = es.enter_context(nc.sbuf_tensor(tag + "_std", [P, NT], F32))
        rstd = es.enter_context(nc.sbuf_tensor(tag + "_rstd", [P, NT], F32))
        eps = es.enter_context(nc.sbuf_tensor(tag + "_eps", [P, 1], F32))
        turned = [es.enter_context(nc.psum_tensor(f"{tag}_turned{c}", [P, N], F32)) for c in range(DC)]
        with stage(nc, tag, "eps_set", "stats_done", "moments_done", "std_done", "rstd_done", "normed", "transposed") as (
                block, eps_set, stats_done, moments_done, std_done, rstd_done, normed, transposed):
            @block.vector
            def _(dve):
                nc.vector.memset(eps[:], EPS).then_inc(eps_set, 1)
                for t in range(NT):
                    nc.vector.bn_stats(stats[:, t, :], X[:, t, :]).then_inc(stats_done, 1)
                dve.wait_ge(stats_done, NT)
                for t in range(NT):
                    nc.vector.bn_aggr(mv[:, t, :], stats[:, t, :]).then_inc(moments_done, 1)
                dve.wait_ge(std_done, 1)
                nc.vector.reciprocal(rstd[:], std[:]).then_inc(rstd_done, 1)
                dve.wait_ge(rstd_done, 1)
                dve.wait_ge(moments_done, NT)
                for t in range(NT):
                    nc.vector.tensor_scalar(XN[:, t, :], X[:, t, :], mv[:, t, 0:1], rstd[:, t:t + 1],
                                            ALU.subtract, ALU.mult).then_inc(normed, 1)
                if XNT is not None:
                    dve.wait_ge(transposed, 2)
                    nc.vector.tensor_copy(XNT[:, 1, :], turned[1][:])

            @block.scalar
            def _(act):
                act.wait_ge(eps_set, 1)
                act.wait_ge(moments_done, NT)
                nc.scalar.activation(std[:], mv[:, :, 1], ACT.Sqrt, bias=eps[:, 0:1]).then_inc(std_done, 1)
                if XNT is not None:
                    act.wait_ge(transposed, 1)
                    nc.scalar.activation(XNT[:, 0, :], turned[0][:], ACT.Copy)

            if XNT is not None:
                @block.tensor
                def _(pe):
                    for c in range(DC):
                        for t in range(NT):
                            pe.wait_ge(normed, t + 1)
                            last = nc.tensor.transpose(turned[c][:, t * P:(t + 1) * P],
                                                       XN[:, t, c * P:(c + 1) * P], ident[:])
                        last.then_inc(transposed, 1)


Job = namedtuple("Job", "dst terms turns relu scale bias add", defaults=((), (), False, 1.0, None, False))


def products(nc, names, ident, jobs):
    tag = names.next("prod")
    on_dve, nth, count = [], [], [0, 0]
    for j, job in enumerate(jobs):
        d = job.bias is not None or job.add or j % 2 == 0
        on_dve.append(d)
        count[d] += 1
        nth.append(count[d])
    with ExitStack() as es:
        banks = [es.enter_context(nc.psum_tensor(f"{tag}_bank{i}", [P, BANK], F32)) for i in range(8)]
        with stage(nc, tag, "filled", "emptied_by_act", "emptied_by_dve") as (
                block, filled, emptied_by_act, emptied_by_dve):
            def bank(j):
                rows, cols = jobs[j].dst.shape[0], jobs[j].dst.shape[-1]
                return banks[j % 8][0:rows, 0:cols]

            @block.tensor
            def _(pe):
                for j, job in enumerate(jobs):
                    if j >= 8:
                        pe.wait_ge(emptied_by_dve if on_dve[j - 8] else emptied_by_act, nth[j - 8])
                    for i, (lhsT, rhs) in enumerate(job.terms):
                        last = nc.tensor.matmul(bank(j), lhsT, rhs, start=(i == 0), stop=(i == len(job.terms) - 1))
                    for i, src in enumerate(job.turns):
                        last = nc.tensor.transpose(banks[j % 8][:, i * P:(i + 1) * P], src, ident[:])
                    last.then_inc(filled, 1)

            @block.scalar
            def _(act):
                for j, job in enumerate(jobs):
                    if not on_dve[j]:
                        act.wait_ge(filled, j + 1)
                        nc.scalar.activation(job.dst, bank(j), ACT.Relu if job.relu else ACT.Copy,
                                             scale=job.scale).then_inc(emptied_by_act, 1)

            @block.vector
            def _(dve):
                for j, job in enumerate(jobs):
                    if on_dve[j]:
                        dve.wait_ge(filled, j + 1)
                        if job.add:
                            ins = nc.vector.tensor_tensor(job.dst, bank(j), job.dst, ALU.add)
                        elif job.bias is not None:
                            ins = nc.vector.tensor_scalar(job.dst, bank(j), job.bias, job.scale, ALU.add, ALU.mult)
                        elif job.relu:
                            ins = nc.vector.tensor_scalar(job.dst, bank(j), job.scale, 0.0, ALU.mult, ALU.max)
                        elif job.scale != 1.0:
                            ins = nc.vector.tensor_scalar(job.dst, bank(j), job.scale, None, ALU.mult)
                        else:
                            ins = nc.vector.tensor_copy(job.dst, bank(j))
                        ins.then_inc(emptied_by_dve, 1)


Unit = namedtuple("Unit", "terms n lo mask qt head")
Group = namedtuple("Group", "heads outputs parts")


def mask_queries(nc, pool, q_masked, source, head_mask, target, heads, per_group):
    for h in range(heads):
        nc.gpsimd.tensor_scalar(target[:, h, :], source[:, h // per_group, :],
                                head_mask[:, h % per_group:h % per_group + 1], 1.0,
                                ALU.mult, ALU.mult).then_inc(q_masked, 1)


def softmax_attention(nc, names, ident, units, groups, V, outT, row_sum, masking=None):
    tag = names.next("attn")
    U = len(units)
    masked = units[0].mask is not None
    slots = len(groups[0].heads)
    last_unit, group_of = {}, {}
    for g, group in enumerate(groups):
        for h in group.heads:
            group_of[h] = g
    for i, u in enumerate(units):
        last_unit[group_of[u.head]] = i
    part_at, copy_at, step = {}, {}, 0
    for g, group in enumerate(groups):
        step = max(step, last_unit[g] + 4)
        for k in range(len(group.parts)):
            part_at.setdefault(step, []).append((g, k))
            step += 1
        copy_at.setdefault(step, []).append(g)
    steps = step + 1
    with ExitStack() as es:
        def sb(name, shape):
            return es.enter_context(nc.sbuf_tensor(f"{tag}_{name}", shape, F32))

        def ps(name):
            return es.enter_context(nc.psum_tensor(f"{tag}_{name}", [P, BANK], F32))

        S = [ps(f"S{i}") for i in range(3)]
        PT = [ps(f"PT{i}") for i in range(3)]
        O = [ps(f"O{i}") for i in range(2)]
        masked_scores = [sb(f"SM{i}", [P, 2 * P]) for i in range(3)] if masked else S
        probs = sb("probs", [P, 3, BANK])
        probsT = sb("probsT", [P, 2 * slots, NT, N])
        neg_max = sb("neg_max", [P, 4])
        with stage(nc, tag, "q_masked", "scores_ready", "mask_added", "max_ready", "probs_ready", "turned", "evac_act",
                   "evac_dve", "pv_done", "out_copied") as (
                block, q_masked, scores_ready, mask_added, max_ready, probs_ready, turned, evac_act, evac_dve,
                pv_done, out_copied):
            if masking is not None:
                @block.gpsimd
                def _(pool):
                    mask_queries(nc, pool, q_masked, *masking)

            def evac_dst(u):
                slot = (group_of[u.head] % 2) * slots + groups[group_of[u.head]].heads.index(u.head)
                return probsT[:, slot, u.lo:u.lo + u.n // P, u.qt * P:(u.qt + 1) * P]

            def evac_src(i):
                return PT[i % 3][:, 0:units[i].n].rearrange("p (k q) -> p k q", q=P)

            def wait_evacuated(eng, i):
                eng.wait_ge(evac_act if i % 2 else evac_dve, i // 2 + 1)

            def wait_slot_free(eng, i):
                if group_of[units[i].head] >= 2:
                    eng.wait_ge(pv_done, group_of[units[i].head] - 1)

            @block.tensor
            def _(pe):
                for step in range(steps):
                    i = step
                    if i < U:
                        u = units[i]
                        if masking is not None and (i == 0 or units[i - 1].head != u.head):
                            pe.wait_ge(q_masked, u.head + 1)
                        if i >= 3:
                            pe.wait_ge(probs_ready, i - 2)
                        for k, (lhsT, rhs) in enumerate(u.terms):
                            ins = nc.tensor.matmul(S[i % 3][:, 0:u.n], lhsT, rhs,
                                                   start=(k == 0), stop=(k == len(u.terms) - 1))
                        ins.then_inc(scores_ready, 1)
                    i = step - 2
                    if 0 <= i < U:
                        pe.wait_ge(probs_ready, i + 1)
                        if i >= 3:
                            wait_evacuated(pe, i - 3)
                        for k in range(units[i].n // P):
                            ins = nc.tensor.transpose(PT[i % 3][:, k * P:(k + 1) * P],
                                                      probs[:, i % 3, k * P:(k + 1) * P], ident[:])
                        ins.then_inc(turned, 1)
                    for g, k in part_at.get(step, ()):
                        group = groups[g]
                        if k == 0:
                            for j in (last_unit[g], last_unit[g] - 1):
                                if j >= 0:
                                    wait_evacuated(pe, j)
                            if g >= 2:
                                pe.wait_ge(out_copied, g - 1)
                        (q0, q1), tiles = group.parts[k]
                        for kt in tiles:
                            for o, row, (v0, v1), h in group.outputs:
                                slot = (g % 2) * slots + group.heads.index(h)
                                ins = nc.tensor.matmul(O[o % 2][row:row + v1 - v0, q0:q1], V[:, kt, v0:v1],
                                                       probsT[:, slot, kt, q0:q1],
                                                       start=(first_tile(group, k) and kt == tiles[0]),
                                                       stop=(last_tile(group, k) and kt == tiles[-1]))
                        if k == len(group.parts) - 1:
                            ins.then_inc(pv_done, 1)

            def copy_out(eng_copy, g):
                outs = sorted({o for o, *_ in groups[g].outputs})
                for o in outs:
                    ins = eng_copy(outT[:, o, :], O[o % 2][:])
                return ins

            @block.scalar
            def _(act):
                for step in range(steps):
                    i = step
                    if i < U:
                        u = units[i]
                        act.wait_ge(max_ready, i + 1)
                        if i >= 3:
                            act.wait_ge(turned, i - 2)
                        nc.scalar.activation(probs[:, i % 3, 0:u.n], masked_scores[i % 3][:, 0:u.n], ACT.Exp,
                                             bias=neg_max[:, i % 4:i % 4 + 1],
                                             accum_out=row_sum[:, u.qt, u.head:u.head + 1]).then_inc(probs_ready, 1)
                    i = step - 2
                    if 0 <= i < U and i % 2:
                        act.wait_ge(turned, i + 1)
                        wait_slot_free(act, i)
                        nc.scalar.activation(evac_dst(units[i]), evac_src(i), ACT.Copy).then_inc(evac_act, 1)
                    for g in copy_at.get(step, ()):
                        act.wait_ge(pv_done, g + 1)
                        copy_out(lambda dst, src: nc.scalar.activation(dst, src, ACT.Copy), g).then_inc(out_copied, 1)

            @block.vector
            def _(dve):
                for step in range(U + 3):
                    i = step
                    if i < U:
                        u = units[i]
                        dve.wait_ge(scores_ready, i + 1)
                        if masked:
                            if i >= 3:
                                dve.wait_ge(probs_ready, i - 2)
                            nc.vector.tensor_tensor(masked_scores[i % 3][:, 0:u.n], S[i % 3][:, 0:u.n], u.mask,
                                                    ALU.add).then_inc(mask_added, 1)
                            dve.wait_ge(mask_added, i + 1)
                        if i >= 4:
                            dve.wait_ge(probs_ready, i - 3)
                        nc.vector.tensor_reduce(neg_max[:, i % 4:i % 4 + 1], masked_scores[i % 3][:, 0:u.n], AX.X,
                                                ALU.max, negate=True).then_inc(max_ready, 1)
                    i = step - 2
                    if 0 <= i < U and i % 2 == 0:
                        dve.wait_ge(turned, i + 1)
                        wait_slot_free(dve, i)
                        nc.vector.tensor_copy(evac_dst(units[i]), evac_src(i)).then_inc(evac_dve, 1)


def full_group(heads, outputs):
    return Group(heads, outputs, [((0, N), [kt]) for kt in range(NT)])


def band_group(heads, outputs):
    return Group(heads, outputs, [((q * P, (q + 1) * P), list(range(max(q - 1, 0), q + 1))) for q in range(NT)])


def pair_groups(kind):
    return [kind([2 * g, 2 * g + 1], [(g, 64 * j, (64 * (2 * g + j), 64 * (2 * g + j + 1)), 2 * g + j)
                                      for j in range(2)]) for g in range(4)]


def first_tile(group, k):
    return k == 0 or group.parts[k][0] != group.parts[k - 1][0]


def last_tile(group, k):
    return k == len(group.parts) - 1 or group.parts[k][0] != group.parts[k + 1][0]


def scale_heads(nc, names, ident, outT, tiles, row_sum, heads, dv, stride, out, residual):
    tag = names.next("scale")
    with ExitStack() as es:
        T = [es.enter_context(nc.psum_tensor(f"{tag}_T{t}", [P, BANK], F32)) for t in range(NT)]
        inv = es.enter_context(nc.sbuf_tensor(f"{tag}_inv", [P, NT, heads], F32))
        with stage(nc, tag, "turned", "inverted", "scaled") as (block, turned, inverted, scaled):
            @block.tensor
            def _(pe):
                for t in range(NT):
                    for c in range(tiles):
                        ins = nc.tensor.transpose(T[t][:, c * P:(c + 1) * P], outT[:, c, t * P:(t + 1) * P], ident[:])
                    ins.then_inc(turned, 1)

            @block.vector
            def _(dve):
                nc.vector.reciprocal(inv[:], row_sum[:]).then_inc(inverted, 1)
                dve.wait_ge(inverted, 1)
                for t in range(NT):
                    dve.wait_ge(turned, t + 1)
                    nc.vector.tensor_tensor(
                        out[:, t, 0:heads * dv].rearrange("p (h v) -> p h v", h=heads),
                        T[t][:, 0:heads * stride].rearrange("p (h v) -> p h v", h=heads)[:, :, 0:dv],
                        inv[:, t, :].unsqueeze(2).to_broadcast([P, heads, dv]), ALU.mult).then_inc(scaled, 1)
                    if residual is not None:
                        dve.wait_ge(scaled, t + 1)
                        nc.vector.tensor_tensor(residual[:, t, :], residual[:, t, :], out[:, t, 0:D], ALU.add)


def silu_attention(nc, names, qm, kT, V, mask, outT, masking, heads=16, per_group=8, slot=32):
    tag = names.next("silu")
    quads = heads // 4
    units = [(g, kt, j) for g in range(quads) for kt in range(NT) for j in range(4)]
    U = len(units)
    RING, SRING = 12, 5
    with ExitStack() as es:
        S = [es.enter_context(nc.psum_tensor(f"{tag}_S{i}", [P, N], F32)) for i in range(SRING)]
        O = [es.enter_context(nc.psum_tensor(f"{tag}_O{i}", [P, BANK], F32)) for i in range(2)]
        A = es.enter_context(nc.sbuf_tensor(f"{tag}_A", [P, 3, N], F32))
        W = es.enter_context(nc.sbuf_tensor(f"{tag}_W", [P, RING, N], F32))
        with stage(nc, tag, "q_masked", "scores_ready", "silu_done", "masked", "pv_done", "out_copied") as (
                block, q_masked, scores_ready, silu_done, masked, pv_done, out_copied):
            @block.gpsimd
            def _(pool):
                mask_queries(nc, pool, q_masked, *masking)

            @block.tensor
            def _(pe):
                for step in range(U + 7):
                    if step < U:
                        g, kt, j = units[step]
                        h = 4 * g + j
                        if kt == 0:
                            pe.wait_ge(q_masked, h + 1)
                        if step >= SRING:
                            pe.wait_ge(silu_done, step - SRING + 1)
                        nc.tensor.matmul(S[step % SRING][:], kT[:, h // per_group, kt * P:(kt + 1) * P],
                                         qm[:, h, :], start=True, stop=True).then_inc(scores_ready, 1)
                    i = step - 3
                    if 0 <= i < U and i % 4 == 3:
                        g, kt, _ = units[i]
                        pe.wait_ge(masked, i + 1)
                        if kt == 0 and g >= 2:
                            pe.wait_ge(out_copied, g - 1)
                        for j in range(4):
                            h = 4 * g + j
                            ins = nc.tensor.matmul(O[g % 2][j * slot:(j + 1) * slot, :],
                                                   V[:, kt, h * slot:(h + 1) * slot], W[:, (i - 3 + j) % RING, :],
                                                   start=(kt == 0), stop=(kt == NT - 1))
                        ins.then_inc(pv_done, 1)

            @block.scalar
            def _(act):
                for i in range(U + 8):
                    if i < U:
                        act.wait_ge(scores_ready, i + 1)
                        if i >= 3:
                            act.wait_ge(masked, i - 2)
                        nc.scalar.activation(A[:, i % 3, :], S[i % SRING][:], ACT.Silu).then_inc(silu_done, 1)
                    k = i - 7
                    if 0 <= k < U and k % (4 * NT) == 4 * NT - 1:
                        g = k // (4 * NT)
                        act.wait_ge(pv_done, NT * (g + 1))
                        nc.scalar.activation(outT[:, g, :], O[g % 2][:], ACT.Copy).then_inc(out_copied, 1)

            @block.vector
            def _(dve):
                for i, (g, kt, j) in enumerate(units):
                    dve.wait_ge(silu_done, i + 1)
                    if i >= RING:
                        dve.wait_ge(pv_done, (i - RING) // 4 + 1)
                    nc.vector.tensor_tensor(W[:, i % RING, :], A[:, i % 3, :], mask[:, kt, :], ALU.mult)\
                        .then_inc(masked, 1)


def turn_jobs(src, dst, chunks):
    return [Job(dst[:, c, :], turns=tuple(src[:, t, c * P:(c + 1) * P] for t in range(NT))) for c in range(chunks)]


def out_projection_jobs(srcT, chunks, weight, residual, ones_row, bias_row):
    jobs = []
    for t in range(NT):
        terms = [(srcT[:, c, t * P:(t + 1) * P], weight[:, c, :]) for c in range(chunks)]
        if bias_row is not None:
            terms.append((ones_row, bias_row))
        jobs.append(Job(residual[:, t, :], terms=tuple(terms), add=True))
    return jobs


def head_major_jobs(dst, xT, weight, groups, relu=False, scale=1.0, bias=None):
    return [Job(dst[:, g, :], terms=tuple((weight[:, c, g * P:(g + 1) * P], xT[:, c, :]) for c in range(DC)),
                relu=relu, scale=scale, bias=None if bias is None else bias[:, g:g + 1]) for g in range(groups)]


def token_major_jobs(dst_of, xT, weight, lo, hi, relu=False, ones_row=None, bias_row=None):
    jobs = []
    for t in range(NT):
        terms = [(xT[:, c, t * P:(t + 1) * P], weight[:, c, lo:hi]) for c in range(DC)]
        if bias_row is not None:
            terms.append((ones_row, bias_row))
        jobs.append(Job(dst_of(t), terms=tuple(terms), relu=relu))
    return jobs


def tiles_of(dram, row, rows):
    return dram[bass.ds(row, rows), :].rearrange("(t p) d -> p t d", p=P)


def store_stage(nc, names, pairs):
    with stage(nc, names.next("store"), "stored") as (block, stored):
        @block.sync
        def _(sp):
            for dst, src in pairs:
                sp.dma_start(dst, src).then_inc(stored, 16)
            sp.wait_ge(stored, 16 * len(pairs))


def rope(nc, names, QK, table_c, table_s, out):
    tag = names.next("rope")
    H, DH = 8, 64
    R = DH // 2
    with ExitStack() as es:
        def sb(name, shape):
            return es.enter_context(nc.sbuf_tensor(f"{tag}_{name}", shape, F32))

        sq = sb("sq", [P, 2, 1024])
        norm = sb("norm", [P, NT, 2 * H])
        root = sb("root", [P, NT, 2 * H])
        inv = sb("inv", [P, NT, 2 * H])
        rot = sb("rot", [P, 2, 1024])
        with stage(nc, tag, "squared", "summed", "rooted", "clipped", "inverted", "scaled", "turned_part",
                   "straight", "done") as (
                block, squared, summed, rooted, clipped, inverted, scaled, turned_part, straight, done):
            def heads(ap):
                return ap.rearrange("p (z h f) -> p z h f", z=2, h=H)

            @block.scalar
            def _(act):
                for t in range(NT):
                    if t >= 2:
                        act.wait_ge(summed, t - 1)
                    nc.scalar.activation(sq[:, t % 2, :], QK[:, t, :], ACT.Square).then_inc(squared, 1)
                act.wait_ge(summed, NT)
                nc.scalar.activation(root[:], norm[:], ACT.Sqrt).then_inc(rooted, 1)

            @block.vector
            def _(dve):
                for t in range(NT):
                    dve.wait_ge(squared, t + 1)
                    nc.vector.tensor_reduce(norm[:, t, :], sq[:, t % 2, :].rearrange("p (h f) -> p h f", f=DH),
                                            AX.X, ALU.add).then_inc(summed, 1)
                dve.wait_ge(rooted, 1)
                nc.vector.tensor_scalar(root[:], root[:], 1e-12, None, ALU.max).then_inc(clipped, 1)
                dve.wait_ge(clipped, 1)
                nc.vector.reciprocal(inv[:], root[:]).then_inc(inverted, 1)
                dve.wait_ge(inverted, 1)
                for t in range(NT):
                    x = QK[:, t, :].rearrange("p (h f) -> p h f", f=DH)
                    nc.vector.tensor_tensor(x, x, inv[:, t, :].unsqueeze(2).to_broadcast([P, 2 * H, DH]),
                                            ALU.mult).then_inc(scaled, 1)
                    dve.wait_ge(scaled, t + 1)
                    for lo in (0, R):
                        for z in range(2):
                            src = heads(QK[:, t, :])[:, z, :, R - lo:DH - lo]
                            dst = heads(rot[:, t % 2, :])[:, z, :, lo:lo + R]
                            tab = table_s[:, t, z, lo:lo + R].unsqueeze(1).to_broadcast([P, H, R])
                            nc.vector.tensor_tensor(dst, src, tab, ALU.mult).then_inc(turned_part, 1)
                    dve.wait_ge(turned_part, 4 * (t + 1))
                    dve.wait_ge(straight, 2 * (t + 1))
                    nc.vector.tensor_tensor(out[:, t, :], out[:, t, :], rot[:, t % 2, :], ALU.add).then_inc(done, 1)
                    dve.wait_ge(done, t + 1)

            @block.gpsimd
            def _(pool):
                for t in range(NT):
                    pool.wait_ge(scaled, t + 1)
                    for z in range(2):
                        tab = table_c[:, t, z, :].unsqueeze(1).to_broadcast([P, H, DH])
                        nc.gpsimd.tensor_tensor(heads(out[:, t, :])[:, z], heads(QK[:, t, :])[:, z], tab,
                                                ALU.mult).then_inc(straight, 1)


def norm_shifted(nc, names, mean_mat, HT, HN, gain, shift):
    tag = names.next("nsh")
    with ExitStack() as es:
        MU = es.enter_context(nc.psum_tensor(f"{tag}_mu", [P, N], F32))
        VAR = es.enter_context(nc.psum_tensor(f"{tag}_var", [P, N], F32))
        dev = es.enter_context(nc.sbuf_tensor(f"{tag}_dev", [P, DC, N], F32))
        sq = es.enter_context(nc.sbuf_tensor(f"{tag}_sq", [P, DC, N], F32))
        std = es.enter_context(nc.sbuf_tensor(f"{tag}_std", [P, N], F32))
        eps = es.enter_context(nc.sbuf_tensor(f"{tag}_eps", [P, 1], F32))
        with stage(nc, tag, "mean_ready", "dev_ready", "squared", "var_ready", "std_ready", "inverted", "scaled",
                   "eps_set") as (
                block, mean_ready, dev_ready, squared, var_ready, std_ready, inverted, scaled, eps_set):
            @block.tensor
            def _(pe):
                for c in range(DC):
                    ins = nc.tensor.matmul(MU[:], mean_mat[:], HT[:, c, 0:N], start=(c == 0), stop=(c == DC - 1))
                ins.then_inc(mean_ready, 1)
                for c in range(DC):
                    pe.wait_ge(squared, c + 1)
                    ins = nc.tensor.matmul(VAR[:], mean_mat[:], sq[:, c, :], start=(c == 0), stop=(c == DC - 1))
                ins.then_inc(var_ready, 1)

            @block.vector
            def _(dve):
                nc.vector.memset(eps[:], EPS).then_inc(eps_set, 1)
                dve.wait_ge(mean_ready, 1)
                for c in range(DC):
                    nc.vector.tensor_tensor(dev[:, c, :], HT[:, c, 0:N], MU[:], ALU.subtract).then_inc(dev_ready, 1)
                dve.wait_ge(std_ready, 1)
                nc.vector.reciprocal(std[:], std[:]).then_inc(inverted, 1)
                dve.wait_ge(inverted, 1)
                dve.wait_ge(squared, DC)
                for c in range(DC):
                    nc.vector.tensor_tensor(sq[:, c, :], dev[:, c, :], std[:], ALU.mult).then_inc(scaled, 1)

            @block.scalar
            def _(act):
                for c in range(DC):
                    act.wait_ge(dev_ready, c + 1)
                    nc.scalar.activation(sq[:, c, :], dev[:, c, :], ACT.Square).then_inc(squared, 1)
                act.wait_ge(var_ready, 1)
                act.wait_ge(eps_set, 1)
                nc.scalar.activation(std[:], VAR[:], ACT.Sqrt, bias=eps[:, 0:1]).then_inc(std_ready, 1)
                for c in range(DC):
                    act.wait_ge(scaled, c + 1)
                    nc.scalar.activation(HN[:, c, :], sq[:, c, :], ACT.Identity, bias=shift[:, c:c + 1],
                                         scale=gain[:, c:c + 1])


def gated_mlp(nc, names, HN, w1, b1a, b1g, w2, ones_row, b2_row, hidden, Y):
    tag = names.next("mlp")
    with ExitStack() as es:
        G = [es.enter_context(nc.psum_tensor(f"{tag}_G{i}", [P, N], F32)) for i in range(3)]
        A = [es.enter_context(nc.psum_tensor(f"{tag}_A{i}", [P, N], F32)) for i in range(3)]
        O = [es.enter_context(nc.psum_tensor(f"{tag}_O{i}", [P, BANK], F32)) for i in range(2)]
        gate = es.enter_context(nc.sbuf_tensor(f"{tag}_gate", [P, 2, N], F32))
        with stage(nc, tag, "pair_ready", "gate_ready", "hidden_ready", "out_ready", "added") as (
                block, pair_ready, gate_ready, hidden_ready, out_ready, added):
            rows = [min(P, HID - f * P) for f in range(HC)]

            @block.tensor
            def _(pe):
                for f, m in enumerate(rows):
                    if f >= 3:
                        pe.wait_ge(hidden_ready, f - 2)
                    for bank, lo in ((G[f % 3], HID + f * P), (A[f % 3], f * P)):
                        for c in range(DC):
                            ins = nc.tensor.matmul(bank[0:m, :], w1[:, c, lo:lo + m], HN[:, c, :],
                                                   start=(c == 0), stop=(c == DC - 1))
                    ins.then_inc(pair_ready, 1)
                for t in range(NT):
                    if t == 0:
                        pe.wait_ge(hidden_ready, HC)
                    if t >= 2:
                        pe.wait_ge(added, t - 1)
                    o = O[t % 2][:, 0:D]
                    for f, m in enumerate(rows):
                        nc.tensor.matmul(o, hidden[0:m, f, t * P:(t + 1) * P], w2[0:m, f, :],
                                         start=(f == 0), stop=False)
                    nc.tensor.matmul(o, ones_row, b2_row, start=False, stop=True).then_inc(out_ready, 1)

            @block.scalar
            def _(act):
                for f, m in enumerate(rows):
                    act.wait_ge(pair_ready, f + 1)
                    if f >= 2:
                        act.wait_ge(hidden_ready, f - 1)
                    nc.scalar.activation(gate[0:m, f % 2, :], G[f % 3][0:m, :], ACT.Gelu,
                                         bias=b1g[0:m, f:f + 1]).then_inc(gate_ready, 1)

            @block.vector
            def _(dve):
                for f, m in enumerate(rows):
                    dve.wait_ge(gate_ready, f + 1)
                    nc.vector.scalar_tensor_tensor(hidden[0:m, f, :], A[f % 3][0:m, :], b1a[0:m, f:f + 1],
                                                   gate[0:m, f % 2, :], ALU.add, ALU.mult).then_inc(hidden_ready, 1)
                for t in range(NT):
                    dve.wait_ge(out_ready, t + 1)
                    nc.vector.tensor_tensor(Y[:, t, :], Y[:, t, :], O[t % 2][:, 0:D], ALU.add).then_inc(added, 1)


def route(nc, names, C, moe, logits_dram, bias_bc, slot, gate, tile_expert):
    tag = names.next("route")
    TE = TT * E
    with ExitStack() as es:
        def sb(name, shape):
            return es.enter_context(nc.sbuf_tensor(f"{tag}_{name}", shape, F32))

        L = sb("L", [P, TT, E])
        L2 = sb("L2", [P, TT, E])
        prio = sb("prio", [P, TT, E])
        top = sb("top", [P, TT])
        best = sb("best", [P, TT])
        sel = sb("sel", [P, 2, TT, E])
        expo = sb("expo", [P, TT, E])
        work = sb("work", [P, 2, TT, E])
        s = sb("s", [P, 2, TT])
        den = sb("den", [P, TT])
        inv = sb("inv", [P, TT])
        loc = sb("loc", [P, 2, TT])
        keep = sb("keep", [P, 2, TT])
        scan = [sb(f"scan{i}", [P, 3, TT, E]) for i in range(2)]
        tiles = sb("tiles", [P, E])
        tcmp = sb("tcmp", [P, E, E])
        start_t = sb("start_t", [P, E])
        end_t = sb("end_t", [P, E])
        place = sb("place", [P, 2, TT])
        te = sb("te", [P, ROUTED + SHARED])
        tecmp = sb("tecmp", [P, ROUTED, E])
        prefix = es.enter_context(nc.psum_tensor(f"{tag}_prefix", [P, BANK], F32))
        total = es.enter_context(nc.psum_tensor(f"{tag}_total", [P, BANK], F32))
        with stage(nc, tag, "landed", "chain", "shifted", "expo_done", "selected", "counted") as (
                block, landed, chain, shifted, expo_done, selected, counted):
            flat_sel = sel[:].rearrange("p c t e -> p (c t e)")

            @block.sync
            def _(sp):
                sp.dma_start(L[:], logits_dram.rearrange("(t p) e -> p t e", p=P)).then_inc(landed, 16)
                sp.wait_ge(landed, 16)

            @block.scalar
            def _(act):
                act.wait_ge(shifted, 1)
                nc.scalar.activation(expo[:], L2[:], ACT.Exp).then_inc(expo_done, 1)

            @block.tensor
            def _(pe):
                pe.wait_ge(selected, 1)
                nc.tensor.matmul(prefix[:, 0:2 * TE], C["upper"], flat_sel, start=True, stop=True)
                nc.tensor.matmul(total[:, 0:2 * TE], C["ones"], flat_sel, start=True, stop=True).then_inc(counted, 1)

            @block.vector
            def _(dve):
                done = [0]

                def link(ins):
                    done[0] += 1
                    ins.then_inc(chain, 1)
                    dve.wait_ge(chain, done[0])

                def over_e(ap):
                    return ap.unsqueeze(2).to_broadcast([P, TT, E])

                v = nc.vector
                dve.wait_ge(landed, 16)
                if bias_bc is not None:
                    link(v.tensor_tensor(L[:], L[:], bias_bc.unsqueeze(1).to_broadcast([P, TT, E]), ALU.add))
                link(v.tensor_reduce(top[:], L[:], AX.X, ALU.max))
                link(v.tensor_tensor(L2[:], L[:], over_e(top[:]), ALU.subtract))
                link(v.tensor_copy(L[:], L2[:]))
                v.sem_inc(shifted, 1)
                countdown = C["countdown"].unsqueeze(1).to_broadcast([P, TT, E])
                for c in range(2):
                    if c:
                        link(v.tensor_reduce(top[:], L[:], AX.X, ALU.max))
                    else:
                        link(v.memset(top[:], 0.0))
                    link(v.tensor_tensor(prio[:], L[:], over_e(top[:]), ALU.is_equal))
                    link(v.tensor_tensor(prio[:], prio[:], countdown, ALU.mult))
                    link(v.tensor_reduce(best[:], prio[:], AX.X, ALU.max))
                    link(v.tensor_tensor(sel[:, c], prio[:], over_e(best[:]), ALU.is_equal))
                    if c == 0:
                        link(v.scalar_tensor_tensor(L[:], sel[:, 0], NEG, L[:], ALU.mult, ALU.add))
                v.sem_inc(selected, 1)
                dve.wait_ge(expo_done, 1)
                for c in range(2):
                    link(v.tensor_tensor(work[:, c], sel[:, c], expo[:], ALU.mult))
                link(v.tensor_reduce(s[:], work[:], AX.X, ALU.add))
                if moe.gates == "top2":
                    link(v.tensor_tensor(den[:], s[:, 0], s[:, 1], ALU.add))
                else:
                    link(v.tensor_reduce(den[:], expo[:], AX.X, ALU.add))
                link(v.reciprocal(inv[:], den[:]))
                for c in range(2):
                    link(v.tensor_tensor(s[:, c], s[:, c], inv[:], ALU.mult))
                dve.wait_ge(counted, 1)
                for i in range(2):
                    link(v.memset(scan[i][:], 0.0))
                link(v.tensor_copy(scan[0][:, 1:3].rearrange("p c t e -> p (c t e)"), total[:, 0:2 * TE]))
                a, b = scan
                hop = 1
                while hop < 2 * TT:
                    fa, fb = (x[:].rearrange("p c t e -> p (c t e)") for x in (a, b))
                    link(v.tensor_tensor(fb[:, TE:3 * TE], fa[:, TE:3 * TE],
                                         fa[:, TE - hop * E:3 * TE - hop * E], ALU.add))
                    a, b = b, a
                    hop *= 2
                fa, fb = (x[:].rearrange("p c t e -> p (c t e)") for x in (a, b))
                count = fa[:, 3 * TE - E:3 * TE]
                fw = work[:].rearrange("p c t e -> p (c t e)")
                link(v.tensor_tensor(fb[:, TE:3 * TE], fa[:, TE - E:3 * TE - E], prefix[:, 0:2 * TE], ALU.add))
                link(v.tensor_tensor(fw, fb[:, TE:3 * TE], flat_sel, ALU.mult))
                link(v.tensor_reduce(loc[:], work[:], AX.X, ALU.add))
                if moe.gates == "capacity":
                    link(v.tensor_scalar(keep[:], loc[:], float(CAPACITY), None, ALU.is_lt))
                    link(v.tensor_tensor(s[:], s[:], keep[:], ALU.mult))
                    link(v.tensor_tensor(den[:], s[:, 0], s[:, 1], ALU.add))
                    link(v.tensor_scalar(den[:], den[:], 1e-9, None, ALU.max))
                    link(v.reciprocal(inv[:], den[:]))
                    for c in range(2):
                        link(v.tensor_tensor(s[:, c], s[:, c], inv[:], ALU.mult))
                link(v.tensor_scalar(gate, s[:], moe.own_scale, None, ALU.mult))
                link(v.tensor_tensor(tcmp[:], count.unsqueeze(2).to_broadcast([P, E, E]),
                                     C["tile_steps"].unsqueeze(1).to_broadcast([P, E, E]), ALU.is_gt))
                link(v.tensor_reduce(tiles[:], tcmp[:], AX.X, ALU.add))
                link(v.tensor_tensor(tcmp[:], tiles[:].unsqueeze(1).to_broadcast([P, E, E]), C["before"], ALU.mult))
                link(v.tensor_reduce(start_t[:], tcmp[:], AX.X, ALU.add))
                link(v.tensor_tensor(end_t[:], start_t[:], tiles[:], ALU.add))
                link(v.tensor_scalar(start_t[:], start_t[:], float(TS), None, ALU.mult))
                for c in range(2):
                    link(v.tensor_tensor(work[:, c], sel[:, c], start_t[:].unsqueeze(1).to_broadcast([P, TT, E]),
                                         ALU.mult))
                link(v.tensor_reduce(place[:], work[:], AX.X, ALU.add))
                link(v.tensor_tensor(place[:], place[:], loc[:], ALU.add))
                link(v.tensor_copy(slot, place[:]))
                link(v.memset(te[:], float(E)))
                link(v.tensor_tensor(tecmp[:], end_t[:].unsqueeze(1).to_broadcast([P, ROUTED, E]),
                                     C["tile_ids"].unsqueeze(2).to_broadcast([P, ROUTED, E]), ALU.is_le))
                link(v.tensor_reduce(te[:, 0:ROUTED], tecmp[:], AX.X, ALU.add))
                link(v.tensor_scalar(te[:, 0:ROUTED], te[:, 0:ROUTED], float(E - 1), None, ALU.min))
                link(v.tensor_copy(tile_expert, te[:]))


def scatter_rows(nc, names, xs, slot, scattered, before):
    tag = names.next("scat")
    with ExitStack() as es:
        rows = es.enter_context(nc.sbuf_tensor(f"{tag}_rows", [P, TT, D], F32))
        with stage(nc, tag, "landed") as (block, landed):
            @block.sync
            def _(sp):
                sp.dma_start(rows[:], xs[ROUTED * TS:ROUTED * TS + TOK, :].rearrange("(t p) d -> p t d", p=P))\
                    .then_inc(landed, 16)
                sp.wait_ge(landed, 16)

            @block.gpsimd
            def _(pool):
                pool.wait_ge(landed, 16)
                for t in range(TT):
                    for c in range(2):
                        pool.indirect_dma_start(xs, bass.IndirectOffsetOnAxis(ap=slot[:, c, t:t + 1], axis=0),
                                                rows[:, t, :], None).then_inc(scattered, 16)
                pool.wait_ge(scattered, before + 2 * TT * 16)


def expert_tiles(nc, names, ident, moe, xs, os_, tile_expert):
    tag = names.next("exp")
    NF = moe.hidden // P
    TILES = ROUTED + (SHARED if moe.shared else 0)
    PAIRS = TILES // 2
    HALF = TS // P
    RING, ORING = 4, 2
    assert NF % RING == 0
    with ExitStack() as es:
        def sb(name, shape):
            return es.enter_context(nc.sbuf_tensor(f"{tag}_{name}", shape, F32))

        def ps(name):
            return es.enter_context(nc.psum_tensor(f"{tag}_{name}", [P, BANK], F32))

        w13 = [sb(f"w13_{u}", [P, 2, DC, moe.hidden]) for u in range(2)]
        w2 = [sb(f"w2_{u}", [P, NF, D]) for u in range(2)]
        X = [sb(f"X{u}", [P, HALF, D]) for u in range(2)]
        XT = [sb(f"XT{u}", [P, DC, TS]) for u in range(2)]
        hidden = [sb(f"hidden{u}", [P, NF, TS]) for u in range(2)]
        gated = sb("gated", [P, 2, TS])
        Y = [sb(f"Y{u}", [P, HALF, D]) for u in range(2)]
        turned = ps("turned")
        H = [ps(f"H{i}") for i in range(RING)]
        O = [ps(f"O{i}") for i in range(ORING)]
        names_ = ["weights0", "weights1", "rows0", "rows1", "rows_turned", "turned_copied", "pair_ready", "gate_ready",
                  "hidden_ready", "out_ready", "out_copied", "stored0", "stored1"]
        with stage(nc, tag, *names_) as (block, weights0, weights1, rows0, rows1, rows_turned, turned_copied,
                                         pair_ready, gate_ready, hidden_ready, out_ready, out_copied,
                                         stored0, stored1):
            weights, rows, stored = (weights0, weights1), (rows0, rows1), (stored0, stored1)

            @block.sync
            def _(sp):
                def load(i, u):
                    e = sp.value_load(tile_expert[0:1, bass.ds(i, 1)], min_val=0,
                                      max_val=E if moe.shared else E - 1)
                    sp.dma_start(X[u][:], xs[bass.ds(i * TS, TS), :].rearrange("(s p) d -> p s d", p=P))\
                        .then_inc(rows[u], 16)
                    sp.dma_start(w13[u][:].rearrange("p a c f -> p (a c f)"),
                                 moe.w13[bass.ds(e, 1)].rearrange("o p f -> (o p) f")).then_inc(weights[u], 16)
                    sp.dma_start(w2[u][:].rearrange("p k d -> p (k d)"),
                                 moe.w2[bass.ds(e, 1)].rearrange("o p f -> (o p) f")).then_inc(weights[u], 16)

                def store(i, u):
                    sp.wait_ge(out_copied, ORING + HALF * (i + 1))
                    sp.dma_start(os_[bass.ds(i * TS, TS), :].rearrange("(s p) d -> p s d", p=P), Y[u][:])\
                        .then_inc(stored[u], 16)

                for u in range(2):
                    sp.sem_inc(stored[u], 16)
                    load(u, u)
                with sp.Fori(0, PAIRS - 1) as pair:
                    for u in range(2):
                        store(2 * pair + u, u)
                        load(2 * pair + u + 2, u)
                for u in range(2):
                    store(TILES - 2 + u, u)
                for u in range(2):
                    sp.wait_ge(stored[u], 16 * (PAIRS + 1))

            @block.tensor
            def _(pe):
                def turn_rows(i, u, nth):
                    pe.wait_ge(rows[u], 16 * nth)
                    for c in range(DC):
                        for s in range(HALF):
                            ins = nc.tensor.transpose(turned[:, c * TS + s * P:c * TS + (s + 1) * P],
                                                      X[u][:, s, c * P:(c + 1) * P], ident[:])
                    ins.then_inc(rows_turned, 1)

                def tile(pair, u, last):
                    i = 2 * pair + u
                    pe.wait_ge(turned_copied, i + 1)
                    pe.wait_ge(weights[u], 32 * (pair + 1))
                    for f in range(NF):
                        pe.wait_ge(hidden_ready, i * NF + f + 1)
                        for a in range(2):
                            for c in range(DC):
                                ins = nc.tensor.matmul(H[f % RING][:, a * TS:(a + 1) * TS],
                                                       w13[u][:, a, c, f * P:(f + 1) * P], XT[u][:, c, :],
                                                       start=(c == 0), stop=(c == DC - 1))
                        ins.then_inc(pair_ready, 1)
                    if not last:
                        turn_rows(i + 1, 1 - u, pair + 1 + u)
                    for s in range(HALF):
                        if s == 0:
                            pe.wait_ge(hidden_ready, (i + 1) * NF + RING)
                        pe.wait_ge(out_copied, HALF * i + s + 1)
                        for f in range(NF):
                            ins = nc.tensor.matmul(O[s][:, 0:D], hidden[u][:, f, s * P:(s + 1) * P], w2[u][:, f, :],
                                                   start=(f == 0), stop=(f == NF - 1))
                        ins.then_inc(out_ready, 1)

                turn_rows(0, 0, 1)
                with pe.Fori(0, PAIRS - 1) as pair:
                    for u in range(2):
                        tile(pair, u, False)
                tile(PAIRS - 1, 0, False)
                tile(PAIRS - 1, 1, True)

            @block.scalar
            def _(act):
                act.sem_inc(out_copied, ORING)
                with act.Fori(0, PAIRS) as pair:
                    for u in range(2):
                        i = 2 * pair + u
                        for f in range(NF):
                            act.wait_ge(pair_ready, i * NF + f + 1)
                            act.wait_ge(hidden_ready, i * NF + f + RING - 1)
                            nc.scalar.activation(gated[:, f % 2, :], H[f % RING][:, 0:TS], moe.func)\
                                .then_inc(gate_ready, 1)
                        for s in range(HALF):
                            act.wait_ge(out_ready, HALF * i + s + 1)
                            act.wait_ge(stored[u], 16 * (pair + 1))
                            nc.scalar.activation(Y[u][:, s, :], O[s][:, 0:D], ACT.Copy).then_inc(out_copied, 1)

            @block.vector
            def _(dve):
                def copy_turned(i, u):
                    dve.wait_ge(rows_turned, i + 1)
                    nc.vector.tensor_copy(XT[u][:], turned[:].rearrange("p (c n) -> p c n", c=DC))\
                        .then_inc(turned_copied, 1)

                def tile(pair, u, last):
                    i = 2 * pair + u
                    for f in range(NF):
                        dve.wait_ge(gate_ready, i * NF + f + 1)
                        nc.vector.tensor_tensor(hidden[u][:, f, :], gated[:, f % 2, :], H[f % RING][:, TS:2 * TS],
                                                ALU.mult).then_inc(hidden_ready, 1)
                    if not last:
                        copy_turned(i + 1, 1 - u)

                dve.sem_inc(hidden_ready, RING)
                copy_turned(0, 0)
                with dve.Fori(0, PAIRS - 1) as pair:
                    for u in range(2):
                        tile(pair, u, False)
                tile(PAIRS - 1, 0, False)
                tile(PAIRS - 1, 1, True)


def combine(nc, names, moe, xres, os_, slot, gate, dst, gathered, before):
    tag = names.next("comb")
    G = len(gathered)
    with ExitStack() as es:
        X = es.enter_context(nc.sbuf_tensor(f"{tag}_X", [P, TT, D], F32))
        S = es.enter_context(nc.sbuf_tensor(f"{tag}_S", [P, TT, D], F32))
        R = es.enter_context(nc.sbuf_tensor(f"{tag}_R", [P, G, 2, D], F32))
        with stage(nc, tag, "landed", "added", "row_done", "stored") as (block, landed, added, row_done, stored):
            loads = 2 if moe.shared else 1

            @block.sync
            def _(sp):
                sp.dma_start(X[:], xres.rearrange("(t p) d -> p t d", p=P)).then_inc(landed, 16)
                if moe.shared:
                    sp.dma_start(S[:], os_[ROUTED * TS:ROUTED * TS + TOK, :].rearrange("(t p) d -> p t d", p=P))\
                        .then_inc(landed, 16)
                sp.wait_ge(landed, 16 * loads)
                sp.wait_ge(row_done, TT)
                sp.dma_start(dst.rearrange("(t p) d -> p t d", p=P), X[:]).then_inc(stored, 16)
                sp.wait_ge(stored, 16)

            @block.gpsimd
            def _(pool):
                for t in range(TT):
                    if t >= G:
                        pool.wait_ge(row_done, t - G + 1)
                    for c in range(2):
                        pool.indirect_dma_start(R[:, t % G, c, :], None, os_,
                                                bass.IndirectOffsetOnAxis(ap=slot[:, c, t:t + 1], axis=0))\
                            .then_inc(gathered[t % G], 16)

            @block.vector
            def _(dve):
                done = 0
                dve.wait_ge(landed, 16 * loads)
                for t in range(TT):
                    dve.wait_ge(gathered[t % G], before + 32 * (t // G + 1))
                    terms = [(R[:, t % G, c, :], gate[:, c, t:t + 1]) for c in range(2)]
                    if moe.shared:
                        terms.append((S[:, t, :], moe.shared_scale))
                    for k, (row, g) in enumerate(terms):
                        ins = nc.vector.scalar_tensor_tensor(X[:, t, :], row, g, X[:, t, :], ALU.mult, ALU.add)
                        if k < len(terms) - 1:
                            done += 1
                            ins.then_inc(added, 1)
                            dve.wait_ge(added, done)
                    ins.then_inc(row_done, 1)


def program(nc, A, out, stop):
    names = Names()
    xres = nc.dram_tensor("xres", [TOK, D], F32, kind="Internal").ap()
    yres = nc.dram_tensor("yres", [TOK, D], F32, kind="Internal").ap()
    xs = nc.dram_tensor("xs", [(ROUTED + SHARED) * TS, D], F32, kind="Internal").ap()
    os_ = nc.dram_tensor("os", [(ROUTED + SHARED) * TS, D], F32, kind="Internal").ap()
    logits = nc.dram_tensor("logits", [TOK, E], F32, kind="Internal").ap()
    with ExitStack() as outer:
        def sbo(name, shape, dt=F32):
            return outer.enter_context(nc.sbuf_tensor(name, shape, dt))

        const_sb = sbo("const_sb", [P, A["consts"].shape[1]])
        slot = sbo("slot", [P, 2, TT], I32)
        gate = sbo("gate", [P, 2, TT])
        tile_expert = sbo("tile_expert", [P, ROUTED + SHARED], I32)
        C, at = {}, 0
        for name, n in CONSTS:
            C[name] = const_sb[:, at:at + n]
            at += n
        ident = C["ident"]
        C["before"] = C["before"].rearrange("p (a b) -> p a b", a=E)
        ones_row = C["ones"][0:1, :]
        load_stage(nc, names, [(const_sb[:], A["consts"])])

        with ExitStack() as es:
            zeros = es.enter_context(nc.sbuf_tensor("zeros", [P, 8 * D], F32))
            with stage(nc, "zero", "set", "stored") as (block, zeros_set, stored):
                @block.vector
                def _(dve):
                    nc.vector.memset(zeros[:], 0.0).then_inc(zeros_set, 1)

                @block.sync
                def _(sp):
                    sp.wait_ge(zeros_set, 1)
                    for i in range(ROUTED * TS // (8 * P)):
                        sp.dma_start(xs[i * 8 * P:(i + 1) * 8 * P, :].rearrange("(p t) d -> p (t d)", p=P),
                                     zeros[:]).then_inc(stored, 16)
                    sp.wait_ge(stored, 16 * (ROUTED * TS // (8 * P)))

        def finish(src):
            with ExitStack() as es:
                t = es.enter_context(nc.sbuf_tensor(names.next("fin"), [P, TT, D], F32))
                load_stage(nc, names, [(t[:], src.rearrange("(t p) d -> p t d", p=P))])
                store_stage(nc, names, [(out.rearrange("(t p) d -> p t d", p=P), t[:])])

        def batch_phase(weights, work, body):
            with ExitStack() as es:
                W = {n: es.enter_context(nc.sbuf_tensor(names.next("w_" + n), list(A[n].shape), F32)) for n in weights}
                if weights:
                    load_stage(nc, names, [(W[n][:], A[n]) for n in weights])
                T = {n: es.enter_context(nc.sbuf_tensor(names.next("t_" + n), shape, dt))
                     for n, (shape, dt) in work.items()}
                with nc.Fori(0, B) as b:
                    body(b, W, T)

        tok = ([P, NT, D], F32)
        wid = ([P, DC, N], F32)
        quad = ([P, 4, N], F32)

        def l0_cross(b, W, T):
            load_stage(nc, names, [(T["X"][:], tiles_of(A["x"], b * N, N)),
                                   (T["ctxT"][:].rearrange("p c n -> p (c n)"),
                                    A["ctxT"][bass.ds(b, 1)].rearrange("o p f -> (o p) f"))])
            layer_norm(nc, names, ident, T["X"], T["XN"], T["XNT"])
            V = T["V"]
            products(nc, names, ident,
                     head_major_jobs(T["qT"], T["XNT"], W["L0_xattn_Wq"], DC, relu=True, scale=0.25)
                     + head_major_jobs(T["kT"], T["ctxT"], W["L0_xattn_Wk"], DC, relu=True)
                     + token_major_jobs(lambda t: V[:, t, :], T["ctxT"], W["L0_xattn_Wv"], 0, 512, relu=True))
            units = [Unit([(T["qm"][:, h, qt * P:(qt + 1) * P], T["kT"][:, h // 8, :])], N, 0, None, qt, h)
                     for h in range(16) for qt in range(NT)]
            groups = [full_group(list(range(4 * g, 4 * g + 4)),
                                 [(g, 32 * j, (32 * (4 * g + j), 32 * (4 * g + j + 1)), 4 * g + j) for j in range(4)])
                      for g in range(4)]
            softmax_attention(nc, names, ident, units, groups, V, T["ONT"], T["row_sum"],
                              (T["qT"], C["head_mask"], T["qm"], 16, 8))
            scale_heads(nc, names, ident, T["ONT"], 4, T["row_sum"], 16, 16, 32, T["ON"], T["X"])
            layer_norm(nc, names, ident, T["X"], T["XN"], None)
            store_stage(nc, names, [(tiles_of(xres, b * N, N), T["X"][:]), (tiles_of(yres, b * N, N), T["XN"][:])])

        batch_phase(["L0_xattn_Wq", "L0_xattn_Wk", "L0_xattn_Wv"],
                    {"X": tok, "XN": tok, "XNT": wid, "ctxT": wid, "qT": wid, "kT": wid, "V": quad, "ON": quad,
                     "ONT": quad, "qm": ([P, 16, N], F32), "row_sum": ([P, NT, 16], F32)},
                    l0_cross)
        if stop == 0:
            return finish(xres)

        ffn_weights = ["wqkv", "wo", "w1", "b1a", "b1g", "w2", "b2", "ln_g", "ln_b", "qk", "qk_sw"]
        with ExitStack() as es:
            W = {n: es.enter_context(nc.sbuf_tensor("w0_" + n, list(A["f_" + n].shape[1:]), F32)) for n in ffn_weights}
            T = {n: es.enter_context(nc.sbuf_tensor("t0_" + n, shape, F32)) for n, shape in {
                "Y": [P, NT, D], "HT": [P, DC, N + 1], "QK": [P, NT, 1024], "QKR": [P, NT, 1024], "V": [P, NT, 512],
                "qT": [P, 4, N], "kT": [P, 4, N], "ON": [P, NT, 512], "ONT": [P, 4, N], "HN": [P, DC, N],
                "hidden": [P, HC, N], "row_sum": [P, NT, 8], "tab_c": [P, NT, 2, 64], "tab_s": [P, NT, 2, 64]}.items()}
            rope_c = C["rope_c"].rearrange("p (t z f) -> p t z f", t=NT, z=2)
            rope_s = C["rope_s"].rearrange("p (t z f) -> p t z f", t=NT, z=2)
            with nc.Fori(0, 2) as depth:
                pairs = []
                for n in ffn_weights:
                    dst, src = W[n][:], A["f_" + n]
                    if len(dst.shape) == 3:
                        dst = dst.rearrange("p a b -> p (a b)")
                    if len(src.shape) == 4:
                        src = src.rearrange("l p a b -> l p (a b)")
                    pairs.append((dst, src[bass.ds(depth, 1)].rearrange("o p f -> (o p) f")))
                load_stage(nc, names, pairs)
                with stage(nc, names.next("tab"), "tables") as (block, tables):
                    @block.vector
                    def _(dve):
                        nc.vector.memset(T["HT"][:, 1, 0:1], 0.0)
                        for t in range(NT):
                            nc.vector.tensor_tensor(T["tab_c"][:, t], rope_c[:, t],
                                                    W["qk"][:].rearrange("p (z f) -> p z f", z=2), ALU.mult)
                            nc.vector.tensor_tensor(T["tab_s"][:, t], rope_s[:, t],
                                                    W["qk_sw"][:].rearrange("p (z f) -> p z f", z=2), ALU.mult)
                with nc.Fori(0, B) as b:
                    Y, HT, QK, V = T["Y"], T["HT"], T["QK"], T["V"]
                    shifted_jobs = [Job(HT[:, c, c:c + N], turns=tuple(Y[:, t, c * P:(c + 1) * P] for t in range(NT)))
                                    for c in range(DC)]
                    load_stage(nc, names, [(Y[:], tiles_of(yres, b * N, N))])
                    products(nc, names, ident, shifted_jobs)
                    xT = HT[:, :, 0:N]
                    products(nc, names, ident,
                             token_major_jobs(lambda t: QK[:, t, 0:512], xT, W["wqkv"], 0, 512)
                             + token_major_jobs(lambda t: QK[:, t, 512:1024], xT, W["wqkv"], 512, 1024)
                             + token_major_jobs(lambda t: V[:, t, :], xT, W["wqkv"], 1024, 1536))
                    rope(nc, names, QK, T["tab_c"], T["tab_s"], T["QKR"])
                    products(nc, names, ident, turn_jobs(T["QKR"], T["qT"], 4)
                             + turn_jobs(T["QKR"][:, :, 512:1024], T["kT"], 4))
                    units = []
                    for h in range(8):
                        r, g = 64 * (h % 2), h // 2
                        for w in range(NT):
                            lo = max(w - 1, 0)
                            units.append(Unit([(T["qT"][r:r + 64, g, w * P:(w + 1) * P],
                                                T["kT"][r:r + 64, g, lo * P:(w + 1) * P])], (w + 1 - lo) * P, lo,
                                              C["mask"] if w else C["mask"][:, P:2 * P], w, h))
                    softmax_attention(nc, names, ident, units, pair_groups(band_group), V, T["ONT"], T["row_sum"])
                    scale_heads(nc, names, ident, T["ONT"], 4, T["row_sum"], 8, 64, 64, T["ON"], None)
                    products(nc, names, ident, turn_jobs(T["ON"], T["ONT"], 4))
                    products(nc, names, ident, out_projection_jobs(T["ONT"], 4, W["wo"], Y, None, None))
                    products(nc, names, ident, shifted_jobs)
                    norm_shifted(nc, names, C["mean"], HT, T["HN"], W["ln_g"], W["ln_b"])
                    gated_mlp(nc, names, T["HN"], W["w1"], W["b1a"], W["b1g"], W["w2"], ones_row,
                              W["b2"][0:1, :], T["hidden"], Y)
                    store_stage(nc, names, [(tiles_of(yres, b * N, N), Y[:])])

        def add_stage(X, Y):
            with stage(nc, names.next("add"), "unused") as (block, _unused):
                @block.vector
                def _(dve):
                    nc.vector.tensor_tensor(X[:], X[:], Y[:], ALU.add)

        if stop == 1:
            with ExitStack() as es:
                X = es.enter_context(nc.sbuf_tensor("dbgX", [P, TT, D], F32))
                Y = es.enter_context(nc.sbuf_tensor("dbgY", [P, TT, D], F32))
                load_stage(nc, names, [(X[:], xres.rearrange("(t p) d -> p t d", p=P)),
                                       (Y[:], yres.rearrange("(t p) d -> p t d", p=P))])
                add_stage(X, Y)
                store_stage(nc, names, [(out.rearrange("(t p) d -> p t d", p=P), X[:])])
            return

        def router_tail(b, T, router):
            layer_norm(nc, names, ident, T["X"], T["XN"], T["XNT"])
            LG = T["LG"]
            products(nc, names, ident, token_major_jobs(lambda t: LG[:, t, :], T["XNT"], router, 0, E))
            store_stage(nc, names, [(tiles_of(xres, b * N, N), T["X"][:]),
                                    (tiles_of(xs, ROUTED * TS + b * N, N), T["XN"][:]),
                                    (tiles_of(logits, b * N, N), LG[:])])

        scattered = outer.enter_context(nc.semaphore("scattered"))
        gathered = [outer.enter_context(nc.semaphore(f"gathered{i}")) for i in range(4)]
        moes_done = []

        def experts(moe, bias_bc, dst):
            route(nc, names, C, moe, logits, bias_bc, slot[:], gate[:], tile_expert[:])
            scatter_rows(nc, names, xs, slot, scattered, len(moes_done) * 2 * TT * 16)
            expert_tiles(nc, names, ident, moe, xs, os_, tile_expert)
            combine(nc, names, moe, xres, os_, slot, gate, dst, gathered,
                    len(moes_done) * 2 * TT // len(gathered) * 16)
            moes_done.append(moe)

        def load_x_ctx(b, T, more=()):
            load_stage(nc, names, [(T["X"][:], tiles_of(xres, b * N, N)),
                                   (T["ctxT"][:].rearrange("p c n -> p (c n)"),
                                    A["ctxT"][bass.ds(b, 1)].rearrange("o p f -> (o p) f"))] + list(more))

        base = {"X": tok, "XN": tok, "XNT": wid, "ctxT": wid, "LG": ([P, NT, E], F32)}

        def l1_cross(b, W, T):
            load_x_ctx(b, T, [(T["XN"][:], tiles_of(yres, b * N, N)),
                              (T["mask_int"][:].rearrange("p k q -> p (k q)"),
                               A["maskT"][bass.ds(b, 1)].rearrange("o p f -> (o p) f"))])
            with stage(nc, names.next("add"), "unused") as (block, _unused):
                @block.vector
                def _(dve):
                    nc.vector.tensor_tensor(T["X"][:], T["X"][:], T["XN"][:], ALU.add)
                    nc.vector.tensor_scalar(T["mask"][:], T["mask_int"][:], 0.0, None, ALU.not_equal)
            layer_norm(nc, names, ident, T["X"], T["XN"], T["XNT"])
            V = T["V"]
            products(nc, names, ident,
                     head_major_jobs(T["qT"], T["XNT"], W["L1_xattn_Wq"], DC, scale=0.25, bias=W["L1_xattn_bq"])
                     + head_major_jobs(T["kT"], T["ctxT"], W["L1_xattn_Wk"], DC, bias=W["L1_xattn_bk"])
                     + token_major_jobs(lambda t: V[:, t, :], T["ctxT"], W["L1_xattn_Wv"], 0, 512,
                                        ones_row=ones_row, bias_row=W["L1_xattn_bv"][0:1, :]))
            silu_attention(nc, names, T["qm"], T["kT"], V, T["mask"], T["ONT"],
                           (T["qT"], C["head_mask"], T["qm"], 16, 8))
            products(nc, names, ident, out_projection_jobs(T["ONT"], 4, W["L1_xattn_Wo"], T["X"], None, None))
            router_tail(b, T, W["L1_ffn_gate_W"])

        batch_phase(["L1_xattn_Wq", "L1_xattn_bq", "L1_xattn_Wk", "L1_xattn_bk", "L1_xattn_Wv", "L1_xattn_bv",
                     "L1_xattn_Wo", "L1_ffn_gate_W"],
                    dict(base, qT=wid, kT=wid, V=quad, ONT=quad, qm=([P, 16, N], F32), mask_int=([P, NT, N], I32), mask=quad),
                    l1_cross)
        if stop == 2:
            return finish(xres)
        experts(Moe("softmax", 1024, ACT.Silu, True, A["L1_w13"], A["L1_w2"], 0.5, 0.5 / 8), None,
                xres if stop != 3 else out)
        if stop == 3:
            return

        def l2_cross(b, W, T):
            load_x_ctx(b, T)
            layer_norm(nc, names, ident, T["X"], T["XN"], T["XNT"])
            V = T["V"]
            products(nc, names, ident,
                     head_major_jobs(T["qT"], T["XNT"], W["L2_xattn_Wq"], 4, scale=0.125)
                     + head_major_jobs(T["kT"], T["ctxT"], W["L2_xattn_Wk"], 4)
                     + token_major_jobs(lambda t: V[:, t, :], T["ctxT"], W["L2_xattn_Wv"], 0, 512))
            units = []
            for h in range(8):
                r, g = 64 * (h % 2), h // 2
                for qt in range(NT):
                    units.append(Unit([(T["qT"][r:r + 64, g, qt * P:(qt + 1) * P], T["kT"][r:r + 64, g, :])], N, 0,
                                      None, qt, h))
            softmax_attention(nc, names, ident, units, pair_groups(full_group), V, T["ONT"], T["row_sum"])
            scale_heads(nc, names, ident, T["ONT"], 4, T["row_sum"], 8, 64, 64, T["ON"], None)
            products(nc, names, ident, turn_jobs(T["ON"], T["ONT"], 4))
            products(nc, names, ident, out_projection_jobs(T["ONT"], 4, W["L2_xattn_Wo"], T["X"], ones_row,
                                                           W["L2_xattn_bo"][0:1, :]))
            router_tail(b, T, W["L2_ffn_router_w"])

        batch_phase(["L2_xattn_Wq", "L2_xattn_Wk", "L2_xattn_Wv", "L2_xattn_Wo", "L2_xattn_bo", "L2_ffn_router_w"],
                    dict(base, qT=quad, kT=quad, V=quad, ON=quad, ONT=quad, row_sum=([P, NT, 8], F32)), l2_cross)
        if stop == 4:
            return finish(xres)
        with ExitStack() as es:
            ebias = es.enter_context(nc.sbuf_tensor("expert_bias", [P, E], F32))
            load_stage(nc, names, [(ebias[:], A["L2_ffn_experts_bias"].to_broadcast([P, E]))])
            experts(Moe("top2", 512, ACT.Silu, True, A["L2_w13"], A["L2_w2"], 1.0, 1.0), ebias[:],
                    xres if stop != 5 else out)
        if stop == 5:
            return

        def l3_cross(b, W, T):
            load_x_ctx(b, T)
            layer_norm(nc, names, ident, T["X"], T["XN"], T["XNT"])
            V = T["V"]
            products(nc, names, ident,
                     head_major_jobs(T["qT"], T["XNT"], W["L3_xattn_Wq"], DC, scale=0.0625, bias=W["L3_xattn_bq"])
                     + head_major_jobs(T["kT"], T["ctxT"], W["L3_xattn_Wk"], DC, bias=W["L3_xattn_bk"])
                     + token_major_jobs(lambda t: V[:, t, 0:D], T["ctxT"], W["L3_xattn_Wv"], 0, D,
                                        ones_row=ones_row, bias_row=W["L3_xattn_bv"][0:1, :]))
            units = [Unit([(T["qT"][:, c, qt * P:(qt + 1) * P], T["kT"][:, c, :]) for c in range(DC)], N, 0, None,
                          qt, 0) for qt in range(NT)]
            groups = [full_group([0], [(c, 0, (c * P, (c + 1) * P), 0) for c in range(DC)])]
            softmax_attention(nc, names, ident, units, groups, V, T["ONT"], T["row_sum"])
            scale_heads(nc, names, ident, T["ONT"], DC, T["row_sum"], 1, D, D, T["ON"], T["X"])
            router_tail(b, T, W["L3_ffn_Wg"])

        batch_phase(["L3_xattn_Wq", "L3_xattn_bq", "L3_xattn_Wk", "L3_xattn_bk", "L3_xattn_Wv", "L3_xattn_bv",
                     "L3_ffn_Wg"],
                    dict(base, qT=quad, kT=quad, V=quad, ON=quad, ONT=quad, row_sum=([P, NT, 1], F32)), l3_cross)
        if stop == 6:
            return finish(xres)
        experts(Moe("capacity", 512, ACT.Gelu, False, A["L3_w13"], A["L3_w2"], 1.0, 0.0), None, out)


CONSTS = [("ident", P), ("ones", P), ("upper", P), ("mean", P), ("mask", 2 * P), ("rope_c", NT * 2 * 64),
          ("rope_s", NT * 2 * 64), ("countdown", E), ("tile_steps", E), ("before", E * E), ("tile_ids", ROUTED), ("head_mask", 8)]


def constants():
    p = np.arange(P)
    pos = (np.arange(NT)[None, :] * P + p[:, None]).astype(np.float32)
    half = np.arange(0, 64, 2, dtype=np.float32)
    inv_freq = (np.float32(1.0) / np.float32(10000.0) ** (half / np.float32(64))).astype(np.float32)
    freqs = (pos[..., None] * inv_freq).astype(np.float32).astype(np.float64)
    freqs = np.concatenate([freqs, freqs], -1)
    base = (half.astype(np.float64) + 0.4 * 64) / (1.4 * 64)
    scale = base[None, None, :] ** ((pos[..., None].astype(np.float64) - N // 2) / 64.0)
    scale = np.concatenate([scale, scale], -1)
    sign = np.where(np.arange(64) < 32, -1.0, 1.0)
    rope_c = np.stack([np.cos(freqs) * scale * 8.0, np.cos(freqs) / scale], 2)
    rope_s = np.stack([np.sin(freqs) * scale * 8.0 * sign, np.sin(freqs) / scale * sign], 2)
    prev = np.where(p[:, None] > p[None, :], NEG, 0.0)
    own = np.where(p[:, None] < p[None, :], NEG, 0.0)
    one = np.ones((P, 1))
    tabs = {
        "ident": np.eye(P), "ones": np.ones((P, P)), "upper": (p[:, None] < p[None, :]),
        "mean": np.full((P, P), 1.0 / D), "mask": np.concatenate([prev, own], 1),
        "rope_c": rope_c.reshape(P, -1), "rope_s": rope_s.reshape(P, -1),
        "countdown": one * (E - np.arange(E)), "tile_steps": one * (TS * np.arange(E)),
        "before": one * (np.arange(E)[None, :] < np.arange(E)[:, None]).reshape(1, -1),
        "tile_ids": one * np.arange(ROUTED),
        "head_mask": p[:, None] // 16 == np.arange(8)[None, :],
    }
    return np.concatenate([np.asarray(tabs[n], np.float32).reshape(P, k) for n, k in CONSTS], 1)


def rows(w):
    w = np.asarray(w)
    return np.ascontiguousarray(w.reshape(-1, P, w.shape[-1]).transpose(1, 0, 2))


def pad_heads(w):
    w = np.asarray(w).reshape(-1, 16, 16)
    out = np.zeros((w.shape[0], 16, 32), w.dtype)
    out[:, :, :16] = w
    return out.reshape(w.shape[0], 512)


def column(v):
    v = np.asarray(v)
    return np.ascontiguousarray(v.reshape(-1, P).T)


def layout(i):
    i = {k: np.asarray(v) for k, v in i.items()}
    A = {"consts": constants(), "x": i["x"].reshape(TOK, D)}
    A["ctxT"] = np.ascontiguousarray(i["ctx_1024"].reshape(B, N, DC, P).transpose(0, 3, 2, 1)).reshape(B, P, DC * N)
    A["maskT"] = np.ascontiguousarray(i["mask_Bx1xSxS2_ik1"].reshape(B, N, NT, P).transpose(0, 3, 2, 1))\
        .reshape(B, P, NT * N)
    for n in ("Wq", "Wk"):
        A["L0_xattn_" + n] = rows(i["L0_xattn_" + n].T)
        A["L1_xattn_" + n] = rows(i["L1_xattn_" + n].T)
        A["L2_xattn_" + n] = rows(i["L2_xattn_" + n])
        A["L3_xattn_" + n] = rows(i["L3_xattn_" + n])
    for n in ("bq", "bk"):
        A["L1_xattn_" + n] = column(i["L1_xattn_" + n])
        A["L3_xattn_" + n] = column(i["L3_xattn_" + n])
    A["L0_xattn_Wv"] = rows(pad_heads(i["L0_xattn_Wv"].T))
    A["L1_xattn_Wv"] = rows(pad_heads(i["L1_xattn_Wv"].T))
    A["L1_xattn_Wo"] = rows(pad_heads(i["L1_xattn_Wo"]).T)
    A["L2_xattn_Wv"] = rows(i["L2_xattn_Wv"])
    A["L2_xattn_Wo"] = rows(i["L2_xattn_Wo"])
    A["L3_xattn_Wv"] = rows(i["L3_xattn_Wv"])
    A["L1_xattn_bv"] = pad_heads(i["L1_xattn_bv"].reshape(1, D))
    for n in ("L2_xattn_bo", "L3_xattn_bv"):
        A[n] = i[n].reshape(1, D)
    A["L1_ffn_gate_W"] = rows(i["L1_ffn_gate_W"].T)
    A["L2_ffn_router_w"] = rows(i["L2_ffn_router_w"].T)
    A["L3_ffn_Wg"] = rows(i["L3_ffn_Wg"])
    A["L2_ffn_experts_bias"] = i["L2_ffn_experts_bias"].reshape(1, E)

    f = {n: i["L0_ffn_" + n] for n in ("wqkv", "q_scale", "k_scale", "wo", "ln_g", "ln_b", "w1", "b1", "w2", "b2")}

    def padded(v, n):
        out = np.zeros((n,) + v.shape[1:], v.dtype)
        out[:v.shape[0]] = v
        return out

    A["f_wqkv"] = np.stack([rows(w) for w in f["wqkv"]])
    A["f_wo"] = np.stack([rows(w) for w in f["wo"]])
    A["f_w1"] = np.stack([rows(w) for w in f["w1"]])
    A["f_w2"] = np.stack([rows(padded(w, HC * P)) for w in f["w2"]])
    A["f_b1a"] = np.stack([column(padded(v[:HID], HC * P)) for v in f["b1"]])
    A["f_b1g"] = np.stack([column(padded(v[HID:], HC * P)) for v in f["b1"]])
    A["f_b2"] = f["b2"].reshape(2, 1, D)
    A["f_ln_g"] = np.stack([column(v) for v in f["ln_g"]])
    A["f_ln_b"] = np.stack([column(v) for v in f["ln_b"]])
    qk = np.stack([f["q_scale"], f["k_scale"]], 1)
    swapped = np.concatenate([qk[..., 32:], qk[..., :32]], -1)
    A["f_qk"] = np.ascontiguousarray(np.broadcast_to(qk.reshape(2, 1, 128), (2, P, 128)))
    A["f_qk_sw"] = np.ascontiguousarray(np.broadcast_to(swapped.reshape(2, 1, 128), (2, P, 128)))

    def expert_weights(w1, w3, w2):
        w13 = np.stack([w1, w3], 1).reshape(w1.shape[0], 2, DC, P, -1).transpose(0, 3, 1, 2, 4)
        w2 = w2.reshape(w2.shape[0], -1, P, D).transpose(0, 2, 1, 3)
        return (np.ascontiguousarray(w13).reshape(w13.shape[0], P, -1),
                np.ascontiguousarray(w2).reshape(w2.shape[0], P, -1))

    def beside(w):
        return w.transpose(1, 0, 2).reshape(1, D, -1)

    A["L1_w13"], A["L1_w2"] = expert_weights(
        np.concatenate([i["L1_ffn_w1_e"], beside(i["L1_ffn_w1_s"])]),
        np.concatenate([i["L1_ffn_w3_e"], beside(i["L1_ffn_w3_s"])]),
        np.concatenate([i["L1_ffn_w2_e"], i["L1_ffn_w2_s"].reshape(1, -1, D)]))
    A["L2_w13"], A["L2_w2"] = expert_weights(
        np.concatenate([i["L2_ffn_w1"], i["L2_ffn_sw1"]]), np.concatenate([i["L2_ffn_w3"], i["L2_ffn_sw3"]]),
        np.concatenate([i["L2_ffn_w2"], i["L2_ffn_sw2"]]))
    A["L3_w13"], A["L3_w2"] = expert_weights(i["L3_ffn_W_in"][:, :, :512], i["L3_ffn_W_in"][:, :, 512:],
                                             i["L3_ffn_W_out"])
    return A


STOP = None


def kernel(**inputs):
    import concourse.bacc as _bacc
    from concourse.bass_utils import run_bass_kernel_spmd as _run

    nc = _bacc.Bacc("TRN2", target_bir_lowering=False, num_devices=1)
    arrays, aps = {}, {}
    for name, a in layout(inputs).items():
        arrays["in_" + name] = a
        aps[name] = nc.dram_tensor("in_" + name, a.shape, mybir.dt.from_np(a.dtype), kind="ExternalInput").ap()
    out = nc.dram_tensor("out_x", (TOK, D), F32, kind="ExternalOutput").ap()
    program(nc, aps, out, STOP)
    r = _run(nc, [arrays], core_ids=[0])
    return r.results[0]["out_x"].reshape(B, N, D)
```

```python
from collections import namedtuple
from contextlib import ExitStack, contextmanager

import numpy as np

import concourse.bass as bass
from concourse import mybir

F32 = mybir.dt.float32
F32R = mybir.dt.float32r
I32 = mybir.dt.int32
ALU = mybir.AluOpType
ACT = mybir.ActivationFunctionType
AX = mybir.AxisListType

P = 128
B, N, D = 4, 512, 256
TOK = B * N
NT = N // P
TT = TOK // P
DC = D // P
BANK = 512
EPS = 1e-5
HID = 682
HC = -(-HID // P)
E = 8
TS = 256
ROUTED = (2 * TOK + E * (TS - 1)) // TS
SHARED = TOK // TS
CAPACITY = 640
NEG = -1.0e30

Moe = namedtuple("Moe", "gates hidden func shared weights own_scale shared_scale")


@contextmanager
def stage(nc, tag, *names):
    with ExitStack() as es:
        sems = [es.enter_context(nc.semaphore(f"{tag}_{n}")) for n in names]
        with nc.Block() as block:
            yield [block] + sems
        for s in sems:
            nc.sync.sem_clear(s)
        nc.all_engine_barrier()


class Names:

    def __init__(self):
        self.n = 0

    def next(self, what):
        self.n += 1
        return f"{what}{self.n}"


def load_stage(nc, names, pairs, on_gpsimd=None):
    with stage(nc, names.next("load"), "landed") as (block, landed):
        if on_gpsimd is not None:
            @block.gpsimd
            def _(pool):
                on_gpsimd(pool)

        @block.sync
        def _(sp):
            for dst, src in pairs:
                sp.dma_start(dst, src).then_inc(landed, 16)
            sp.wait_ge(landed, 16 * len(pairs))


def copy_stage(nc, names, on_vector, on_scalar=()):
    with stage(nc, names.next("copy"), "unused") as (block, _unused):
        @block.vector
        def _(dve):
            for dst, src in on_vector:
                nc.vector.tensor_copy(dst, src)

        if on_scalar:
            @block.scalar
            def _(act):
                for dst, src in on_scalar:
                    nc.scalar.activation(dst, src, ACT.Copy)


def layer_norm(nc, names, ident, X, XN, XNT):
    tag = names.next("ln")
    with ExitStack() as es:
        stats = es.enter_context(nc.sbuf_tensor(tag + "_stats", [P, NT, 6], F32))
        mv = es.enter_context(nc.sbuf_tensor(tag + "_mv", [P, NT, 2], F32))
        std = es.enter_context(nc.sbuf_tensor(tag + "_std", [P, NT], F32))
        rstd = es.enter_context(nc.sbuf_tensor(tag + "_rstd", [P, NT], F32))
        eps = es.enter_context(nc.sbuf_tensor(tag + "_eps", [P, 1], F32))
        turned = [es.enter_context(nc.psum_tensor(f"{tag}_turned{c}", [P, N], F32)) for c in range(DC)]
        with stage(nc, tag, "eps_set", "stats_done", "moments_done", "std_done", "rstd_done", "normed", "transposed") as (
                block, eps_set, stats_done, moments_done, std_done, rstd_done, normed, transposed):
            @block.vector
            def _(dve):
                nc.vector.memset(eps[:], EPS).then_inc(eps_set, 1)
                for t in range(NT):
                    nc.vector.bn_stats(stats[:, t, :], X[:, t, :]).then_inc(stats_done, 1)
                dve.wait_ge(stats_done, NT)
                for t in range(NT):
                    nc.vector.bn_aggr(mv[:, t, :], stats[:, t, :]).then_inc(moments_done, 1)
                dve.wait_ge(std_done, 1)
                nc.vector.reciprocal(rstd[:], std[:]).then_inc(rstd_done, 1)
                dve.wait_ge(rstd_done, 1)
                dve.wait_ge(moments_done, NT)
                for t in range(NT):
                    nc.vector.tensor_scalar(XN[:, t, :], X[:, t, :], mv[:, t, 0:1], rstd[:, t:t + 1],
                                            ALU.subtract, ALU.mult).then_inc(normed, 1)
                if XNT is not None:
                    dve.wait_ge(transposed, 2)
                    nc.vector.tensor_copy(XNT[:, 1, :], turned[1][:])

            @block.scalar
            def _(act):
                act.wait_ge(eps_set, 1)
                act.wait_ge(moments_done, NT)
                nc.scalar.activation(std[:], mv[:, :, 1], ACT.Sqrt, bias=eps[:, 0:1]).then_inc(std_done, 1)
                if XNT is not None:
                    act.wait_ge(transposed, 1)
                    nc.scalar.activation(XNT[:, 0, :], turned[0][:], ACT.Copy)

            if XNT is not None:
                @block.tensor
                def _(pe):
                    for c in range(DC):
                        for t in range(NT):
                            pe.wait_ge(normed, t + 1)
                            last = nc.tensor.transpose(turned[c][:, t * P:(t + 1) * P],
                                                       XN[:, t, c * P:(c + 1) * P], ident[:])
                        last.then_inc(transposed, 1)


Job = namedtuple("Job", "dst terms turns relu scale bias add", defaults=((), (), False, 1.0, None, False))


def products(nc, names, ident, jobs, on_gpsimd=None):
    tag = names.next("prod")
    on_dve, nth, count = [], [], [0, 0]
    for j, job in enumerate(jobs):
        d = job.bias is not None or job.add or j % 2 == 0
        on_dve.append(d)
        count[d] += 1
        nth.append(count[d])
    with ExitStack() as es:
        banks = [es.enter_context(nc.psum_tensor(f"{tag}_bank{i}", [P, BANK], F32)) for i in range(8)]
        with stage(nc, tag, "filled", "emptied_by_act", "emptied_by_dve") as (
                block, filled, emptied_by_act, emptied_by_dve):
            if on_gpsimd is not None:
                @block.gpsimd
                def _(pool):
                    on_gpsimd(pool)

            def bank(j):
                rows, cols = jobs[j].dst.shape[0], jobs[j].dst.shape[-1]
                return banks[j % 8][0:rows, 0:cols]

            @block.tensor
            def _(pe):
                for j, job in enumerate(jobs):
                    if j >= 8:
                        pe.wait_ge(emptied_by_dve if on_dve[j - 8] else emptied_by_act, nth[j - 8])
                    for i, (lhsT, rhs) in enumerate(job.terms):
                        last = nc.tensor.matmul(bank(j), lhsT, rhs, start=(i == 0), stop=(i == len(job.terms) - 1))
                    for i, src in enumerate(job.turns):
                        last = nc.tensor.transpose(banks[j % 8][:, i * P:(i + 1) * P], src, ident[:])
                    last.then_inc(filled, 1)

            @block.scalar
            def _(act):
                for j, job in enumerate(jobs):
                    if not on_dve[j]:
                        act.wait_ge(filled, j + 1)
                        nc.scalar.activation(job.dst, bank(j), ACT.Relu if job.relu else ACT.Copy,
                                             scale=job.scale).then_inc(emptied_by_act, 1)

            @block.vector
            def _(dve):
                for j, job in enumerate(jobs):
                    if on_dve[j]:
                        dve.wait_ge(filled, j + 1)
                        if job.add:
                            ins = nc.vector.tensor_tensor(job.dst, bank(j), job.dst, ALU.add)
                        elif job.bias is not None:
                            ins = nc.vector.tensor_scalar(job.dst, bank(j), job.bias, job.scale, ALU.add, ALU.mult)
                        elif job.relu:
                            ins = nc.vector.tensor_scalar(job.dst, bank(j), job.scale, 0.0, ALU.mult, ALU.max)
                        elif job.scale != 1.0:
                            ins = nc.vector.tensor_scalar(job.dst, bank(j), job.scale, None, ALU.mult)
                        else:
                            ins = nc.vector.tensor_copy(job.dst, bank(j))
                        ins.then_inc(emptied_by_dve, 1)


Unit = namedtuple("Unit", "terms n lo mask qt head")
Group = namedtuple("Group", "heads outputs parts")


def mask_queries(nc, pool, q_masked, source, head_mask, target, per_group, heads):
    for h in heads:
        nc.gpsimd.tensor_scalar(target[:, h, :], source[:, h // per_group, :],
                                head_mask[:, h % per_group:h % per_group + 1], 1.0,
                                ALU.mult, ALU.mult).then_inc(q_masked, 1)


def softmax_attention(nc, names, ident, units, groups, V, outT, row_sum, masking=None, normalise=False):
    tag = names.next("attn")
    U = len(units)
    masked = units[0].mask is not None
    slots = len(groups[0].heads)
    LAG = 3 if normalise else 2
    RING = LAG + 1
    last_unit, group_of = {}, {}
    for g, group in enumerate(groups):
        for h in group.heads:
            group_of[h] = g
    for i, u in enumerate(units):
        last_unit[group_of[u.head]] = i
    part_at, copy_at, step = {}, {}, 0
    spacing = max(1, U // sum(len(group.parts) for group in groups))
    for g, group in enumerate(groups):
        step = max(step, last_unit[g] + LAG + 2)
        for k in range(len(group.parts)):
            part_at.setdefault(step, []).append((g, k))
            last_part = step
            step += spacing if step < U else 1
        copy_at.setdefault(last_part + 1, []).append(g)
    steps = step + 1
    with ExitStack() as es:
        def sb(name, shape):
            return es.enter_context(nc.sbuf_tensor(f"{tag}_{name}", shape, F32))

        def ps(name):
            return es.enter_context(nc.psum_tensor(f"{tag}_{name}", [P, BANK], F32))

        S = [ps(f"S{i}") for i in range(3)]
        PT = [ps(f"PT{i}") for i in range(3)]
        O = [ps(f"O{i}") for i in range(2)]
        masked_scores = [sb(f"SM{i}", [P, 2 * P]) for i in range(3)] if masked else S
        probs = sb("probs", [P, RING, BANK])
        probsT = sb("probsT", [P, 2 * slots, NT, N])
        neg_max = sb("neg_max", [P, 4])
        inv = sb("inv", [P, 4])
        with stage(nc, tag, "q_masked", "scores_ready", "mask_added", "max_ready", "probs_ready", "inverted", "normalised",
                   "turned", "evac_act", "evac_dve", "pv_done", "out_copied") as (
                block, q_masked, scores_ready, mask_added, max_ready, probs_ready, inverted, normalised, turned,
                evac_act, evac_dve, pv_done, out_copied):
            if masking is not None:
                @block.gpsimd
                def _(pool):
                    mask_queries(nc, pool, q_masked, *masking, heads=range(0, 2 if normalise else slots * len(groups)))
                    for i in range(U if normalise else 0):
                        pool.wait_ge(inverted, i + 1)
                        row = probs[:, i % RING, 0:units[i].n]
                        nc.gpsimd.tensor_scalar(row, row, inv[:, i % 4:i % 4 + 1], 1.0, ALU.mult, ALU.mult)\
                            .then_inc(normalised, 1)
                        ahead = units[i].head + 2
                        if units[i].head != units[i - 1].head and ahead < slots * len(groups):
                            mask_queries(nc, pool, q_masked, *masking, heads=[ahead])

            def evac_dst(u):
                slot = (group_of[u.head] % 2) * slots + groups[group_of[u.head]].heads.index(u.head)
                return probsT[:, slot, u.lo:u.lo + u.n // P, u.qt * P:(u.qt + 1) * P]

            def evac_src(i):
                return PT[i % 3][:, 0:units[i].n].rearrange("p (k q) -> p k q", q=P)

            def wait_evacuated(eng, i):
                eng.wait_ge(evac_act if i % 2 else evac_dve, i // 2 + 1)

            def wait_slot_free(eng, i):
                if group_of[units[i].head] >= 2:
                    eng.wait_ge(pv_done, group_of[units[i].head] - 1)

            @block.tensor
            def _(pe):
                for step in range(steps):
                    i = step
                    if i < U:
                        u = units[i]
                        if masking is not None and (i == 0 or units[i - 1].head != u.head):
                            pe.wait_ge(q_masked, u.head + 1)
                        if i >= 3:
                            pe.wait_ge(probs_ready, i - 2)
                        for k, (lhsT, rhs) in enumerate(u.terms):
                            ins = nc.tensor.matmul(S[i % 3][:, 0:u.n], lhsT, rhs,
                                                   start=(k == 0), stop=(k == len(u.terms) - 1))
                        ins.then_inc(scores_ready, 1)
                    i = step - LAG
                    if 0 <= i < U:
                        pe.wait_ge(normalised if normalise else probs_ready, i + 1)
                        if i >= 3:
                            wait_evacuated(pe, i - 3)
                        for k in range(units[i].n // P):
                            ins = nc.tensor.transpose(PT[i % 3][:, k * P:(k + 1) * P],
                                                      probs[:, i % RING, k * P:(k + 1) * P], ident[:])
                        ins.then_inc(turned, 1)
                    for g, k in part_at.get(step, ()):
                        group = groups[g]
                        if k == 0:
                            for j in (last_unit[g], last_unit[g] - 1):
                                if j >= 0:
                                    wait_evacuated(pe, j)
                            if g >= 2:
                                pe.wait_ge(out_copied, g - 1)
                        (q0, q1), tiles = group.parts[k]
                        for kt in tiles:
                            for o, row, (v0, v1), h in group.outputs:
                                slot = (g % 2) * slots + group.heads.index(h)
                                ins = nc.tensor.matmul(O[o % 2][row:row + v1 - v0, q0:q1], V[:, kt, v0:v1],
                                                       probsT[:, slot, kt, q0:q1],
                                                       start=(first_tile(group, k) and kt == tiles[0]),
                                                       stop=(last_tile(group, k) and kt == tiles[-1]))
                        if k == len(group.parts) - 1:
                            ins.then_inc(pv_done, 1)

            def copy_out(eng_copy, g):
                outs = sorted({o for o, *_ in groups[g].outputs})
                for o in outs:
                    ins = eng_copy(outT[:, o, :], O[o % 2][:])
                return ins

            @block.scalar
            def _(act):
                for step in range(steps):
                    i = step
                    if i < U:
                        u = units[i]
                        act.wait_ge(max_ready, i + 1)
                        if i >= RING:
                            act.wait_ge(turned, i - RING + 1)
                        nc.scalar.activation(probs[:, i % RING, 0:u.n], masked_scores[i % 3][:, 0:u.n], ACT.Exp,
                                             bias=neg_max[:, i % 4:i % 4 + 1],
                                             accum_out=row_sum[:, u.qt, u.head:u.head + 1]).then_inc(probs_ready, 1)
                    i = step - LAG
                    if 0 <= i < U and i % 2:
                        act.wait_ge(turned, i + 1)
                        wait_slot_free(act, i)
                        nc.scalar.activation(evac_dst(units[i]), evac_src(i), ACT.Copy).then_inc(evac_act, 1)
                    for g in copy_at.get(step, ()):
                        act.wait_ge(pv_done, g + 1)
                        copy_out(lambda dst, src: nc.scalar.activation(dst, src, ACT.Copy), g).then_inc(out_copied, 1)

            @block.vector
            def _(dve):
                for step in range(U + LAG + 1):
                    i = step
                    if i < U:
                        u = units[i]
                        dve.wait_ge(scores_ready, i + 1)
                        if masked:
                            if i >= 3:
                                dve.wait_ge(probs_ready, i - 2)
                            nc.vector.tensor_tensor(masked_scores[i % 3][:, 0:u.n], S[i % 3][:, 0:u.n], u.mask,
                                                    ALU.add).then_inc(mask_added, 1)
                            dve.wait_ge(mask_added, i + 1)
                        if i >= 4:
                            dve.wait_ge(probs_ready, i - 3)
                        nc.vector.tensor_reduce(neg_max[:, i % 4:i % 4 + 1], masked_scores[i % 3][:, 0:u.n], AX.X,
                                                ALU.max, negate=True).then_inc(max_ready, 1)
                    i = step - 1
                    if normalise and 0 <= i < U:
                        dve.wait_ge(probs_ready, i + 1)
                        if i >= 4:
                            dve.wait_ge(normalised, i - 3)
                        nc.vector.reciprocal(inv[:, i % 4:i % 4 + 1],
                                             row_sum[:, units[i].qt, units[i].head:units[i].head + 1])\
                            .then_inc(inverted, 1)
                    i = step - LAG
                    if 0 <= i < U and i % 2 == 0:
                        dve.wait_ge(turned, i + 1)
                        wait_slot_free(dve, i)
                        nc.vector.tensor_copy(evac_dst(units[i]), evac_src(i)).then_inc(evac_dve, 1)


def full_group(heads, outputs):
    return Group(heads, outputs, [((0, N), [kt]) for kt in range(NT)])


def band_group(heads, outputs):
    return Group(heads, outputs, [((q * P, (q + 1) * P), list(range(max(q - 1, 0), q + 1))) for q in range(NT)])


def pair_groups(kind):
    return [kind([2 * g, 2 * g + 1], [(g, 64 * j, (64 * (2 * g + j), 64 * (2 * g + j + 1)), 2 * g + j)
                                      for j in range(2)]) for g in range(4)]


def first_tile(group, k):
    return k == 0 or group.parts[k][0] != group.parts[k - 1][0]


def last_tile(group, k):
    return k == len(group.parts) - 1 or group.parts[k][0] != group.parts[k + 1][0]


def scale_heads(nc, names, ident, outT, tiles, row_sum, heads, dv, stride, out, residual):
    tag = names.next("scale")
    with ExitStack() as es:
        T = [es.enter_context(nc.psum_tensor(f"{tag}_T{t}", [P, BANK], F32)) for t in range(NT)]
        inv = es.enter_context(nc.sbuf_tensor(f"{tag}_inv", [P, NT, heads], F32))
        with stage(nc, tag, "turned", "inverted", "scaled") as (block, turned, inverted, scaled):
            @block.tensor
            def _(pe):
                for t in range(NT):
                    for c in range(tiles):
                        ins = nc.tensor.transpose(T[t][:, c * P:(c + 1) * P], outT[:, c, t * P:(t + 1) * P], ident[:])
                    ins.then_inc(turned, 1)

            @block.vector
            def _(dve):
                nc.vector.reciprocal(inv[:], row_sum[:]).then_inc(inverted, 1)
                dve.wait_ge(inverted, 1)
                for t in range(NT):
                    dve.wait_ge(turned, t + 1)
                    nc.vector.tensor_tensor(
                        out[:, t, 0:heads * dv].rearrange("p (h v) -> p h v", h=heads),
                        T[t][:, 0:heads * stride].rearrange("p (h v) -> p h v", h=heads)[:, :, 0:dv],
                        inv[:, t, :].unsqueeze(2).to_broadcast([P, heads, dv]), ALU.mult).then_inc(scaled, 1)
                    if residual is not None:
                        dve.wait_ge(scaled, t + 1)
                        nc.vector.tensor_tensor(residual[:, t, :], residual[:, t, :], out[:, t, 0:D], ALU.add)


def stacked_projections(nc, names, repeats, qT, kT, q_stack, k_stack, scale, V_jobs):
    tag = names.next("stack")
    HALF_PAIRS = 4
    projections = [(x, c) for c in range(DC) for x in range(2)]
    order = [("V", 0), ("V", 1)]
    for c in range(DC):
        order += [("stack", x, c, p) for p in range(HALF_PAIRS) for x in range(2)]
        order += [("V", t) for t in range(2 + c * (NT - 2) // DC, 2 + (c + 1) * (NT - 2) // DC)]
    RING = 4
    with ExitStack() as es:
        banks = [es.enter_context(nc.psum_tensor(f"{tag}_P{i}", [P, BANK], F32)) for i in range(len(projections))]
        ring = [es.enter_context(nc.psum_tensor(f"{tag}_R{i}", [P, BANK], F32)) for i in range(RING)]
        high = es.enter_context(nc.sbuf_tensor(f"{tag}_high", [P, 2, DC, N], F32R))
        low = es.enter_context(nc.sbuf_tensor(f"{tag}_low", [P, 2, DC, N], F32R))
        with stage(nc, tag, "projected", "rounded", "split", "filled", "emptied_by_act", "emptied_by_dve") as (
                block, projected, rounded, split, filled, emptied_by_act, emptied_by_dve):
            sides = (qT, kT)

            def job(j):
                return V_jobs[order[j][1]] if order[j][0] == "V" else None

            @block.tensor
            def _(pe):
                for i, (x, c) in enumerate(projections):
                    terms = sides[x][0][c]
                    for k, (lhsT, rhs) in enumerate(terms):
                        ins = nc.tensor.matmul(banks[i][:], lhsT, rhs, start=(k == 0), stop=(k == len(terms) - 1))
                    ins.then_inc(projected, 1)
                for j, what in enumerate(order):
                    if j >= RING:
                        pe.wait_ge(emptied_by_act if j % 2 else emptied_by_dve, (j - RING) // 2 + 1)
                    if what[0] == "V":
                        terms = job(j).terms
                        for k, (lhsT, rhs) in enumerate(terms):
                            ins = nc.tensor.matmul(ring[j % RING][:], lhsT, rhs,
                                                   start=(k == 0), stop=(k == len(terms) - 1))
                    else:
                        _, x, c, p = what
                        pe.wait_ge(split, projections.index((x, c)) + 1)
                        for k, part in enumerate((high, low)):
                            ins = nc.tensor.matmul(ring[j % RING][:], repeats[:, p, x, k, :], part[:, x, c, :],
                                                   start=(k == 0), stop=(k == 1))
                    ins.then_inc(filled, 1)

            def empty(eng_copy, j):
                if order[j][0] == "V":
                    return eng_copy(job(j).dst, ring[j % RING][:], job(j).relu, 1.0)
                _, x, c, p = order[j]
                return eng_copy((q_stack, k_stack)[x][:, c * HALF_PAIRS + p, :], ring[j % RING][:], False,
                                1.0 if x else scale)

            @block.scalar
            def _(act):
                for i, (x, c) in enumerate(projections):
                    act.wait_ge(projected, i + 1)
                    bias = sides[x][1]
                    if bias is None:
                        ins = nc.scalar.activation(high[:, x, c, :], banks[i][:], ACT.Relu)
                    else:
                        ins = nc.scalar.activation(high[:, x, c, :], banks[i][:], ACT.Identity, bias=bias[c])
                    ins.then_inc(rounded, 1)
                for j in range(1, len(order), 2):
                    act.wait_ge(filled, j + 1)
                    empty(lambda dst, src, relu, by: nc.scalar.activation(dst, src, ACT.Relu if relu else ACT.Copy,
                                                                          scale=by), j).then_inc(emptied_by_act, 1)

            @block.vector
            def _(dve):
                for i, (x, c) in enumerate(projections):
                    dve.wait_ge(rounded, i + 1)
                    bias = sides[x][1]
                    nc.vector.scalar_tensor_tensor(low[:, x, c, :], banks[i][:], 0.0 if bias is None else bias[c],
                                                   high[:, x, c, :], ALU.max if bias is None else ALU.add,
                                                   ALU.subtract).then_inc(split, 1)
                for j in range(0, len(order), 2):
                    dve.wait_ge(filled, j + 1)
                    empty(lambda dst, src, relu, by: nc.vector.tensor_scalar(
                        dst, src, by, 0.0 if relu else None, ALU.mult, ALU.max) if relu
                        else nc.vector.tensor_scalar(dst, src, by, None, ALU.mult), j).then_inc(emptied_by_dve, 1)


def silu_attention(nc, names, q_of, k_of, V, mask, outT, heads=16, slot=32):
    tag = names.next("silu")
    quads = heads // 4
    units = [(g, kt, j) for g in range(quads) for kt in range(NT) for j in range(4)]
    U = len(units)
    RING, SRING = 16, 6
    LAG = 7
    with ExitStack() as es:
        S = [es.enter_context(nc.psum_tensor(f"{tag}_S{i}", [P, N], F32)) for i in range(SRING)]
        O = [es.enter_context(nc.psum_tensor(f"{tag}_O{i}", [P, BANK], F32)) for i in range(2)]
        A = es.enter_context(nc.sbuf_tensor(f"{tag}_A", [P, 3, N], F32))
        W = es.enter_context(nc.sbuf_tensor(f"{tag}_W", [P, RING, N], F32))
        with stage(nc, tag, "scores_ready", "silu_done", "masked", "pv_done", "out_copied") as (
                block, scores_ready, silu_done, masked, pv_done, out_copied):
            @block.tensor
            def _(pe):
                for step in range(U + LAG):
                    if step < U:
                        g, kt, j = units[step]
                        h = 4 * g + j
                        if step >= SRING:
                            pe.wait_ge(silu_done, step - SRING + 1)
                        nc.tensor.matmul(S[step % SRING][:], k_of(h)[:, kt * P:(kt + 1) * P],
                                         q_of(h), start=True, stop=True).then_inc(scores_ready, 1)
                    i = step - LAG
                    if 0 <= i < U and i % 4 == 3:
                        g, kt, _ = units[i]
                        pe.wait_ge(masked, i + 1)
                        if kt == 0 and g >= 2:
                            pe.wait_ge(out_copied, g - 1)
                        for j in range(4):
                            h = 4 * g + j
                            ins = nc.tensor.matmul(O[g % 2][j * slot:(j + 1) * slot, :],
                                                   V[:, kt, h * slot:(h + 1) * slot], W[:, (i - 3 + j) % RING, :],
                                                   start=(kt == 0), stop=(kt == NT - 1))
                        ins.then_inc(pv_done, 1)

            @block.scalar
            def _(act):
                for i in range(U + LAG + 4):
                    if i < U:
                        act.wait_ge(scores_ready, i + 1)
                        if i >= 3:
                            act.wait_ge(masked, i - 2)
                        nc.scalar.activation(A[:, i % 3, :], S[i % SRING][:], ACT.Silu).then_inc(silu_done, 1)
                    k = i - LAG - 3
                    if 0 <= k < U and k % (4 * NT) == 4 * NT - 1:
                        g = k // (4 * NT)
                        act.wait_ge(pv_done, NT * (g + 1))
                        nc.scalar.activation(outT[:, g, :], O[g % 2][:], ACT.Copy).then_inc(out_copied, 1)

            @block.vector
            def _(dve):
                for i, (g, kt, j) in enumerate(units):
                    dve.wait_ge(silu_done, i + 1)
                    if i >= RING:
                        dve.wait_ge(pv_done, (i - RING) // 4 + 1)
                    nc.vector.tensor_tensor(W[:, i % RING, :], A[:, i % 3, :], mask[:, kt, :], ALU.mult)\
                        .then_inc(masked, 1)


def out_projection_jobs(srcT, chunks, weight, residual, ones_row, bias_row):
    jobs = []
    for t in range(NT):
        terms = [(srcT[:, c, t * P:(t + 1) * P], weight[:, c, :]) for c in range(chunks)]
        if bias_row is not None:
            terms.append((ones_row, bias_row))
        jobs.append(Job(residual[:, t, :], terms=tuple(terms), add=True))
    return jobs


def head_major_jobs(dst, xT, weight, groups, relu=False, scale=1.0, bias=None):
    return [Job(dst[:, g, :], terms=tuple((weight[:, c, g * P:(g + 1) * P], xT[:, c, :]) for c in range(DC)),
                relu=relu, scale=scale, bias=None if bias is None else bias[:, g:g + 1]) for g in range(groups)]


def token_major_jobs(dst_of, xT, weight, lo, hi, relu=False, ones_row=None, bias_row=None):
    jobs = []
    for t in range(NT):
        terms = [(xT[:, c, t * P:(t + 1) * P], weight[:, c, lo:hi]) for c in range(DC)]
        if bias_row is not None:
            terms.append((ones_row, bias_row))
        jobs.append(Job(dst_of(t), terms=tuple(terms), relu=relu))
    return jobs


def store_stage(nc, names, pairs):
    with stage(nc, names.next("store"), "stored") as (block, stored):
        @block.sync
        def _(sp):
            for dst, src in pairs:
                sp.dma_start(dst, src).then_inc(stored, 16)
            sp.wait_ge(stored, 16 * len(pairs))


def qkv_rope(nc, names, ident, HT, wqkv, table_c, table_s, qT, kT, V):
    tag = names.next("rope")
    H, DH = 8, 64
    R = DH // 2
    HH = 2 * H
    W = HH * DH
    with ExitStack() as es:
        def sb(name, shape):
            return es.enter_context(nc.sbuf_tensor(f"{tag}_{name}", shape, F32))

        QK = [es.enter_context(nc.psum_tensor(f"{tag}_QK{i}", [P, W], F32)) for i in range(3)]
        VB = es.enter_context(nc.psum_tensor(f"{tag}_VB", [P, BANK], F32))
        TR = es.enter_context(nc.psum_tensor(f"{tag}_TR", [P, BANK], F32))
        sq = sb("sq", [P, 2, W])
        norm = sb("norm", [P, NT, HH])
        root = sb("root", [P, NT, HH])
        clip = sb("clip", [P, NT, HH])
        inv = sb("inv", [P, NT, HH])
        unit = sb("unit", [P, 2, W])
        rot = sb("rot", [P, 2, W])
        out = sb("out", [P, 2, W])
        with stage(nc, tag, "qk_ready", "v_ready", "v_copied", "squared", "summed", "rooted", "clipped", "inverted",
                   "scaled", "rot_done", "straight", "roped", "turned", "turned_copied") as (
                block, qk_ready, v_ready, v_copied, squared, summed, rooted, clipped, inverted,
                scaled, rot_done, straight, roped, turned, turned_copied):
            def heads(ap):
                return ap.rearrange("p (z h f) -> p z h f", z=2, h=H)

            @block.tensor
            def _(pe):
                for step in range(NT + 3):
                    t = step
                    if t < NT:
                        if t >= 3:
                            pe.wait_ge(scaled, t - 2)
                        for n in range(3):
                            bank = VB[:] if n == 2 else QK[t % 3][:, n * BANK:(n + 1) * BANK]
                            if n == 2 and t:
                                pe.wait_ge(v_copied, t)
                            for c in range(DC):
                                ins = nc.tensor.matmul(bank, HT[:, c, t * P:(t + 1) * P],
                                                       wqkv[:, c, n * BANK:(n + 1) * BANK],
                                                       start=(c == 0), stop=(c == DC - 1))
                            if n:
                                ins.then_inc(v_ready if n == 2 else qk_ready, 1)
                    t = step - 3
                    if t >= 0:
                        pe.wait_ge(roped, t + 1)
                        for z in range(2):
                            if 2 * t + z:
                                pe.wait_ge(turned_copied, 2 * t + z)
                            for c in range(4):
                                ins = nc.tensor.transpose(TR[:, c * P:(c + 1) * P],
                                                          out[:, t % 2, (4 * z + c) * P:(4 * z + c + 1) * P], ident[:])
                            ins.then_inc(turned, 1)

            @block.scalar
            def _(act):
                for step in range(NT + 3):
                    t = step
                    if t < NT:
                        act.wait_ge(qk_ready, t + 1)
                        if t >= 2:
                            act.wait_ge(summed, t - 1)
                        nc.scalar.activation(sq[:, t % 2, :], QK[t % 3][:], ACT.Square).then_inc(squared, 1)
                        act.wait_ge(summed, t + 1)
                        nc.scalar.activation(root[:, t, :], norm[:, t, :], ACT.Sqrt).then_inc(rooted, 1)
                        act.wait_ge(v_ready, t + 1)
                        nc.scalar.activation(V[:, t, :], VB[:], ACT.Copy).then_inc(v_copied, 1)
                    t = step - 3
                    if t >= 0:
                        for z, dst in enumerate((qT, kT)):
                            act.wait_ge(turned, 2 * t + z + 1)
                            nc.scalar.activation(dst[:, :, t * P:(t + 1) * P],
                                                 TR[:].rearrange("p (c n) -> p c n", c=4),
                                                 ACT.Copy).then_inc(turned_copied, 1)

            @block.vector
            def _(dve):
                def total(t):
                    dve.wait_ge(squared, t + 1)
                    nc.vector.tensor_reduce(norm[:, t, :], sq[:, t % 2, :].rearrange("p (h f) -> p h f", f=DH),
                                            AX.X, ALU.add).then_inc(summed, 1)

                def add(t):
                    dve.wait_ge(straight, 2 * (t + 1))
                    dve.wait_ge(rot_done, 4 * (t + 1))
                    nc.vector.tensor_tensor(out[:, t % 2, :], out[:, t % 2, :], rot[:, t % 2, :],
                                            ALU.add).then_inc(roped, 1)

                total(0)
                for t in range(NT):
                    if t + 1 < NT:
                        total(t + 1)
                    dve.wait_ge(rooted, t + 1)
                    nc.vector.tensor_scalar(clip[:, t, :], root[:, t, :], 1e-12, None, ALU.max).then_inc(clipped, 1)
                    dve.wait_ge(clipped, t + 1)
                    nc.vector.reciprocal(inv[:, t, :], clip[:, t, :]).then_inc(inverted, 1)
                    dve.wait_ge(inverted, t + 1)
                    if t >= 2:
                        dve.wait_ge(straight, 2 * (t - 1))
                        dve.wait_ge(roped, t - 1)
                    nc.vector.tensor_tensor(unit[:, t % 2, :].rearrange("p (h f) -> p h f", f=DH),
                                            QK[t % 3][:].rearrange("p (h f) -> p h f", f=DH),
                                            inv[:, t, :].unsqueeze(2).to_broadcast([P, HH, DH]),
                                            ALU.mult).then_inc(scaled, 1)
                    dve.wait_ge(scaled, t + 1)
                    for lo in (0, R):
                        for z in range(2):
                            nc.vector.tensor_tensor(heads(rot[:, t % 2, :])[:, z, :, lo:lo + R],
                                                    heads(unit[:, t % 2, :])[:, z, :, R - lo:DH - lo],
                                                    table_s[:, t, z, lo:lo + R].unsqueeze(1).to_broadcast([P, H, R]),
                                                    ALU.mult).then_inc(rot_done, 1)
                    if t >= 1:
                        add(t - 1)
                add(NT - 1)

            @block.gpsimd
            def _(pool):
                for t in range(NT):
                    pool.wait_ge(scaled, t + 1)
                    if t >= 2:
                        pool.wait_ge(turned, 2 * (t - 1))
                    for z in range(2):
                        tab = table_c[:, t, z, :].unsqueeze(1).to_broadcast([P, H, DH])
                        nc.gpsimd.tensor_tensor(heads(out[:, t % 2, :])[:, z], heads(unit[:, t % 2, :])[:, z], tab,
                                                ALU.mult).then_inc(straight, 1)


def norm_shifted(nc, names, mean_mat, HT, HN, gain, shift):
    tag = names.next("nsh")
    with ExitStack() as es:
        MU = es.enter_context(nc.psum_tensor(f"{tag}_mu", [P, N], F32))
        VAR = es.enter_context(nc.psum_tensor(f"{tag}_var", [P, N], F32))
        dev = es.enter_context(nc.sbuf_tensor(f"{tag}_dev", [P, DC, N], F32))
        sq = es.enter_context(nc.sbuf_tensor(f"{tag}_sq", [P, DC, N], F32))
        std = es.enter_context(nc.sbuf_tensor(f"{tag}_std", [P, N], F32))
        eps = es.enter_context(nc.sbuf_tensor(f"{tag}_eps", [P, 1], F32))
        with stage(nc, tag, "mean_ready", "dev_ready", "squared", "var_ready", "std_ready", "inverted", "scaled",
                   "eps_set") as (
                block, mean_ready, dev_ready, squared, var_ready, std_ready, inverted, scaled, eps_set):
            @block.tensor
            def _(pe):
                for c in range(DC):
                    ins = nc.tensor.matmul(MU[:], mean_mat[:], HT[:, c, 0:N], start=(c == 0), stop=(c == DC - 1))
                ins.then_inc(mean_ready, 1)
                for c in range(DC):
                    pe.wait_ge(squared, c + 1)
                    ins = nc.tensor.matmul(VAR[:], mean_mat[:], sq[:, c, :], start=(c == 0), stop=(c == DC - 1))
                ins.then_inc(var_ready, 1)

            @block.vector
            def _(dve):
                nc.vector.memset(eps[:], EPS).then_inc(eps_set, 1)
                dve.wait_ge(mean_ready, 1)
                for c in range(DC):
                    nc.vector.tensor_tensor(dev[:, c, :], HT[:, c, 0:N], MU[:], ALU.subtract).then_inc(dev_ready, 1)
                dve.wait_ge(std_ready, 1)
                nc.vector.reciprocal(std[:], std[:]).then_inc(inverted, 1)
                dve.wait_ge(inverted, 1)
                dve.wait_ge(squared, DC)
                for c in range(DC):
                    nc.vector.tensor_tensor(sq[:, c, :], dev[:, c, :], std[:], ALU.mult).then_inc(scaled, 1)

            @block.scalar
            def _(act):
                for c in range(DC):
                    act.wait_ge(dev_ready, c + 1)
                    nc.scalar.activation(sq[:, c, :], dev[:, c, :], ACT.Square).then_inc(squared, 1)
                act.wait_ge(var_ready, 1)
                act.wait_ge(eps_set, 1)
                nc.scalar.activation(std[:], VAR[:], ACT.Sqrt, bias=eps[:, 0:1]).then_inc(std_ready, 1)
                for c in range(DC):
                    act.wait_ge(scaled, c + 1)
                    nc.scalar.activation(HN[:, c, :], sq[:, c, :], ACT.Identity, bias=shift[:, c:c + 1],
                                         scale=gain[:, c:c + 1])


def gated_mlp(nc, names, HN, w1, b1a, b1g, w2, ones_row, b2_row, hidden, Y):
    tag = names.next("mlp")
    with ExitStack() as es:
        G = [es.enter_context(nc.psum_tensor(f"{tag}_G{i}", [P, N], F32)) for i in range(3)]
        A = [es.enter_context(nc.psum_tensor(f"{tag}_A{i}", [P, N], F32)) for i in range(3)]
        O = [es.enter_context(nc.psum_tensor(f"{tag}_O{i}", [P, BANK], F32)) for i in range(2)]
        gate = es.enter_context(nc.sbuf_tensor(f"{tag}_gate", [P, 2, N], F32))
        with stage(nc, tag, "pair_ready", "gate_ready", "hidden_ready", "out_ready", "added") as (
                block, pair_ready, gate_ready, hidden_ready, out_ready, added):
            rows = [min(P, HID - f * P) for f in range(HC)]

            @block.tensor
            def _(pe):
                for f, m in enumerate(rows):
                    if f >= 3:
                        pe.wait_ge(hidden_ready, f - 2)
                    for bank, lo in ((G[f % 3], HID + f * P), (A[f % 3], f * P)):
                        for c in range(DC):
                            ins = nc.tensor.matmul(bank[0:m, :], w1[:, c, lo:lo + m], HN[:, c, :],
                                                   start=(c == 0), stop=(c == DC - 1))
                    ins.then_inc(pair_ready, 1)
                for t in range(NT):
                    if t == 0:
                        pe.wait_ge(hidden_ready, HC)
                    if t >= 2:
                        pe.wait_ge(added, t - 1)
                    o = O[t % 2][:, 0:D]
                    for f, m in enumerate(rows):
                        nc.tensor.matmul(o, hidden[0:m, f, t * P:(t + 1) * P], w2[0:m, f, :],
                                         start=(f == 0), stop=False)
                    nc.tensor.matmul(o, ones_row, b2_row, start=False, stop=True).then_inc(out_ready, 1)

            @block.scalar
            def _(act):
                for f, m in enumerate(rows):
                    act.wait_ge(pair_ready, f + 1)
                    if f >= 2:
                        act.wait_ge(hidden_ready, f - 1)
                    nc.scalar.activation(gate[0:m, f % 2, :], G[f % 3][0:m, :], ACT.Gelu,
                                         bias=b1g[0:m, f:f + 1]).then_inc(gate_ready, 1)

            @block.vector
            def _(dve):
                for f, m in enumerate(rows):
                    dve.wait_ge(gate_ready, f + 1)
                    nc.vector.scalar_tensor_tensor(hidden[0:m, f, :], A[f % 3][0:m, :], b1a[0:m, f:f + 1],
                                                   gate[0:m, f % 2, :], ALU.add, ALU.mult).then_inc(hidden_ready, 1)
                for t in range(NT):
                    dve.wait_ge(out_ready, t + 1)
                    nc.vector.tensor_tensor(Y[:, t, :], Y[:, t, :], O[t % 2][:, 0:D], ALU.add).then_inc(added, 1)


def route(nc, names, C, moe, logits, bias_bc, slot, gate, tile_expert, XN_all, xs, zeroed, first):
    tag = names.next("route")
    TE = TT * E
    with ExitStack() as es:
        def sb(name, shape):
            return es.enter_context(nc.sbuf_tensor(f"{tag}_{name}", shape, F32))

        L = sb("L", [P, TT, E])
        L2 = sb("L2", [P, TT, E])
        prio = sb("prio", [P, TT, E])
        top = sb("top", [P, TT])
        best = sb("best", [P, TT])
        sel = sb("sel", [P, 2, TT, E])
        expo = sb("expo", [P, TT, E])
        work = sb("work", [P, 2, TT, E])
        s = sb("s", [P, 2, TT])
        den = sb("den", [P, TT])
        inv = sb("inv", [P, TT])
        loc = sb("loc", [P, 2, TT])
        keep = sb("keep", [P, 2, TT])
        scan = [sb(f"scan{i}", [P, 3, TT, E]) for i in range(2)]
        tiles = sb("tiles", [P, E])
        tcmp = sb("tcmp", [P, E, E])
        start_t = sb("start_t", [P, E])
        end_t = sb("end_t", [P, E])
        place = sb("place", [P, 2, TT])
        te = sb("te", [P, SHARED + ROUTED])
        tecmp = sb("tecmp", [P, ROUTED, E])
        prefix = es.enter_context(nc.psum_tensor(f"{tag}_prefix", [P, BANK], F32))
        total = es.enter_context(nc.psum_tensor(f"{tag}_total", [P, BANK], F32))
        with stage(nc, tag, "stored", "chain", "shifted", "expo_done", "selected", "counted") as (
                block, stored, chain, shifted, expo_done, selected, counted):
            flat_sel = sel[:].rearrange("p c t e -> p (c t e)")

            @block.sync
            def _(sp):
                if first:
                    sp.wait_ge(zeroed, 16)
                if moe.shared:
                    sp.dma_start(xs[0:TOK, :].rearrange("(t p) d -> p t d", p=P), XN_all[:]).then_inc(stored, 16)
                    sp.wait_ge(stored, 16)

            @block.scalar
            def _(act):
                act.wait_ge(shifted, 1)
                nc.scalar.activation(expo[:], L2[:], ACT.Exp).then_inc(expo_done, 1)

            @block.tensor
            def _(pe):
                pe.wait_ge(selected, 1)
                nc.tensor.matmul(prefix[:, 0:2 * TE], C["upper"], flat_sel, start=True, stop=True)
                nc.tensor.matmul(total[:, 0:2 * TE], C["ones"], flat_sel, start=True, stop=True).then_inc(counted, 1)

            @block.vector
            def _(dve):
                done = [0]

                def link(ins):
                    done[0] += 1
                    ins.then_inc(chain, 1)
                    dve.wait_ge(chain, done[0])

                def over_e(ap):
                    return ap.unsqueeze(2).to_broadcast([P, TT, E])

                v = nc.vector
                if bias_bc is None:
                    link(v.tensor_copy(L[:], logits[:]))
                else:
                    link(v.tensor_tensor(L[:], logits[:], bias_bc.unsqueeze(1).to_broadcast([P, TT, E]), ALU.add))
                link(v.tensor_reduce(top[:], L[:], AX.X, ALU.max))
                link(v.tensor_tensor(L2[:], L[:], over_e(top[:]), ALU.subtract))
                link(v.tensor_copy(L[:], L2[:]))
                v.sem_inc(shifted, 1)
                countdown = C["countdown"].unsqueeze(1).to_broadcast([P, TT, E])
                for c in range(2):
                    if c:
                        link(v.tensor_reduce(top[:], L[:], AX.X, ALU.max))
                    else:
                        link(v.memset(top[:], 0.0))
                    link(v.tensor_tensor(prio[:], L[:], over_e(top[:]), ALU.is_equal))
                    link(v.tensor_tensor(prio[:], prio[:], countdown, ALU.mult))
                    link(v.tensor_reduce(best[:], prio[:], AX.X, ALU.max))
                    link(v.tensor_tensor(sel[:, c], prio[:], over_e(best[:]), ALU.is_equal))
                    if c == 0:
                        link(v.scalar_tensor_tensor(L[:], sel[:, 0], NEG, L[:], ALU.mult, ALU.add))
                v.sem_inc(selected, 1)
                dve.wait_ge(expo_done, 1)
                for c in range(2):
                    link(v.tensor_tensor(work[:, c], sel[:, c], expo[:], ALU.mult))
                link(v.tensor_reduce(s[:], work[:], AX.X, ALU.add))
                if moe.gates == "top2":
                    link(v.tensor_tensor(den[:], s[:, 0], s[:, 1], ALU.add))
                else:
                    link(v.tensor_reduce(den[:], expo[:], AX.X, ALU.add))
                link(v.reciprocal(inv[:], den[:]))
                for c in range(2):
                    link(v.tensor_tensor(s[:, c], s[:, c], inv[:], ALU.mult))
                dve.wait_ge(counted, 1)
                for i in range(2):
                    link(v.memset(scan[i][:], 0.0))
                link(v.tensor_copy(scan[0][:, 1:3].rearrange("p c t e -> p (c t e)"), total[:, 0:2 * TE]))
                a, b = scan
                hop = 1
                while hop < 2 * TT:
                    fa, fb = (x[:].rearrange("p c t e -> p (c t e)") for x in (a, b))
                    link(v.tensor_tensor(fb[:, TE:3 * TE], fa[:, TE:3 * TE],
                                         fa[:, TE - hop * E:3 * TE - hop * E], ALU.add))
                    a, b = b, a
                    hop *= 2
                fa, fb = (x[:].rearrange("p c t e -> p (c t e)") for x in (a, b))
                count = fa[:, 3 * TE - E:3 * TE]
                fw = work[:].rearrange("p c t e -> p (c t e)")
                link(v.tensor_tensor(fb[:, TE:3 * TE], fa[:, TE - E:3 * TE - E], prefix[:, 0:2 * TE], ALU.add))
                link(v.tensor_tensor(fw, fb[:, TE:3 * TE], flat_sel, ALU.mult))
                link(v.tensor_reduce(loc[:], work[:], AX.X, ALU.add))
                if moe.gates == "capacity":
                    link(v.tensor_scalar(keep[:], loc[:], float(CAPACITY), None, ALU.is_lt))
                    link(v.tensor_tensor(s[:], s[:], keep[:], ALU.mult))
                    link(v.tensor_tensor(den[:], s[:, 0], s[:, 1], ALU.add))
                    link(v.tensor_scalar(den[:], den[:], 1e-9, None, ALU.max))
                    link(v.reciprocal(inv[:], den[:]))
                    for c in range(2):
                        link(v.tensor_tensor(s[:, c], s[:, c], inv[:], ALU.mult))
                link(v.tensor_scalar(gate, s[:], moe.own_scale, None, ALU.mult))
                link(v.tensor_tensor(tcmp[:], count.unsqueeze(2).to_broadcast([P, E, E]),
                                     C["tile_steps"].unsqueeze(1).to_broadcast([P, E, E]), ALU.is_gt))
                link(v.tensor_reduce(tiles[:], tcmp[:], AX.X, ALU.add))
                link(v.tensor_tensor(tcmp[:], tiles[:].unsqueeze(1).to_broadcast([P, E, E]), C["before"], ALU.mult))
                link(v.tensor_reduce(start_t[:], tcmp[:], AX.X, ALU.add))
                link(v.tensor_tensor(end_t[:], start_t[:], tiles[:], ALU.add))
                link(v.tensor_scalar(start_t[:], start_t[:], float(TS), None, ALU.mult))
                for c in range(2):
                    link(v.tensor_tensor(work[:, c], sel[:, c], start_t[:].unsqueeze(1).to_broadcast([P, TT, E]),
                                         ALU.mult))
                link(v.tensor_reduce(place[:], work[:], AX.X, ALU.add))
                link(v.tensor_tensor(place[:], place[:], loc[:], ALU.add))
                link(v.tensor_scalar(slot, place[:], float(SHARED * TS), None, ALU.add))
                link(v.memset(te[:], float(E)))
                link(v.tensor_tensor(tecmp[:], end_t[:].unsqueeze(1).to_broadcast([P, ROUTED, E]),
                                     C["tile_ids"].unsqueeze(2).to_broadcast([P, ROUTED, E]), ALU.is_le))
                link(v.tensor_reduce(te[:, SHARED:], tecmp[:], AX.X, ALU.add))
                link(v.tensor_scalar(te[:, SHARED:], te[:, SHARED:], float(E - 1), None, ALU.min))
                link(v.tensor_copy(tile_expert, te[:]))


def expert_tiles(nc, names, ident, moe, xs, os_, tile_expert, XN_all, slot, scattered, before):
    tag = names.next("exp")
    NF = moe.hidden // P
    W13 = 2 * DC * P
    QUARTERS, PER = 4, NF // 4
    BASE = 0 if moe.shared else SHARED
    TILES = ROUTED + SHARED - BASE
    PAIRS = TILES // 2
    assert TILES == 2 * PAIRS + 1
    HALF = TS // P
    RING, ORING = 4, 2
    assert NF % RING == 0
    with ExitStack() as es:
        def sb(name, shape, dtype=F32):
            return es.enter_context(nc.sbuf_tensor(f"{tag}_{name}", shape, dtype))

        def ps(name):
            return es.enter_context(nc.psum_tensor(f"{tag}_{name}", [P, BANK], F32))

        raw = sb("raw", [P, NF, W13 + D])
        w_high = [sb(f"w_high{u}", [P, NF, W13 + D], F32R) for u in range(2)]
        w_low = [sb(f"w_low{u}", [P, NF, W13 + D], F32R) for u in range(2)]
        X = sb("X", [P, HALF, D])
        x_high = sb("x_high", [P, DC, TS], F32R)
        x_low = sb("x_low", [P, DC, TS], F32R)
        h_high = sb("h_high", [P, NF, TS], F32R)
        h_low = sb("h_low", [P, NF, TS], F32R)
        gated = sb("gated", [P, 2, TS])
        hidden = sb("hidden", [P, 2, TS])
        Y = sb("Y", [P, HALF, D])
        turned = ps("turned")
        H = [ps(f"H{i}") for i in range(RING)]
        O = [ps(f"O{i}") for i in range(ORING)]
        names_ = ["raw0", "raw1", "raw2", "raw3", "rows_landed", "stored",
                  "weights_rounded", "w13_split", "w2_split", "rows_turned", "rows_rounded", "rows_split", "pair_ready", "gate_ready",
                  "hidden_ready", "hidden_split", "out_ready", "out_copied"]
        with stage(nc, tag, *names_) as (block, raw0, raw1, raw2, raw3, rows_landed, stored,
                                         weights_rounded, w13_split, w2_split, rows_turned, rows_rounded, rows_split,
                                         pair_ready, gate_ready, hidden_ready, hidden_split, out_ready, out_copied):
            landed = (raw0, raw1, raw2, raw3)

            @block.sync
            def _(sp):
                def expert(i):
                    return sp.value_load(tile_expert[0:1, bass.ds(BASE + i, 1)], min_val=0,
                                         max_val=E if moe.shared else E - 1)

                def load_rows(i):
                    sp.dma_start(X[:], xs[bass.ds((BASE + i) * TS, TS), :].rearrange("(s p) d -> p s d", p=P))\
                        .then_inc(rows_landed, 16)

                def load_quarter(e, q):
                    n = PER * (W13 + D)
                    sp.dma_start(raw[:, q * PER:(q + 1) * PER, :].rearrange("p f n -> p (f n)"),
                                 moe.weights[bass.ds(e, 1), :, q * n:(q + 1) * n].rearrange("o p f -> (o p) f"))\
                        .then_inc(landed[q], 16)

                def load_weights(i):
                    e = expert(i)
                    for q in range(QUARTERS):
                        sp.wait_ge(w13_split, (i - 1) * NF + (q + 1) * PER)
                        sp.wait_ge(w2_split, (i - 1) * NF + (q + 1) * PER)
                        load_quarter(e, q)

                def store(i):
                    sp.wait_ge(out_copied, ORING + HALF * (i + 1))
                    sp.dma_start(os_[bass.ds((BASE + i) * TS, TS), :].rearrange("(s p) d -> p s d", p=P), Y[:])\
                        .then_inc(stored, 16)

                def turns(lo, hi):
                    with sp.Fori(lo, hi) as pair:
                        for u in range(2):
                            i = 2 * pair + u
                            sp.wait_ge(rows_turned, i + 2)
                            load_rows(i + 2)
                            load_weights(i + 2)
                            store(i)

                sp.sem_inc(stored, 16)
                if not moe.shared:
                    sp.wait_ge(scattered, before + 2 * TT * 16)
                load_rows(0)
                e = expert(0)
                for q in range(QUARTERS):
                    load_quarter(e, q)
                sp.wait_ge(rows_turned, 1)
                load_rows(1)
                load_weights(1)
                if moe.shared:
                    turns(0, SHARED // 2 - 1)
                    sp.wait_ge(scattered, before + 2 * TT * 16)
                    turns(SHARED // 2 - 1, PAIRS - 1)
                else:
                    turns(0, PAIRS - 1)
                sp.wait_ge(rows_turned, TILES - 1)
                load_rows(TILES - 1)
                load_weights(TILES - 1)
                for i in range(TILES - 3, TILES):
                    store(i)
                sp.wait_ge(stored, 16 * (TILES + 1))

            @block.gpsimd
            def _(pool):
                def scatter(t):
                    for c in range(2):
                        pool.indirect_dma_start(xs, bass.IndirectOffsetOnAxis(ap=slot[:, c, t:t + 1], axis=0),
                                                XN_all[:, t, :], None).then_inc(scattered, 16)

                def split_w2(i, u, f):
                    pool.wait_ge(weights_rounded, i * NF + f + 1)
                    nc.gpsimd.tensor_tensor(w_low[u][:, f, W13:], raw[:, f, W13:], w_high[u][:, f, W13:],
                                            ALU.subtract).then_inc(w2_split, 1)

                def tile(i, u, last=False, scattering=()):
                    for f in range(NF):
                        if not last and f % 2 == 1:
                            split_w2(i + 1, 1 - u, f // 2)
                        pool.wait_ge(hidden_ready, RING + i * NF + f + 1)
                        nc.gpsimd.tensor_tensor(h_low[:, f, :], hidden[:, f % 2, :], h_high[:, f, :], ALU.subtract)\
                            .then_inc(hidden_split, 1)
                    if not last:
                        for f in range(NF // 2, NF):
                            split_w2(i + 1, 1 - u, f)
                    for t in scattering:
                        scatter(t)

                if not moe.shared:
                    for t in range(TT):
                        scatter(t)
                for f in range(NF):
                    split_w2(0, 0, f)
                if moe.shared:
                    for i in range(SHARED - 2):
                        tile(i, i % 2, scattering=range(i * TT // (SHARED - 2), (i + 1) * TT // (SHARED - 2)))
                with pool.Fori((SHARED - 2) // 2 if moe.shared else 0, PAIRS) as pair:
                    for u in range(2):
                        tile(2 * pair + u, u)
                tile(2 * PAIRS, 0, True)
                pool.wait_ge(scattered, before + 2 * TT * 16)

            @block.tensor
            def _(pe):
                def turn_rows(i):
                    pe.wait_ge(rows_landed, 16 * (i + 1))
                    for c in range(DC):
                        for s in range(HALF):
                            ins = nc.tensor.transpose(turned[:, c * TS + s * P:c * TS + (s + 1) * P],
                                                      X[:, s, c * P:(c + 1) * P], ident[:])
                    ins.then_inc(rows_turned, 1)

                def tile(pair, u, last):
                    i = 2 * pair + u
                    pe.wait_ge(rows_split, i + 1)
                    for f in range(NF):
                        pe.wait_ge(w13_split, i * NF + f + 1)
                        pe.wait_ge(hidden_ready, i * NF + f + 1)
                        for a in range(2):
                            for c in range(DC):
                                cols = slice((a * DC + c) * P, (a * DC + c + 1) * P)
                                for k, (w, x) in enumerate(((w_high, x_high), (w_high, x_low), (w_low, x_high))):
                                    ins = nc.tensor.matmul(H[f % RING][:, a * TS:(a + 1) * TS], w[u][:, f, cols],
                                                           x[:, c, :], start=(c == 0 and k == 0),
                                                           stop=(c == DC - 1 and k == 2))
                        ins.then_inc(pair_ready, 1)
                    if not last:
                        turn_rows(i + 1)
                    for s in range(HALF):
                        pe.wait_ge(out_copied, HALF * i + s + 1)
                        for f in range(NF):
                            if s == 0:
                                pe.wait_ge(w2_split, i * NF + f + 1)
                                pe.wait_ge(hidden_split, 2 + i * NF + f + 1)
                            for k, (h, w) in enumerate(((h_high, w_high), (h_high, w_low), (h_low, w_high))):
                                ins = nc.tensor.matmul(O[s][:, 0:D], h[:, f, s * P:(s + 1) * P], w[u][:, f, W13:],
                                                       start=(f == 0 and k == 0), stop=(f == NF - 1 and k == 2))
                        ins.then_inc(out_ready, 1)

                turn_rows(0)
                with pe.Fori(0, PAIRS) as pair:
                    for u in range(2):
                        tile(pair, u, False)
                tile(PAIRS, 0, True)

            @block.scalar
            def _(act):
                def round_weights(u, f, nth):
                    if f % PER == 0:
                        act.wait_ge(landed[f // PER], 16 * nth)
                    nc.scalar.activation(w_high[u][:, f, :], raw[:, f, :], ACT.Copy).then_inc(weights_rounded, 1)

                def tile(pair, u, last=False):
                    i = 2 * pair + u
                    for f in range(NF):
                        act.wait_ge(pair_ready, i * NF + f + 1)
                        act.wait_ge(hidden_ready, i * NF + f + RING - 1)
                        nc.scalar.activation(gated[:, f % 2, :], H[f % RING][:, 0:TS], moe.func)\
                            .then_inc(gate_ready, 1)
                        if not last:
                            round_weights(1 - u, f, i + 2)
                    for s in range(HALF):
                        act.wait_ge(out_ready, HALF * i + s + 1)
                        act.wait_ge(stored, 16 * (i + 1))
                        nc.scalar.activation(Y[:, s, :], O[s][:, 0:D], ACT.Copy).then_inc(out_copied, 1)

                act.sem_inc(out_copied, ORING)
                for f in range(NF):
                    round_weights(0, f, 1)
                with act.Fori(0, PAIRS) as pair:
                    for u in range(2):
                        tile(pair, u)
                tile(PAIRS, 0, True)

            @block.vector
            def _(dve):
                def split_rows(i):
                    dve.wait_ge(rows_turned, i + 1)
                    both = turned[:].rearrange("p (c n) -> p c n", c=DC)
                    nc.vector.tensor_copy(x_high[:], both).then_inc(rows_rounded, 1)
                    dve.wait_ge(rows_rounded, i + 1)
                    nc.vector.tensor_tensor(x_low[:], both, x_high[:], ALU.subtract).then_inc(rows_split, 1)

                def split_w13(i, u, f):
                    dve.wait_ge(weights_rounded, i * NF + f + 1)
                    nc.vector.tensor_tensor(w_low[u][:, f, 0:W13], raw[:, f, 0:W13], w_high[u][:, f, 0:W13],
                                            ALU.subtract).then_inc(w13_split, 1)

                def tile(pair, u, last):
                    i = 2 * pair + u
                    for f in range(NF):
                        dve.wait_ge(gate_ready, i * NF + f + 1)
                        dve.wait_ge(hidden_split, i * NF + f + 1)
                        for dst in (h_high[:, f, :], hidden[:, f % 2, :]):
                            ins = nc.vector.tensor_tensor(dst, gated[:, f % 2, :], H[f % RING][:, TS:2 * TS],
                                                          ALU.mult)
                        ins.then_inc(hidden_ready, 1)
                        if not last and f < 3 * NF // 4:
                            split_w13(i + 1, 1 - u, f)
                    if not last:
                        split_rows(i + 1)
                        for f in range(3 * NF // 4, NF):
                            split_w13(i + 1, 1 - u, f)

                dve.sem_inc(hidden_ready, RING)
                dve.sem_inc(hidden_split, 2)
                split_rows(0)
                for f in range(NF):
                    split_w13(0, 0, f)
                with dve.Fori(0, PAIRS) as pair:
                    for u in range(2):
                        tile(pair, u, False)
                tile(PAIRS, 0, True)


def combine(nc, names, moe, X_all, os_, slot, gate, dst, gathered, before):
    tag = names.next("comb")
    G = len(gathered)
    with ExitStack() as es:
        S = es.enter_context(nc.sbuf_tensor(f"{tag}_S", [P, TT, D], F32))
        R = es.enter_context(nc.sbuf_tensor(f"{tag}_R", [P, G, 2, D], F32))
        with stage(nc, tag, "landed", "added", "row_done", "stored") as (block, landed, added, row_done, stored):
            @block.sync
            def _(sp):
                if moe.shared:
                    sp.dma_start(S[:], os_[0:TOK, :].rearrange("(t p) d -> p t d", p=P)).then_inc(landed, 16)
                if dst is not None:
                    for k in range(NT):
                        sp.wait_ge(row_done, NT * (k + 1))
                        sp.dma_start(dst[k * N:(k + 1) * N, :].rearrange("(t p) d -> p t d", p=P),
                                     X_all[:, NT * k:NT * (k + 1), :]).then_inc(stored, 16)
                    sp.wait_ge(stored, 16 * NT)

            @block.gpsimd
            def _(pool):
                for t in range(TT):
                    if t >= G:
                        pool.wait_ge(row_done, t - G + 1)
                    for c in range(2):
                        pool.indirect_dma_start(R[:, t % G, c, :], None, os_,
                                                bass.IndirectOffsetOnAxis(ap=slot[:, c, t:t + 1], axis=0))\
                            .then_inc(gathered[t % G], 16)

            @block.vector
            def _(dve):
                done = 0
                if moe.shared:
                    dve.wait_ge(landed, 16)
                for t in range(TT):
                    dve.wait_ge(gathered[t % G], before + 32 * (t // G + 1))
                    terms = [(R[:, t % G, c, :], gate[:, c, t:t + 1]) for c in range(2)]
                    if moe.shared:
                        terms.append((S[:, t, :], moe.shared_scale))
                    for k, (row, g) in enumerate(terms):
                        ins = nc.vector.scalar_tensor_tensor(X_all[:, t, :], row, g, X_all[:, t, :],
                                                             ALU.mult, ALU.add)
                        if k < len(terms) - 1:
                            done += 1
                            ins.then_inc(added, 1)
                            dve.wait_ge(added, done)
                    ins.then_inc(row_done, 1)


def issue_gathers(pool, R, os_, slots, rows_gathered):
    for t in range(NT):
        for c in range(2):
            pool.indirect_dma_start(R[:, t, c, :], None, os_,
                                    bass.IndirectOffsetOnAxis(ap=slots[:, c, t:t + 1], axis=0))\
                .then_inc(rows_gathered, 16)


def fetch_combined(nc, names, moe, b, T, X_all, ctx_all, os_, slot, gate, rows_gathered, shared_landed, before):
    with stage(nc, names.next("combfetch"), "copied", "added") as (block, copied, added):
        @block.sync
        def _(sp):
            sp.dma_start(T["S"][:], os_[bass.ds(b * N, N), :].rearrange("(t p) d -> p t d", p=P))\
                .then_inc(shared_landed, 16)

        @block.scalar
        def _(act):
            nc.scalar.activation(T["ctxT"][:].rearrange("p c n -> p (c n)"),
                                 ctx_all[:, bass.ds(b, 1), :].rearrange("p o f -> p (o f)"), ACT.Copy)

        @block.vector
        def _(dve):
            nc.vector.tensor_copy(T["slots"][:], slot[:, :, bass.ds((b + 1) * NT, NT)])
            nc.vector.tensor_copy(T["gates"][:], gate[:, :, bass.ds(b * NT, NT)]).then_inc(copied, 1)
            dve.wait_ge(copied, 1)
            dve.wait_ge(rows_gathered, before[0] + 2 * NT * 16 * (b + 1))
            dve.wait_ge(shared_landed, before[1] + 16 * (b + 1))
            for k in range(3):
                for t in range(NT):
                    row, g = ((T["R"][:, t, k, :], T["gates"][:, k, t:t + 1]) if k < 2
                              else (T["S"][:, t, :], moe.shared_scale))
                    if k:
                        dve.wait_ge(added, NT * (k - 1) + t + 1)
                    earlier = T["X"] if k else X_all[:, bass.ds(b * NT, NT), :]
                    nc.vector.scalar_tensor_tensor(T["X"][:, t, :], row, g, earlier[:, t, :], ALU.mult, ALU.add)\
                        .then_inc(added, 1)


def program(nc, A, out, stop):
    names = Names()
    xs = nc.dram_tensor("xs", [(ROUTED + SHARED) * TS, D], F32, kind="Internal").ap()
    os_ = nc.dram_tensor("os", [(ROUTED + SHARED) * TS, D], F32, kind="Internal").ap()
    with ExitStack() as outer:
        def sbo(name, shape, dt=F32):
            return outer.enter_context(nc.sbuf_tensor(name, shape, dt))

        const_sb = sbo("const_sb", [P, A["consts"].shape[1]])
        slot = sbo("slot", [P, 2, TT + NT], I32)
        gate = sbo("gate", [P, 2, TT])
        tile_expert = sbo("tile_expert", [P, SHARED + ROUTED], I32)
        X_all = sbo("X_all", [P, TT, D])
        Y_all = sbo("Y_all", [P, TT, D])
        ctx_all = sbo("ctx_all", [P, B, DC * N])
        logits = sbo("logits", [P, TT, E])
        zeros = sbo("zeros", [P, D])
        zeroed = outer.enter_context(nc.semaphore("zeroed"))
        mask_landed = outer.enter_context(nc.semaphore("mask_landed"))
        C, at = {}, 0
        for name, n in CONSTS:
            C[name] = const_sb[:, at:at + n]
            at += n
        ident = C["ident"]
        C["before"] = C["before"].rearrange("p (a b) -> p a b", a=E)
        ones_row = C["ones"][0:1, :]
        load_stage(nc, names, [(const_sb[:], A["consts"]), (X_all[:], A["x"].rearrange("(t p) d -> p t d", p=P)),
                               (ctx_all[:], A["ctxT"].rearrange("b p f -> p b f"))])

        with stage(nc, "zero", "set") as (block, zeros_set):
            @block.vector
            def _(dve):
                nc.vector.memset(zeros[:], 0.0).then_inc(zeros_set, 1)

            @block.sync
            def _(sp):
                sp.wait_ge(zeros_set, 1)
                each = ROUTED * TS // P
                sp.dma_start(xs[TOK:, :].rearrange("(p t) d -> p t d", p=P),
                             zeros[:].unsqueeze(1).to_broadcast([P, each, D])).then_inc(zeroed, 16)

        with stage(nc, "behind", "unused") as (block, _unused):
            @block.vector
            def _(dve):
                nc.vector.memset(slot[:, :, TT:], 0)

        def finish():
            store_stage(nc, names, [(out.rearrange("(t p) d -> p t d", p=P), X_all[:])])

        def element(whole, b):
            return whole[:, bass.ds(b * NT, NT), :]

        def fetch(b, T):
            copy_stage(nc, names, [(T["X"][:], element(X_all, b))],
                       [(T["ctxT"][:].rearrange("p c n -> p (c n)"), ctx_all[:, bass.ds(b, 1), :]
                         .rearrange("p o f -> p (o f)"))])

        def stacked(stack, h):
            return stack[64 * (h % 2):64 * (h % 2 + 1), h // 2, :]

        def width_terms(xT, weight):
            return [[(weight[:, c, g * P:(g + 1) * P], xT[:, c, :]) for c in range(DC)] for g in range(DC)]

        def chunks_of(column):
            return [column[:, c:c + 1] for c in range(DC)]

        def batch_phase(weights, work, body, stacking=False, on_gpsimd=None):
            with ExitStack() as es:
                if stacking:
                    repeats = es.enter_context(nc.sbuf_tensor(names.next("w_repeats"), [P, 4, 2, 2, P], F32R))
                    with nc.sbuf_tensor(names.next("w_repeats_f32"), [P, 4 * 2 * 2 * P], F32) as loaded:
                        load_stage(nc, names, [(loaded[:], A["repeats"])])
                        copy_stage(nc, names, [(repeats[:].rearrange("p a b c n -> p (a b c n)"), loaded[:])])
                W = {n: es.enter_context(nc.sbuf_tensor(names.next("w_" + n), list(A[n].shape), F32)) for n in weights}
                if weights:
                    load_stage(nc, names, [(W[n][:], A[n]) for n in weights], on_gpsimd)
                if stacking:
                    W["repeats"] = repeats
                T = {n: es.enter_context(nc.sbuf_tensor(names.next("t_" + n), shape, dt))
                     for n, (shape, dt) in work.items()}
                with nc.Fori(0, B) as b:
                    body(b, W, T)

        tok = ([P, NT, D], F32)
        wid = ([P, DC, N], F32)
        quad = ([P, 4, N], F32)

        def l0_cross(b, W, T):
            fetch(b, T)
            layer_norm(nc, names, ident, T["X"], T["XN"], T["XNT"])
            V = T["V"]
            stacked_projections(nc, names, W["repeats"],
                                (width_terms(T["XNT"], W["L0_xattn_Wq"]), None),
                                (width_terms(T["ctxT"], W["L0_xattn_Wk"]), None),
                                T["q_stack"], T["k_stack"], 0.25,
                                token_major_jobs(lambda t: V[:, t, :], T["ctxT"], W["L0_xattn_Wv"], 0, 512,
                                                 relu=True))
            units = [Unit([(stacked(T["q_stack"], h)[:, qt * P:(qt + 1) * P], stacked(T["k_stack"], h))], N, 0, None,
                          qt, h)
                     for h in range(16) for qt in range(NT)]
            groups = [full_group(list(range(4 * g, 4 * g + 4)),
                                 [(g, 32 * j, (32 * (4 * g + j), 32 * (4 * g + j + 1)), 4 * g + j) for j in range(4)])
                      for g in range(4)]
            softmax_attention(nc, names, ident, units, groups, V, T["ONT"], T["row_sum"])
            scale_heads(nc, names, ident, T["ONT"], 4, T["row_sum"], 16, 16, 32, T["XN"], T["X"])
            layer_norm(nc, names, ident, T["X"], T["XN"], None)
            copy_stage(nc, names, [(element(X_all, b), T["X"][:])], [(element(Y_all, b), T["XN"][:])])

        batch_phase(["L0_xattn_Wq", "L0_xattn_Wk", "L0_xattn_Wv"],
                    {"X": tok, "XN": tok, "XNT": wid, "ctxT": wid, "V": quad, "ONT": quad,
                     "q_stack": ([P, 8, N], F32R), "k_stack": ([P, 8, N], F32R), "row_sum": ([P, NT, 16], F32)},
                    l0_cross, stacking=True)
        if stop == 0:
            return finish()

        ffn_weights = ["wqkv", "wo", "w1", "b1a", "b1g", "w2", "b2", "ln_g", "ln_b", "qk", "qk_sw"]
        with ExitStack() as es:
            W = {n: es.enter_context(nc.sbuf_tensor("w0_" + n, list(A["f_" + n].shape[1:]), F32)) for n in ffn_weights}
            T = {n: es.enter_context(nc.sbuf_tensor("t0_" + n, shape, F32)) for n, shape in {
                "Y": [P, NT, D], "HT": [P, DC, N + 1], "V": [P, NT, 512],
                "qT": [P, 4, N], "kT": [P, 4, N], "ONT": [P, 4, N], "HN": [P, DC, N],
                "row_sum": [P, NT, 8], "qm": [P, 8, N], "tab_c": [P, NT, 2, 64], "tab_s": [P, NT, 2, 64]}.items()}
            rope_c = C["rope_c"].rearrange("p (t z f) -> p t z f", t=NT, z=2)
            rope_s = C["rope_s"].rearrange("p (t z f) -> p t z f", t=NT, z=2)
            with nc.Fori(0, 2) as depth:
                pairs = []
                for n in ffn_weights:
                    dst, src = W[n][:], A["f_" + n]
                    if len(dst.shape) == 3:
                        dst = dst.rearrange("p a b -> p (a b)")
                    if len(src.shape) == 4:
                        src = src.rearrange("l p a b -> l p (a b)")
                    pairs.append((dst, src[bass.ds(depth, 1)].rearrange("o p f -> (o p) f")))
                load_stage(nc, names, pairs)
                with stage(nc, names.next("tab"), "tables") as (block, tables):
                    @block.vector
                    def _(dve):
                        nc.vector.memset(T["HT"][:, 1, 0:1], 0.0)
                        for t in range(NT):
                            nc.vector.tensor_tensor(T["tab_c"][:, t], rope_c[:, t],
                                                    W["qk"][:].rearrange("p (z f) -> p z f", z=2), ALU.mult)
                            nc.vector.tensor_tensor(T["tab_s"][:, t], rope_s[:, t],
                                                    W["qk_sw"][:].rearrange("p (z f) -> p z f", z=2), ALU.mult)
                with nc.Fori(0, B) as b:
                    Y, HT, V = T["Y"], T["HT"], T["V"]
                    shifted_jobs = [Job(HT[:, c, c:c + N], turns=tuple(Y[:, t, c * P:(c + 1) * P] for t in range(NT)))
                                    for c in range(DC)]
                    copy_stage(nc, names, [(Y[:], element(Y_all, b))])
                    products(nc, names, ident, shifted_jobs)
                    qkv_rope(nc, names, ident, HT, W["wqkv"], T["tab_c"], T["tab_s"], T["qT"], T["kT"], V)
                    units = []
                    for h in range(8):
                        for w in range(NT):
                            lo = max(w - 1, 0)
                            units.append(Unit([(T["qm"][:, h, w * P:(w + 1) * P],
                                                T["kT"][:, h // 2, lo * P:(w + 1) * P])], (w + 1 - lo) * P, lo,
                                              C["mask"] if w else C["mask"][:, P:2 * P], w, h))
                    softmax_attention(nc, names, ident, units, pair_groups(band_group), V, T["ONT"], T["row_sum"],
                                      (T["qT"], C["pair_mask"], T["qm"], 2), normalise=True)
                    products(nc, names, ident, out_projection_jobs(T["ONT"], 4, W["wo"], Y, None, None))
                    products(nc, names, ident, shifted_jobs)
                    norm_shifted(nc, names, C["mean"], HT, T["HN"], W["ln_g"], W["ln_b"])
                    gated_mlp(nc, names, T["HN"], W["w1"], W["b1a"], W["b1g"], W["w2"], ones_row,
                              W["b2"][0:1, :], T["qm"][:, 0:HC, :], Y)
                    copy_stage(nc, names, [(element(Y_all, b), Y[:])])

        if stop == 1:
            with stage(nc, names.next("add"), "unused") as (block, _unused):
                @block.vector
                def _(dve):
                    nc.vector.tensor_tensor(X_all[:], X_all[:], Y_all[:], ALU.add)
            return finish()

        def router_tail(b, T, router):
            layer_norm(nc, names, ident, T["X"], T["XN"], T["XNT"])
            LG = T["LG"]
            products(nc, names, ident, token_major_jobs(lambda t: LG[:, t, :], T["XNT"], router, 0, E))
            copy_stage(nc, names, [(element(X_all, b), T["X"][:]), (element(logits, b), LG[:])],
                       [(element(Y_all, b), T["XN"][:])])

        scattered = outer.enter_context(nc.semaphore("scattered"))
        gathered = [outer.enter_context(nc.semaphore(f"gathered{i}")) for i in range(4)]
        moes_done = []

        def experts(moe, bias_bc, dst):
            n = len(moes_done)
            route(nc, names, C, moe, logits, bias_bc, slot[:, :, 0:TT], gate[:], tile_expert[:], Y_all, xs, zeroed, n == 0)
            expert_tiles(nc, names, ident, moe, xs, os_, tile_expert, Y_all, slot, scattered, n * 2 * TT * 16)
            if n == 2 or dst is not None:
                combine(nc, names, moe, X_all, os_, slot, gate, dst, gathered, 0)
            moes_done.append(moe)

        rows_gathered = outer.enter_context(nc.semaphore("rows_gathered"))
        shared_landed = outer.enter_context(nc.semaphore("shared_landed"))
        GATHERS = 2 * NT * 16 * (B + 1)

        def next_gathers(T):
            return lambda pool: issue_gathers(pool, T["R"], os_, T["slots"], rows_gathered)

        def combined_phase(nth, weights, work, body):
            with ExitStack() as es:
                extra = {n: es.enter_context(nc.sbuf_tensor(f"{n}_{nth}", shape, dt)) for n, (shape, dt) in {
                    "R": ([P, NT, 2, D], F32), "S": ([P, NT, D], F32), "slots": ([P, 2, NT], I32),
                    "gates": ([P, 2, NT], F32)}.items()}
                def first_gathers(pool):
                    issue_gathers(pool, extra["R"], os_, slot[:, :, 0:NT], rows_gathered)

                def whole(b, W, T):
                    T = dict(T, **extra)
                    fetch_combined(nc, names, moes_done[-1], b, T, X_all, ctx_all, os_, slot, gate, rows_gathered,
                                   shared_landed, (nth * GATHERS, nth * 16 * B))
                    layer_norm(nc, names, ident, T["X"], T["XN"], T["XNT"])
                    body(b, W, T)

                batch_phase(weights, work, whole, on_gpsimd=first_gathers)
                with stage(nc, names.next("gather"), "unused") as (block, _unused):
                    @block.gpsimd
                    def _(pool):
                        pool.wait_ge(rows_gathered, (nth + 1) * GATHERS)

        base = {"X": tok, "XN": tok, "XNT": wid, "ctxT": wid, "LG": ([P, NT, E], F32)}

        def l1_cross(b, W, T):
            with stage(nc, names.next("mask"), "unused") as (block, _unused):
                @block.sync
                def _(sp):
                    sp.dma_start(T["mask_int"][:].rearrange("p k q -> p (k q)"),
                                 A["maskT"][bass.ds(b, 1)].rearrange("o p f -> (o p) f")).then_inc(mask_landed, 16)

                @block.vector
                def _(dve):
                    nc.vector.tensor_tensor(T["X"][:], element(X_all, b), element(Y_all, b), ALU.add)

                @block.scalar
                def _(act):
                    nc.scalar.activation(T["ctxT"][:].rearrange("p c n -> p (c n)"),
                                         ctx_all[:, bass.ds(b, 1), :].rearrange("p o f -> p (o f)"), ACT.Copy)
            layer_norm(nc, names, ident, T["X"], T["XN"], T["XNT"])
            V = T["V"]
            stacked_projections(nc, names, W["repeats"],
                                (width_terms(T["XNT"], W["L1_xattn_Wq"]), chunks_of(W["L1_xattn_bq"])),
                                (width_terms(T["ctxT"], W["L1_xattn_Wk"]), chunks_of(W["L1_xattn_bk"])),
                                T["q_stack"], T["k_stack"], 0.25,
                                token_major_jobs(lambda t: V[:, t, :], T["ctxT"], W["L1_xattn_Wv"], 0, 512,
                                                 ones_row=ones_row, bias_row=W["L1_xattn_bv"][0:1, :]))
            with stage(nc, names.next("mask"), "unused") as (block, _unused):
                @block.vector
                def _(dve):
                    dve.wait_ge(mask_landed, 16)
                    nc.vector.tensor_scalar(T["mask"][:], T["mask_int"][:], 0.0, None, ALU.not_equal)
            nc.sync.sem_clear(mask_landed)
            nc.all_engine_barrier()
            silu_attention(nc, names, lambda h: stacked(T["q_stack"], h), lambda h: stacked(T["k_stack"], h),
                           V, T["mask"], T["ONT"])
            products(nc, names, ident, out_projection_jobs(T["ONT"], 4, W["L1_xattn_Wo"], T["X"], None, None))
            router_tail(b, T, W["L1_ffn_gate_W"])

        batch_phase(["L1_xattn_Wq", "L1_xattn_bq", "L1_xattn_Wk", "L1_xattn_bk", "L1_xattn_Wv", "L1_xattn_bv",
                     "L1_xattn_Wo", "L1_ffn_gate_W"],
                    dict(base, V=quad, ONT=quad, q_stack=([P, 8, N], F32R), k_stack=([P, 8, N], F32R),
                         mask_int=([P, NT, N], I32), mask=quad), l1_cross, stacking=True)
        if stop == 2:
            return finish()
        experts(Moe("softmax", 1024, ACT.Silu, True, A["L1_weights"], 0.5, 0.5 / 8), None,
                out if stop == 3 else None)
        if stop == 3:
            return

        def l2_cross(b, W, T):
            V = T["V"]
            products(nc, names, ident,
                     head_major_jobs(T["qT"], T["XNT"], W["L2_xattn_Wq"], 4, scale=0.125)
                     + head_major_jobs(T["kT"], T["ctxT"], W["L2_xattn_Wk"], 4)
                     + token_major_jobs(lambda t: V[:, t, :], T["ctxT"], W["L2_xattn_Wv"], 0, 512),
                     on_gpsimd=next_gathers(T))
            units = []
            for h in range(8):
                for qt in range(NT):
                    units.append(Unit([(T["qm"][:, h, qt * P:(qt + 1) * P], T["kT"][:, h // 2, :])], N, 0,
                                      None, qt, h))
            softmax_attention(nc, names, ident, units, pair_groups(full_group), V, T["ONT"], T["row_sum"],
                              (T["qT"], C["pair_mask"], T["qm"], 2), normalise=True)
            products(nc, names, ident, out_projection_jobs(T["ONT"], 4, W["L2_xattn_Wo"], T["X"], ones_row,
                                                           W["L2_xattn_bo"][0:1, :]))
            router_tail(b, T, W["L2_ffn_router_w"])

        combined_phase(0, ["L2_xattn_Wq", "L2_xattn_Wk", "L2_xattn_Wv", "L2_xattn_Wo", "L2_xattn_bo", "L2_ffn_router_w"],
                    dict(base, qT=quad, kT=quad, V=quad, ONT=quad, qm=([P, 8, N], F32),
                         row_sum=([P, NT, 8], F32)), l2_cross)
        if stop == 4:
            return finish()
        with ExitStack() as es:
            ebias = es.enter_context(nc.sbuf_tensor("expert_bias", [P, E], F32))
            load_stage(nc, names, [(ebias[:], A["L2_ffn_experts_bias"].to_broadcast([P, E]))])
            experts(Moe("top2", 512, ACT.Silu, True, A["L2_weights"], 1.0, 1.0), ebias[:],
                    out if stop == 5 else None)
        if stop == 5:
            return

        def l3_cross(b, W, T):
            V = T["V"]
            products(nc, names, ident,
                     head_major_jobs(T["qT"], T["XNT"], W["L3_xattn_Wq"], DC, scale=0.0625, bias=W["L3_xattn_bq"])
                     + head_major_jobs(T["kT"], T["ctxT"], W["L3_xattn_Wk"], DC, bias=W["L3_xattn_bk"])
                     + token_major_jobs(lambda t: V[:, t, 0:D], T["ctxT"], W["L3_xattn_Wv"], 0, D,
                                        ones_row=ones_row, bias_row=W["L3_xattn_bv"][0:1, :]),
                     on_gpsimd=next_gathers(T))
            units = [Unit([(T["qT"][:, c, qt * P:(qt + 1) * P], T["kT"][:, c, :]) for c in range(DC)], N, 0, None,
                          qt, 0) for qt in range(NT)]
            groups = [full_group([0], [(c, 0, (c * P, (c + 1) * P), 0) for c in range(DC)])]
            softmax_attention(nc, names, ident, units, groups, V, T["ONT"], T["row_sum"])
            scale_heads(nc, names, ident, T["ONT"], DC, T["row_sum"], 1, D, D, T["XN"], T["X"])
            router_tail(b, T, W["L3_ffn_Wg"])

        combined_phase(1, ["L3_xattn_Wq", "L3_xattn_bq", "L3_xattn_Wk", "L3_xattn_bk", "L3_xattn_Wv", "L3_xattn_bv",
                     "L3_ffn_Wg"],
                    dict(base, qT=quad, kT=quad, V=quad, ONT=quad, row_sum=([P, NT, 1], F32)), l3_cross)
        if stop == 6:
            return finish()
        experts(Moe("capacity", 512, ACT.Gelu, False, A["L3_weights"], 1.0, 0.0), None, out)


CONSTS = [("ident", P), ("ones", P), ("upper", P), ("mean", P), ("mask", 2 * P), ("rope_c", NT * 2 * 64),
          ("rope_s", NT * 2 * 64), ("countdown", E), ("tile_steps", E), ("before", E * E), ("tile_ids", ROUTED), ("head_mask", 8), ("pair_mask", 2)]


def constants():
    p = np.arange(P)
    pos = (np.arange(NT)[None, :] * P + p[:, None]).astype(np.float32)
    half = np.arange(0, 64, 2, dtype=np.float32)
    inv_freq = (np.float32(1.0) / np.float32(10000.0) ** (half / np.float32(64))).astype(np.float32)
    freqs = (pos[..., None] * inv_freq).astype(np.float32).astype(np.float64)
    freqs = np.concatenate([freqs, freqs], -1)
    base = (half.astype(np.float64) + 0.4 * 64) / (1.4 * 64)
    scale = base[None, None, :] ** ((pos[..., None].astype(np.float64) - N // 2) / 64.0)
    scale = np.concatenate([scale, scale], -1)
    sign = np.where(np.arange(64) < 32, -1.0, 1.0)
    rope_c = np.stack([np.cos(freqs) * scale * 8.0, np.cos(freqs) / scale], 2)
    rope_s = np.stack([np.sin(freqs) * scale * 8.0 * sign, np.sin(freqs) / scale * sign], 2)
    prev = np.where(p[:, None] > p[None, :], NEG, 0.0)
    own = np.where(p[:, None] < p[None, :], NEG, 0.0)
    one = np.ones((P, 1))
    tabs = {
        "ident": np.eye(P), "ones": np.ones((P, P)), "upper": (p[:, None] < p[None, :]),
        "mean": np.full((P, P), 1.0 / D), "mask": np.concatenate([prev, own], 1),
        "rope_c": rope_c.reshape(P, -1), "rope_s": rope_s.reshape(P, -1),
        "countdown": one * (E - np.arange(E)), "tile_steps": one * (TS * np.arange(E)),
        "before": one * (np.arange(E)[None, :] < np.arange(E)[:, None]).reshape(1, -1),
        "tile_ids": one * np.arange(ROUTED),
        "head_mask": p[:, None] // 16 == np.arange(8)[None, :],
        "pair_mask": p[:, None] // 64 == np.arange(2)[None, :],
    }
    return np.concatenate([np.asarray(tabs[n], np.float32).reshape(P, k) for n, k in CONSTS], 1)


def repeats():
    out = np.zeros((P, 4, 2, 2, P), np.float32)
    for p in range(4):
        for x in range(2):
            for j in range(2):
                for s in range(4):
                    low = s // 2 if x == 0 else s % 2
                    for d in range(16):
                        out[(2 * p + j) * 16 + d, p, x, low, 64 * j + 16 * s + d] = 1.0
    return out.reshape(P, -1)


def rows(w):
    w = np.asarray(w)
    return np.ascontiguousarray(w.reshape(-1, P, w.shape[-1]).transpose(1, 0, 2))


def pad_heads(w):
    w = np.asarray(w).reshape(-1, 16, 16)
    out = np.zeros((w.shape[0], 16, 32), w.dtype)
    out[:, :, :16] = w
    return out.reshape(w.shape[0], 512)


def column(v):
    v = np.asarray(v)
    return np.ascontiguousarray(v.reshape(-1, P).T)


def layout(i):
    i = {k: np.asarray(v) for k, v in i.items()}
    A = {"consts": constants(), "repeats": repeats(), "x": i["x"].reshape(TOK, D)}
    A["ctxT"] = np.ascontiguousarray(i["ctx_1024"].reshape(B, N, DC, P).transpose(0, 3, 2, 1)).reshape(B, P, DC * N)
    A["maskT"] = np.ascontiguousarray(i["mask_Bx1xSxS2_ik1"].reshape(B, N, NT, P).transpose(0, 3, 2, 1))\
        .reshape(B, P, NT * N)
    for n in ("Wq", "Wk"):
        A["L0_xattn_" + n] = rows(i["L0_xattn_" + n].T)
        A["L1_xattn_" + n] = rows(i["L1_xattn_" + n].T)
        A["L2_xattn_" + n] = rows(i["L2_xattn_" + n])
        A["L3_xattn_" + n] = rows(i["L3_xattn_" + n])
    for n in ("bq", "bk"):
        A["L1_xattn_" + n] = column(i["L1_xattn_" + n])
        A["L3_xattn_" + n] = column(i["L3_xattn_" + n])
    A["L0_xattn_Wv"] = rows(pad_heads(i["L0_xattn_Wv"].T))
    A["L1_xattn_Wv"] = rows(pad_heads(i["L1_xattn_Wv"].T))
    A["L1_xattn_Wo"] = rows(pad_heads(i["L1_xattn_Wo"]).T)
    A["L2_xattn_Wv"] = rows(i["L2_xattn_Wv"])
    A["L2_xattn_Wo"] = rows(i["L2_xattn_Wo"])
    A["L3_xattn_Wv"] = rows(i["L3_xattn_Wv"])
    A["L1_xattn_bv"] = pad_heads(i["L1_xattn_bv"].reshape(1, D))
    for n in ("L2_xattn_bo", "L3_xattn_bv"):
        A[n] = i[n].reshape(1, D)
    A["L1_ffn_gate_W"] = rows(i["L1_ffn_gate_W"].T)
    A["L2_ffn_router_w"] = rows(i["L2_ffn_router_w"].T)
    A["L3_ffn_Wg"] = rows(i["L3_ffn_Wg"])
    A["L2_ffn_experts_bias"] = i["L2_ffn_experts_bias"].reshape(1, E)

    f = {n: i["L0_ffn_" + n] for n in ("wqkv", "q_scale", "k_scale", "wo", "ln_g", "ln_b", "w1", "b1", "w2", "b2")}

    def padded(v, n):
        out = np.zeros((n,) + v.shape[1:], v.dtype)
        out[:v.shape[0]] = v
        return out

    A["f_wqkv"] = np.stack([rows(w) for w in f["wqkv"]])
    A["f_wo"] = np.stack([rows(w) for w in f["wo"]])
    A["f_w1"] = np.stack([rows(w) for w in f["w1"]])
    A["f_w2"] = np.stack([rows(padded(w, HC * P)) for w in f["w2"]])
    A["f_b1a"] = np.stack([column(padded(v[:HID], HC * P)) for v in f["b1"]])
    A["f_b1g"] = np.stack([column(padded(v[HID:], HC * P)) for v in f["b1"]])
    A["f_b2"] = f["b2"].reshape(2, 1, D)
    A["f_ln_g"] = np.stack([column(v) for v in f["ln_g"]])
    A["f_ln_b"] = np.stack([column(v) for v in f["ln_b"]])
    qk = np.stack([f["q_scale"], f["k_scale"]], 1)
    swapped = np.concatenate([qk[..., 32:], qk[..., :32]], -1)
    A["f_qk"] = np.ascontiguousarray(np.broadcast_to(qk.reshape(2, 1, 128), (2, P, 128)))
    A["f_qk_sw"] = np.ascontiguousarray(np.broadcast_to(swapped.reshape(2, 1, 128), (2, P, 128)))

    def expert_weights(w1, w3, w2):
        n = w1.shape[0]
        w13 = np.stack([w1, w3], 1).reshape(n, 2, DC, P, -1, P).transpose(0, 3, 4, 1, 2, 5)
        w2 = w2.reshape(n, -1, P, D).transpose(0, 2, 1, 3)
        return np.ascontiguousarray(np.concatenate([w13.reshape(n, P, -1, 2 * DC * P), w2], -1)).reshape(n, P, -1)

    def beside(w):
        return w.transpose(1, 0, 2).reshape(1, D, -1)

    A["L1_weights"] = expert_weights(
        np.concatenate([i["L1_ffn_w1_e"], beside(i["L1_ffn_w1_s"])]),
        np.concatenate([i["L1_ffn_w3_e"], beside(i["L1_ffn_w3_s"])]),
        np.concatenate([i["L1_ffn_w2_e"], i["L1_ffn_w2_s"].reshape(1, -1, D)]))
    A["L2_weights"] = expert_weights(
        np.concatenate([i["L2_ffn_w1"], i["L2_ffn_sw1"]]), np.concatenate([i["L2_ffn_w3"], i["L2_ffn_sw3"]]),
        np.concatenate([i["L2_ffn_w2"], i["L2_ffn_sw2"]]))
    A["L3_weights"] = expert_weights(i["L3_ffn_W_in"][:, :, :512], i["L3_ffn_W_in"][:, :, 512:],
                                             i["L3_ffn_W_out"])
    return A


STOP = None


def kernel(**inputs):
    import concourse.bacc as _bacc
    from concourse.bass_utils import run_bass_kernel_spmd as _run

    nc = _bacc.Bacc("TRN2", target_bir_lowering=False, num_devices=1)
    arrays, aps = {}, {}
    for name, a in layout(inputs).items():
        arrays["in_" + name] = a
        aps[name] = nc.dram_tensor("in_" + name, a.shape, mybir.dt.from_np(a.dtype), kind="ExternalInput").ap()
    out = nc.dram_tensor("out_x", (TOK, D), F32, kind="ExternalOutput").ap()
    program(nc, aps, out, STOP)
    r = _run(nc, [arrays], core_ids=[0])
    return r.results[0]["out_x"].reshape(B, N, D)
```
